# Optimizing a Trainium2 kernel written in Bass

```python
import numpy as np
import jax
import jax.numpy as jnp

def _softmax(x, axis=-1):
    return jax.nn.softmax(x, axis=axis)

def _gelu(x):
    return jax.nn.gelu(x, approximate=True)

def _silu(x):
    return jax.nn.silu(x)

def _sigmoid(x):
    return jax.nn.sigmoid(x)

def _layernorm(x, axis=-1, eps=1e-05):
    m = jnp.mean(x, axis=axis, keepdims=True)
    v = jnp.var(x, axis=axis, keepdims=True)
    return (x - m) / jnp.sqrt(v + eps)

def _scatter_add(tgt, idx, src, axis=0):
    return tgt.at[idx].add(src)

def _segment_sum(src, seg, n):
    return jax.ops.segment_sum(src, seg, n)
kernel_name = 'mk_flamingo_gated_d1_seqx_r4_a90fb8'

def setup_inputs(seed: int=0):
    np.random.seed(seed)
    _w = jnp.asarray

    def _rec_inputs():
        import jax
        import jax.numpy as jnp
        _rk = jax.random.key(seed)
        x = -0.0002928 + 1 * jax.random.normal(jax.random.fold_in(_rk, 1), (2, 1024, 256), jnp.float32)
        _lenS = 1024 - jax.random.randint(jax.random.fold_in(_rk, 7), (2,), 0, max(1, 1024 // 4) + 1, jnp.int32)
        _lenS2 = 77 - jax.random.randint(jax.random.fold_in(_rk, 8), (2,), 0, max(1, 77 // 4) + 1, jnp.int32)
        _ctx_1024P = jax.random.normal(jax.random.fold_in(_rk, 11), (2, 16, 256), jnp.float32)
        _ctx_1024c = jax.random.dirichlet(jax.random.fold_in(_rk, 511), 0.3 * jnp.ones((16,), jnp.float32), (2, 77))
        _ctx_1024t = jnp.einsum('bsk,bkd->bsd', _ctx_1024c, _ctx_1024P)
        _ctx_1024t = _ctx_1024t * jax.lax.rsqrt(jnp.mean(jnp.square(_ctx_1024t)) + 1e-12) * 0.953939
        ctx_1024 = -1.39393e-06 + 0.999914 * (_ctx_1024t + 0.3 * jax.random.normal(jax.random.fold_in(_rk, 611), (2, 77, 256), jnp.float32))
        _g = jax.random.normal(jax.random.fold_in(_rk, 9001), (2, 1), jnp.float32)
        _g = jnp.sign(_g) * jnp.maximum(jnp.abs(_g), 1.0) + (_g == 0) * 1.0
        g_xattn = _g[0]
        g_ffn = _g[1]
        return (x, ctx_1024, g_xattn, g_ffn)
    x, ctx_1024, g_xattn, g_ffn = _rec_inputs()

    def _L0_xattn_setup():
        import jax, jax.numpy as jnp
        import numpy as np
        D_MODEL = 256
        NUM_HEADS = 16
        HEAD_DIM = D_MODEL // NUM_HEADS
        B, S = (2, 512)

        def _split_heads(x):
            b, s, _ = x.shape
            return x.reshape(b, s, NUM_HEADS, HEAD_DIM).transpose(0, 2, 1, 3)
        key = jax.random.key(seed)
        ks = jax.random.split(key, 11)
        scale = 1.0 / np.sqrt(D_MODEL)
        inp = {'Q': jax.random.normal(ks[0], (B, S, D_MODEL), jnp.float32), 'K': jax.random.normal(ks[1], (B, S, D_MODEL), jnp.float32), 'V': jax.random.normal(ks[2], (B, S, D_MODEL), jnp.float32), 'Wq': jax.random.normal(ks[3], (D_MODEL, D_MODEL), jnp.float32) * scale, 'bq': jax.random.normal(ks[4], (D_MODEL,), jnp.float32) * scale, 'Wk': jax.random.normal(ks[5], (D_MODEL, D_MODEL), jnp.float32) * scale, 'bk': jax.random.normal(ks[6], (D_MODEL,), jnp.float32) * scale, 'Wv': jax.random.normal(ks[7], (D_MODEL, D_MODEL), jnp.float32) * scale, 'bv': jax.random.normal(ks[8], (D_MODEL,), jnp.float32) * scale, 'Wo': jax.random.normal(ks[9], (D_MODEL, D_MODEL), jnp.float32) * scale, 'bo': jax.random.normal(ks[10], (D_MODEL,), jnp.float32) * scale}
        return inp
    _L0_xattn_all = _L0_xattn_setup()
    _L0_xattn_in = {k: v for k, v in _L0_xattn_all.items() if k in ('Wq', 'bq', 'Wk', 'bk', 'Wv', 'bv', 'Wo', 'bo')}
    del _L0_xattn_all

    def _L0_ffn_setup():
        import jax, jax.numpy as jnp
        import numpy as np
        E = 8
        TOP_K = 2
        D = 256
        H = 2 * D
        key = jax.random.key(seed)
        k0, k1, k2, k3, k4 = jax.random.split(key, 5)
        scale = 0.02
        x = jax.random.normal(k0, (4, 512, D), dtype=jnp.float32)
        Wg = jax.random.normal(k1, (D, E), dtype=jnp.float32) * scale
        W1 = jax.random.normal(k2, (E, D, H), dtype=jnp.float32) * scale
        W2 = jax.random.normal(k3, (E, D, H), dtype=jnp.float32) * scale
        W3 = jax.random.normal(k4, (E, H, D), dtype=jnp.float32) * scale
        return {'x': x, 'Wg': Wg, 'W1': W1, 'W2': W2, 'W3': W3}
    _L0_ffn_all = _L0_ffn_setup()
    _L0_ffn_in = {k: v for k, v in _L0_ffn_all.items() if k in ('Wg', 'W1', 'W2', 'W3')}
    del _L0_ffn_all
    return {'x': x, 'ctx_1024': ctx_1024, 'g_xattn': g_xattn, 'g_ffn': g_ffn, 'L0_xattn_Wq': _L0_xattn_in['Wq'], 'L0_xattn_bq': _L0_xattn_in['bq'], 'L0_xattn_Wk': _L0_xattn_in['Wk'], 'L0_xattn_bk': _L0_xattn_in['bk'], 'L0_xattn_Wv': _L0_xattn_in['Wv'], 'L0_xattn_bv': _L0_xattn_in['bv'], 'L0_xattn_Wo': _L0_xattn_in['Wo'], 'L0_xattn_bo': _L0_xattn_in['bo'], 'L0_ffn_Wg': _L0_ffn_in['Wg'], 'L0_ffn_W1': _L0_ffn_in['W1'], 'L0_ffn_W2': _L0_ffn_in['W2'], 'L0_ffn_W3': _L0_ffn_in['W3']}

def reference(x, ctx_1024, g_xattn, g_ffn, L0_xattn_Wq, L0_xattn_bq, L0_xattn_Wk, L0_xattn_bk, L0_xattn_Wv, L0_xattn_bv, L0_xattn_Wo, L0_xattn_bo, L0_ffn_Wg, L0_ffn_W1, L0_ffn_W2, L0_ffn_W3):
    import jax
    import jax.numpy as jnp

    def _L0_xattn_ref(Q, K, V, Wq, bq, Wk, bk, Wv, bv, Wo, bo):
        import jax, jax.numpy as jnp
        import numpy as np
        D_MODEL = 256
        NUM_HEADS = 16
        HEAD_DIM = D_MODEL // NUM_HEADS
        B, S = (2, 512)

        def _split_heads(x):
            b, s, _ = x.shape
            return x.reshape(b, s, NUM_HEADS, HEAD_DIM).transpose(0, 2, 1, 3)
        q = _split_heads(Q @ Wq + bq)
        k = _split_heads(K @ Wk + bk)
        v = _split_heads(V @ Wv + bv)
        scores = jnp.einsum('bhqd,bhkd->bhqk', q, k) / jnp.sqrt(jnp.asarray(HEAD_DIM, q.dtype))
        attn = jax.nn.softmax(scores, axis=-1)
        out = jnp.einsum('bhqk,bhkd->bhqd', attn, v)
        out = out.transpose(0, 2, 1, 3).reshape(Q.shape[0], -1, D_MODEL)
        return out @ Wo + bo

    def _L0_ffn_ref(x, Wg, W1, W2, W3):
        import jax, jax.numpy as jnp
        import numpy as np
        E = 8
        TOP_K = 2
        D = 256
        H = 2 * D
        logits = jnp.einsum('bsd,de->bse', x, Wg)
        top_vals, top_idx = jax.lax.top_k(logits, TOP_K)
        probs = jax.nn.softmax(top_vals, axis=-1)
        onehot = jax.nn.one_hot(top_idx, E, dtype=x.dtype)
        weights = jnp.einsum('bsk,bske->bse', probs, onehot)
        out = jnp.zeros_like(x)
        for e in range(E):
            u = jnp.einsum('bsd,dh->bsh', x, W1[e])
            v = jnp.einsum('bsd,dh->bsh', x, W2[e])
            h = u * jax.nn.sigmoid(u) * v
            y = jnp.einsum('bsh,hd->bsd', h, W3[e])
            out = out + y * weights[..., e][..., None]
        return out
    x = x + jnp.tanh(g_xattn[0]) * _L0_xattn_ref(_layernorm(x, axis=-1), ctx_1024, ctx_1024, L0_xattn_Wq, L0_xattn_bq, L0_xattn_Wk, L0_xattn_bk, L0_xattn_Wv, L0_xattn_bv, L0_xattn_Wo, L0_xattn_bo)
    x = x + jnp.tanh(g_ffn[0]) * _L0_ffn_ref(_layernorm(x, axis=-1), L0_ffn_Wg, L0_ffn_W1, L0_ffn_W2, L0_ffn_W3)
    return x

_drawn_inputs = setup_inputs


def setup_inputs(seed=0):
    import zlib

    import numpy as np

    out = dict(_drawn_inputs(seed))
    spreads = {}
    factors = {'L0_xattn_bq': 5.116,
     'L0_xattn_bk': 8.0,
     'L0_ffn_Wg': 4.428,
     'L0_ffn_W1': 3.89,
     'L0_ffn_W2': 3.84,
     'L0_ffn_W3': 3.845}
    for name, (base, spread) in spreads.items():
        noise = np.random.default_rng([zlib.crc32(name.encode()), seed]).standard_normal(out[name].shape)
        drawn = base * np.exp(spread * noise) if base else spread * noise
        out[name] = jnp.asarray(drawn.astype(out[name].dtype))
    for name, factor in factors.items():
        out[name] = (out[name] * factor).astype(out[name].dtype)
    return out
```

```python
from contextlib import ExitStack

import concourse.bass as bass
from concourse import mybir

P = 128
ALU = mybir.AluOpType
ACT = mybir.ActivationFunctionType
AX_X = mybir.AxisListType.X
F32 = mybir.dt.float32
BF16 = mybir.dt.bfloat16
I32 = mybir.dt.int32
U32 = mybir.dt.uint32


def middle(t, low, high):
    return low <= t < high if isinstance(t, int) else True


def run_steps(eng, step, loop_from, loop_to, end):
    for t in range(loop_from):
        step(t, t % 2)
    with eng.Fori(loop_from // 2, loop_to // 2) as i:
        for parity in range(2):
            step(i * 2 + parity, parity)
    for t in range(loop_to, end):
        step(t, t % 2)


def flamingo_layer(nc, x, ctx, g_xattn, g_ffn, wq, bq, wk, bk, wv, bv, wo, bo, wg, w1, w2, w3, out):
    B, S, D = x.shape
    KEYS = ctx.shape[1]
    HD = 16
    HEADS = D // HD
    E, _, HID = w1.shape
    DK = D // P
    HK = HID // P
    T = B * S
    TT = T // P
    HEADS_HALF = P // HD
    FLAT = HEADS * KEYS
    PCH = -(-FLAT // P)
    VW = HD + 1
    BANK_HEADS = 6
    TOPK = 2
    SQ = 1.0 / float(HD) ** 0.5
    EPS = 1e-5
    META = 4
    ROW = D + META
    CAPACITY = T + P
    XS_ROWS = E * CAPACITY + P
    NT = T * TOPK // P + E - 1
    assert B == 2 and S % P == 0 and DK == 2 and HEADS == 16 and TT % 2 == 0 and NT % 2 == 1
    head0 = [c * P // KEYS for c in range(PCH)]
    heads_in = [min(c * P + P - 1, FLAT - 1) // KEYS - head0[c] + 1 for c in range(PCH)]
    SPAN = max(heads_in)

    xs = nc.dram_tensor("sorted_rows", (XS_ROWS, ROW), F32).ap()
    acc = nc.dram_tensor("accumulator", (T + P, D), F32).ap()
    vflat_dram = nc.dram_tensor("values_by_head", (B, PCH * P, VW), F32).ap()

    with ExitStack() as stack:
        def sb(name, shape, dt=F32):
            return stack.enter_context(nc.sbuf_tensor(name, shape, dt))

        def sem(name):
            return stack.enter_context(nc.semaphore(name))

        bank = [stack.enter_context(nc.psum_tensor(f"bank{i}", [P, 512], F32)) for i in range(6)]
        score_banks = stack.enter_context(nc.psum_tensor("score_banks", [P, 2, 512], F32))

        ident = sb("ident", [P, P])
        ones_f = sb("ones_f", [P, P])
        before_b = sb("before_b", [P, P], BF16)
        ones_b = sb("ones_b", [P, P], BF16)
        kmask = sb("kmask", [P, HEADS_HALF])
        vmask = sb("vmask", [P, PCH, SPAN])
        desc = sb("desc", [P, E])
        desc_i = sb("desc_i", [P, E], I32)
        cap_base = sb("cap_base", [P, E])
        cap_base_i = sb("cap_base_i", [P, E], I32)
        tile_no = sb("tile_no", [P, NT])
        tile_no_i = sb("tile_no_i", [P, NT], I32)
        tile_128 = sb("tile_128", [P, TT])
        tile_128_i = sb("tile_128_i", [P, TT], I32)
        scan_keep = sb("scan_keep", [P, E, TT])
        pad_rows = sb("pad_rows", [P, ROW])

        ctx_sb = sb("ctx_sb", [KEYS, B, D])
        wq_sb = sb("wq_sb", [P, DK, D])
        wk_sb = sb("wk_sb", [P, DK, D])
        wv_sb = sb("wv_sb", [P, DK, D])
        wo_sb = sb("wo_sb", [P, DK, D])
        wg_sb = sb("wg_sb", [P, DK, E])
        bq_sb = sb("bq_sb", [P, DK])
        bk_sb = sb("bk_sb", [P, DK])
        bv_sb = sb("bv_sb", [KEYS, D])
        bo_sb = sb("bo_sb", [P, D])
        gates = sb("gates", [P, 2])
        tg = sb("tg", [P, 2])
        w1_sb = sb("w1_sb", [P, E, DK, HID])
        w2_sb = sb("w2_sb", [P, E, DK, HID])
        w3_sb = sb("w3_sb", [P, E, HK, D])

        ctxT = sb("ctxT", [P, DK, B * KEYS])
        kT = sb("kT", [P, DK, B * KEYS])
        kblock = sb("kblock", [P, B, DK, HEADS_HALF, KEYS])
        v_sb = sb("v_sb", [KEYS, B, HEADS, VW])
        vflat = sb("vflat", [P, B, PCH, VW])
        vblock = sb("vblock", [P, B, PCH, SPAN, VW])

        rows = sb("rows", [P, TT, ROW])
        x_sb = rows[:, :, 0:D]
        x1 = sb("x1", [P, TT, D])
        st1 = sb("st1", [P, TT, 6])
        mv1 = sb("mv1", [P, TT, 2])
        std1 = sb("std1", [P, TT])
        rstd1 = sb("rstd1", [P, TT])
        xn = sb("xn", [P, 2, D])
        xnT = sb("xnT", [P, 2, DK, P])
        qT = sb("qT", [P, 2, DK, P])
        negmax = sb("negmax", [P, 2, HEADS])
        shifted = sb("shifted", [P, 2, FLAT])
        before = shifted[:, 0, 0:P]
        probs = sb("probs", [P, 2, PCH * P])
        probsT = sb("probsT", [P, 2, PCH, P])
        rden = sb("rden", [P, 2, HEADS])
        o_sb = sb("o_sb", [P, 2, D])
        oT = sb("oT", [P, 2, DK, P])
        st2 = sb("st2", [P, TT, 6])

        mean2 = sb("mean2", [P, TT])
        half_diff = sb("half_diff", [P, TT])
        var2 = sb("var2", [P, TT])
        std2 = sb("std2", [P, TT])
        rstd2 = sb("rstd2", [P, TT])
        xg, xgT = xn, xnT
        kblock_flat = kblock[:, :, :, :, :].rearrange("p b m h k -> p (b m h k)")
        carved = [0]

        def carve(a, b):
            at = carved[0]
            carved[0] += a * b
            assert carved[0] <= B * DK * HEADS_HALF * KEYS
            return kblock_flat[:, at:at + a * b].rearrange("p (a b) -> p a b", a=a)

        logits = carve(TT, E)
        best = [sb(f"best{c}", [P, TT]) for c in range(TOPK)]
        key = [sb(f"key{c}", [P, TT]) for c in range(TOPK)]
        onehot = [carve(TT, E) for c in range(TOPK)]
        scratch = carve(TT, E)
        logits2 = carve(TT, E)
        gap = sb("gap", [P, TT])
        egap = sb("egap", [P, TT])
        esum = sb("esum", [P, TT])
        p1 = sb("p1", [P, TT])
        p1g = sb("p1g", [P, TT])
        sel = sb("sel", [P, TT, E], BF16)
        totals = carve(E, TT)
        upto = carve(E, TT)
        offset = carve(E, TT)
        position = carve(TT, E)
        slot_f = [sb(f"slot_f{c}", [P, TT]) for c in range(TOPK)]
        slot = [sb(f"slot{c}", [P, TT], I32) for c in range(TOPK)]
        tile_cmp = carve(E, TT)
        ntiles = sb("ntiles", [P, E])
        tiles_upto = sb("tiles_upto", [P, E])
        counts_i = sb("counts_i", [P, E], I32)
        past = carve(NT, E)
        past_n = carve(NT, E)
        tile_expert = sb("tile_expert", [P, NT])
        tile_expert_i = sb("tile_expert_i", [P, NT], I32)
        tiles_before = sb("tiles_before", [P, NT])
        tile_used = sb("tile_used", [P, NT])
        tile_row = sb("tile_row", [P, NT])
        tile_row_i = sb("tile_row_i", [P, NT], I32)

        xT = qT
        xt = probs[:, :, 0:ROW]
        y_sb = [o_sb[:, c, :] for c in range(2)]
        spare = shifted[:, :, :].rearrange("p a f -> p (a f)")
        silu = spare[:, 0:2 * HID].rearrange("p (a f) -> p a f", a=2)
        h = spare[:, 2 * HID:4 * HID].rearrange("p (a f) -> p a f", a=2)
        hT = probsT[:, :, 0:HK, :]
        weight1 = sb("weight1", [P, 2])
        weight = sb("weight", [P, NT])
        ids = sb("ids", [P, NT], I32)

        ctx_loaded = sem("ctx_loaded")
        kv_weights_loaded = sem("kv_weights_loaded")
        small_loaded = sem("small_loaded")
        x_loaded = sem("x_loaded")
        qo_loaded = sem("qo_loaded")
        experts_loaded = sem("experts_loaded")
        pool_step = sem("pool_step")
        tanh_ready = sem("tanh_ready")
        ctxT_in_psum = sem("ctxT_in_psum")
        ctxT_ready = sem("ctxT_ready")
        kT_in_psum = sem("kT_in_psum")
        kT_ready = sem("kT_ready")
        v_in_psum = sem("v_in_psum")
        v_ready = sem("v_ready")
        v_stored = sem("v_stored")
        vflat_cleared = sem("vflat_cleared")
        vflat_loaded = sem("vflat_loaded")
        blocks_ready = sem("blocks_ready")
        dve_step = sem("dve_step")
        var1_ready = sem("var1_ready")
        std1_ready = sem("std1_ready")
        residual_ready = sem("residual_ready")
        xn_ready = sem("xn_ready")
        xnT_in_psum = sem("xnT_in_psum")
        xnT_ready = sem("xnT_ready")
        q_in_psum = sem("q_in_psum")
        q_ready = sem("q_ready")
        scores_in_psum = sem("scores_in_psum")
        max_ready = sem("max_ready")
        shifted_ready = sem("shifted_ready")
        probs_ready = sem("probs_ready")
        probsT_in_psum = sem("probsT_in_psum")
        probsT_ready = sem("probsT_ready")
        pv_in_psum = sem("pv_in_psum")
        rden_ready = sem("rden_ready")
        o_ready = sem("o_ready")
        oT_in_psum = sem("oT_in_psum")
        oT_ready = sem("oT_ready")
        attn_in_psum = sem("attn_in_psum")
        x1_ready = sem("x1_ready")
        stats_ready = sem("stats_ready")
        acc_written = sem("acc_written")
        var2_ready = sem("var2_ready")
        std2_ready = sem("std2_ready")
        xg_ready = sem("xg_ready")
        xg_copied = sem("xg_copied")
        xgT_in_psum = sem("xgT_in_psum")
        xgT_ready = sem("xgT_ready")
        logits_in_psum = sem("logits_in_psum")
        gap_ready = sem("gap_ready")
        egap_ready = sem("egap_ready")
        sel_ready = sem("sel_ready")
        ranks_in_psum = sem("ranks_in_psum")
        slots_ready = sem("slots_ready")
        counts_ready = sem("counts_ready")
        tables_ready = sem("tables_ready")
        rows_scattered = sem("rows_scattered")
        padding_written = sem("padding_written")
        tile_loaded = [sem(f"tile_loaded{c}") for c in range(2)]
        xT_in_psum = sem("xT_in_psum")
        xT_ready = sem("xT_ready")
        u_in_psum = sem("u_in_psum")
        v2_in_psum = sem("v2_in_psum")
        silu_ready = sem("silu_ready")
        weight1_ready = sem("weight1_ready")
        meta_ready = sem("meta_ready")
        h_ready = sem("h_ready")
        hT_in_psum = sem("hT_in_psum")
        hT_ready = sem("hT_ready")
        y_in_psum = sem("y_in_psum")
        y_ready = sem("y_ready")
        y_added = sem("y_added")
        out_written = sem("out_written")

        bank_x, bank_o, bank_pv = bank[0], bank[1], bank[2]
        bank_p = [bank[3], bank[4]]
        scores_last = bank[5]
        q_psum = bank_x[:, D:2 * D].rearrange("p (k n) -> p k n", k=DK)
        pv_psum = bank_pv[:, 0:HEADS * VW].rearrange("p (h w) -> p h w", h=HEADS)

        N_POOL_SETUP = [0]

        def u_bank(parity):
            return bank[2 + parity][:, :]

        def v_bank(parity):
            return score_banks[:, parity, :]

        def y_bank(parity):
            return bank[4 + parity][:, 0:D]

        def bcast(ap, axis, n):
            shape = list(ap.shape)
            shape.insert(axis, n)
            return ap.unsqueeze(axis).to_broadcast(shape)

        def token_view(dram, b):
            return dram[b * S:(b + 1) * S, :].rearrange("(m p) d -> p m d", p=P)

        def tiles_of(tensor, b):
            return tensor[:, :, :].rearrange("p (m b) d -> p m b d", b=B)[:, :, b, :]

        block = stack.enter_context(nc.Block())

        @block.gpsimd
        def _(pool):
            def done(ins):
                N_POOL_SETUP[0] += 1
                ins.then_inc(pool_step, 1)
                pool.wait_ge(pool_step, N_POOL_SETUP[0])

            done(pool.memset(ones_f[:, :], 1.0))
            done(pool.affine_select(out=ident[:, :], in_=ones_f[:, :], compare_op=ALU.is_equal, fill=0.0,
                                    base=0, pattern=[[-1, P]], channel_multiplier=1))
            done(pool.affine_select(out=kmask[:, :], in_=ones_f[:, 0:HEADS_HALF], compare_op=ALU.is_ge, fill=0.0,
                                    base=0, pattern=[[-HD, HEADS_HALF]], channel_multiplier=1))
            done(pool.affine_select(out=kmask[:, :], in_=kmask[:, :], compare_op=ALU.is_ge, fill=0.0,
                                    base=HD - 1, pattern=[[HD, HEADS_HALF]], channel_multiplier=-1))
            for c in range(PCH):
                pool.affine_select(out=vmask[:, c, :], in_=ones_f[:, 0:SPAN], compare_op=ALU.is_ge, fill=0.0,
                                   base=c * P - KEYS * head0[c], pattern=[[-KEYS, SPAN]],
                                   channel_multiplier=1).then_inc(pool_step, 1)
            N_POOL_SETUP[0] += PCH
            pool.wait_ge(pool_step, N_POOL_SETUP[0])
            for c in range(PCH):
                pool.affine_select(out=vmask[:, c, :], in_=vmask[:, c, :], compare_op=ALU.is_ge, fill=0.0,
                                   base=KEYS * head0[c] + KEYS - 1 - c * P, pattern=[[KEYS, SPAN]],
                                   channel_multiplier=-1).then_inc(pool_step, 1)
            N_POOL_SETUP[0] += PCH
            pool.memset(probs[:, :, FLAT:PCH * P], 0.0).then_inc(pool_step, 1)
            pool.memset(pad_rows[:, :], 0.0).then_inc(pool_step, 1)
            pool.memset(scan_keep[:, :, :], 1.0).then_inc(pool_step, 1)
            pool.affine_select(out=before, in_=ones_f[:, :], compare_op=ALU.is_gt, fill=0.0,
                               base=0, pattern=[[1, P]], channel_multiplier=-1).then_inc(pool_step, 1)
            pool.iota(desc_i[:, :], pattern=[[-1, E]], base=E, channel_multiplier=0).then_inc(pool_step, 1)
            pool.iota(cap_base_i[:, :], pattern=[[CAPACITY, E]], base=0, channel_multiplier=0).then_inc(pool_step, 1)
            pool.iota(tile_no_i[:, :], pattern=[[1, NT]], base=0, channel_multiplier=0).then_inc(pool_step, 1)
            pool.iota(tile_128_i[:, :], pattern=[[P, TT]], base=0, channel_multiplier=0).then_inc(pool_step, 1)
            pool.iota(rows[:, :, D:D + 1].bitcast(I32), pattern=[[P, TT // B], [S, B], [0, 1]], base=0,
                      channel_multiplier=1).then_inc(pool_step, 1)
            N_POOL_SETUP[0] += 9
            pool.wait_ge(pool_step, N_POOL_SETUP[0])
            pool.iota(pad_rows[:, D:D + 1].bitcast(I32), pattern=[[0, 1]], base=T,
                      channel_multiplier=1).then_inc(pool_step, 1)
            pool.memset(scan_keep[:, :, 0:1], 0.0).then_inc(pool_step, 1)
            pool.tensor_copy(before_b[:, :], before).then_inc(pool_step, 1)
            pool.tensor_copy(ones_b[:, :], ones_f[:, :]).then_inc(pool_step, 1)
            pool.tensor_copy(desc[:, :], desc_i[:, :]).then_inc(pool_step, 1)
            pool.tensor_copy(cap_base[:, :], cap_base_i[:, :]).then_inc(pool_step, 1)
            pool.tensor_copy(tile_no[:, :], tile_no_i[:, :]).then_inc(pool_step, 1)
            pool.tensor_copy(tile_128[:, :], tile_128_i[:, :]).then_inc(pool_step, 1)
            N_POOL_SETUP[0] += 8
            pool.wait_ge(tanh_ready, 1)
            pool.wait_ge(x_loaded, 16 * B)
            pool.tensor_scalar(bo_sb[:, :], bo_sb[:, :], tg[:, 0:1], 0.0, ALU.mult, ALU.add).then_inc(residual_ready, 1)
            pool.wait_ge(residual_ready, 1)
            pool.tensor_tensor(x1[:, :, :], x_sb[:, :, :], bcast(bo_sb[:, :], 1, TT), ALU.add).then_inc(residual_ready, 1)

            for t in range(TT):
                pool.wait_ge(xg_ready, t + 1)
                pool.tensor_copy(rows[:, t, 0:D], xg[:, t % 2, :]).then_inc(xg_copied, 1)
            pool.wait_ge(xg_copied, TT)
            pool.wait_ge(slots_ready, 1)
            for t in range(TT):
                for c in range(TOPK):
                    pool.indirect_dma_start(
                        out=xs, out_offset=bass.IndirectOffsetOnAxis(ap=slot[c][:, t:t + 1].bitcast(U32), axis=0),
                        in_=rows[:, t, :], in_offset=None).then_inc(rows_scattered, 16)
            pool.wait_ge(acc_written, 16 * (B + 1))

            for j in range(NT):
                pool.wait_ge(y_ready, j + 1)
                if j >= 1:
                    pool.wait_ge(y_added, j * 16)
                pool.indirect_dma_start(
                    out=acc, out_offset=bass.IndirectOffsetOnAxis(ap=ids[:, j:j + 1].bitcast(U32), axis=0),
                    in_=y_sb[j % 2], in_offset=None, compute_op=ALU.add).then_inc(y_added, 16)

        @block.sync
        def _(sp):
            sp.dma_start(ctx_sb[:, :, :], ctx.rearrange("b k d -> k b d")).then_inc(ctx_loaded, 16)
            for w, dst in ((wk, wk_sb), (wv, wv_sb)):
                sp.dma_start(dst[:, :, :], w.rearrange("(k p) n -> p k n", p=P)).then_inc(kv_weights_loaded, 16)
            x_rows = x.rearrange("b s d -> (b s) d")
            for b in range(B):
                sp.dma_start(tiles_of(x_sb, b), token_view(x_rows, b)).then_inc(x_loaded, 16)
            for w, dst in ((wq, wq_sb), (wo, wo_sb), (wg, wg_sb)):
                sp.dma_start(dst[:, :, :], w.rearrange("(k p) n -> p k n", p=P)).then_inc(qo_loaded, 16)
            sp.wait_ge(v_ready, B + 1)
            for b in range(B):
                sp.dma_start(vflat_dram[b, 0:FLAT, :].rearrange("(h k) w -> k h w", h=HEADS),
                             v_sb[:, b, :, :]).then_inc(v_stored, 16)
            sp.wait_ge(v_stored, 16 * B)
            sp.wait_ge(vflat_cleared, 1)
            full = FLAT // P
            for b in range(B):
                sp.dma_start(vflat[:, b, 0:full, :],
                             vflat_dram[b, 0:full * P, :].rearrange("(c p) w -> p c w", p=P)).then_inc(vflat_loaded, 16)
                sp.dma_start(vflat[0:FLAT - full * P, b, full, :],
                             vflat_dram[b, full * P:FLAT, :]).then_inc(vflat_loaded, 16)
            for e in range(E):
                sp.dma_start(w1_sb[:, e, :, :], w1[e].rearrange("(k p) n -> p k n", p=P)).then_inc(experts_loaded, 16)
                sp.dma_start(w2_sb[:, e, :, :], w2[e].rearrange("(k p) n -> p k n", p=P)).then_inc(experts_loaded, 16)
                sp.dma_start(w3_sb[:, e, :, :], w3[e].rearrange("(k p) n -> p k n", p=P)).then_inc(experts_loaded, 16)
            sp.wait_ge(pool_step, N_POOL_SETUP[0])
            sp.dma_start(acc[T:T + P, :], pad_rows[:, 0:D]).then_inc(acc_written, 16)
            sp.dma_start(xs[E * CAPACITY:XS_ROWS, :], pad_rows[:, :]).then_inc(padding_written, 16)
            sp.wait_ge(x1_ready, TT)
            for b in range(B):
                sp.dma_start(token_view(acc, b), tiles_of(x1, b)).then_inc(acc_written, 16)
            sp.wait_ge(counts_ready, 1)
            for e in range(E):
                n = sp.value_load(counts_i[0:1, e:e + 1], min_val=0, max_val=T)
                sp.dma_start(xs[bass.ds(n + e * CAPACITY, P), :], pad_rows[:, :]).then_inc(padding_written, 16)
            sp.wait_ge(tables_ready, 1)
            sp.wait_ge(padding_written, 16 * (E + 1))
            sp.wait_ge(rows_scattered, 16 * TOPK * TT)

            def load(j, parity):
                if not isinstance(j, int) or j >= 2:
                    sp.wait_ge(xT_in_psum, j - 1)
                    sp.wait_ge(meta_ready, j - 1)
                row = sp.value_load(tile_row_i[0:1, bass.ds(j, 1)], min_val=0, max_val=XS_ROWS - P)
                sp.dma_start(xt[:, parity, :], xs[bass.ds(row, P), :]).then_inc(tile_loaded[parity], 16)

            run_steps(sp, load, 2, NT - 1, NT)
            sp.wait_ge(y_added, 16 * NT)
            sp.dma_start(out.rearrange("b s d -> (b s) d"), acc[0:T, :]).then_inc(out_written, 16)
            sp.wait_ge(out_written, 16)

        @block.scalar
        def _(act):
            act.dma_start(gates[:, 0:1], g_xattn.partition_broadcast(P)).then_inc(small_loaded, 16)
            act.dma_start(gates[:, 1:2], g_ffn.partition_broadcast(P)).then_inc(small_loaded, 16)
            act.dma_start(bk_sb[:, :], bk.rearrange("(k p) -> p k", p=P), allow_slow_non_contiguous=True).then_inc(small_loaded, 16)
            act.dma_start(bq_sb[:, :], bq.rearrange("(k p) -> p k", p=P), allow_slow_non_contiguous=True).then_inc(small_loaded, 16)
            act.dma_start(bv_sb[:, :], bv.partition_broadcast(KEYS)).then_inc(small_loaded, 16)
            act.dma_start(bo_sb[:, :], bo.partition_broadcast(P)).then_inc(small_loaded, 16)
            act.wait_ge(small_loaded, 96)
            act.activation(tg[:, :], gates[:, :], ACT.Tanh).then_inc(tanh_ready, 1)
            act.wait_ge(ctxT_in_psum, 1)
            act.copy(ctxT[:, :, :], bank[0][:, 0:DK * B * KEYS].rearrange("p (k n) -> p k n", k=DK)).then_inc(ctxT_ready, 1)
            act.wait_ge(var1_ready, 1)
            act.activation(std1[:, :], std1[:, :], ACT.Sqrt).then_inc(std1_ready, 1)

            def evacuate_xnT(t, parity):
                act.wait_ge(xnT_in_psum, t + 1)
                act.copy(xnT[:, parity, :, :].rearrange("p k n -> p (k n)"), bank_x[:, 0:D]).then_inc(xnT_ready, 1)

            def attention_step(t, parity):
                other = 1 - parity
                if middle(t, 2, TT + 2):
                    act.wait_ge(oT_in_psum, t - 1)
                    act.copy(oT[:, parity, :, :].rearrange("p k n -> p (k n)"), bank_o[:, 0:D]).then_inc(oT_ready, 1)
                if middle(t, 0, TT - 1):
                    evacuate_xnT(t + 1, other)
                if middle(t, 1, TT + 1):
                    for g in range(3):
                        n = min(4, PCH - 4 * g)
                        act.wait_ge(probsT_in_psum, (t - 1) * 3 + g + 1)
                        act.copy(probsT[:, other, 4 * g:4 * g + n, :].rearrange("p k n -> p (k n)"),
                                 bank_p[(3 * other + g) % 2][:, 0:n * P]).then_inc(probsT_ready, 1)
                if middle(t, 0, TT):
                    act.wait_ge(shifted_ready, t + 1)
                    act.activation(probs[:, parity, 0:FLAT], shifted[:, parity, :], ACT.Exp, scale=SQ).then_inc(probs_ready, 1)

            evacuate_xnT(0, 0)
            run_steps(act, attention_step, 2, TT - 2, TT + 2)

            act.wait_ge(var2_ready, 1)
            act.activation(std2[:, :], var2[:, :], ACT.Sqrt).then_inc(std2_ready, 1)

            def gate_step(t, parity):
                act.wait_ge(xgT_in_psum, t + 1)
                act.copy(xgT[:, parity, :, :].rearrange("p k n -> p (k n)"), bank_p[parity][:, 0:D]).then_inc(xgT_ready, 1)

            run_steps(act, gate_step, 0, TT, TT)
            act.wait_ge(gap_ready, 1)
            act.activation(egap[:, :], gap[:, :], ACT.Exp).then_inc(egap_ready, 1)

            def evacuate_xT(j, parity):
                act.wait_ge(xT_in_psum, j + 1)
                act.copy(xT[:, parity, :, :].rearrange("p k n -> p (k n)"), bank[0][:, 0:D]).then_inc(xT_ready, 1)

            def expert_step(j, parity):
                other = 1 - parity
                if middle(j, 0, NT):
                    act.wait_ge(u_in_psum, j + 1)
                    if middle(j, 2, NT):
                        act.wait_ge(h_ready, j - 1)
                    act.activation(silu[:, parity, :], u_bank(parity), ACT.Silu).then_inc(silu_ready, 1)
                if middle(j, 1, NT + 1):
                    act.wait_ge(hT_in_psum, j)
                    act.copy(hT[:, other, :, :].rearrange("p k n -> p (k n)"), bank[1][:, :]).then_inc(hT_ready, 1)
                if middle(j, 0, NT - 1):
                    evacuate_xT(j + 1, other)

            evacuate_xT(0, 0)
            run_steps(act, expert_step, 2, NT - 1, NT + 1)

        @block.tensor
        def _(pe):
            pe.wait_ge(pool_step, 2)
            pe.wait_ge(ctx_loaded, 16)
            for b in range(B):
                for k in range(DK):
                    at = (k * B + b) * KEYS
                    ins = pe.transpose(bank[0][:, at:at + KEYS], ctx_sb[:, b, k * P:(k + 1) * P], ident[0:KEYS, 0:KEYS])
            ins.then_inc(ctxT_in_psum, 1)
            pe.wait_ge(ctxT_ready, 1)
            pe.wait_ge(kv_weights_loaded, 32)
            for m in range(DK):
                for k in range(DK):
                    ins = pe.matmul(bank[1][:, m * B * KEYS:(m + 1) * B * KEYS], wk_sb[:, k, m * P:(m + 1) * P],
                                    ctxT[:, k, :], start=k == 0, stop=k == DK - 1)
            ins.then_inc(kT_in_psum, 1)
            for b in range(B):
                for k in range(DK):
                    ins = pe.matmul(bank[2][0:KEYS, b * D:(b + 1) * D], ctxT[:, k, b * KEYS:(b + 1) * KEYS],
                                    wv_sb[:, k, :], start=k == 0, stop=k == DK - 1)
            ins.then_inc(v_in_psum, 1)

            def transpose_xn(t, parity):
                pe.wait_ge(xn_ready, t + 1)
                for k in range(DK):
                    ins = pe.transpose(bank_x[:, k * P:(k + 1) * P], xn[:, parity, k * P:(k + 1) * P], ident[:, :])
                ins.then_inc(xnT_in_psum, 1)

            def project_q(t, parity):
                pe.wait_ge(xnT_ready, t + 1)
                for m in range(DK):
                    for k in range(DK):
                        ins = pe.matmul(q_psum[:, m, :], wq_sb[:, k, m * P:(m + 1) * P], xnT[:, parity, k, :],
                                        start=k == 0, stop=k == DK - 1)
                ins.then_inc(q_in_psum, 1)

            def attention_step(t, parity):
                other = 1 - parity
                if middle(t, 0, TT):
                    pe.wait_ge(q_ready, t + 1)
                    if middle(t, 1, TT):
                        pe.wait_ge(shifted_ready, t)
                    for m, h0, h1 in ((0, 0, 6), (0, 6, 8), (1, 8, 12), (1, 12, 16)):
                        target = scores_last if h0 // BANK_HEADS == 2 else score_banks[:, h0 // BANK_HEADS, :]
                        at = h0 % BANK_HEADS * KEYS
                        half0 = m * HEADS_HALF
                        ins = pe.matmul(target[:, at:at + (h1 - h0) * KEYS], qT[:, parity, m, :],
                                        kblock[:, parity, m, h0 - half0:h1 - half0, :].rearrange("p h k -> p (h k)"),
                                        start=True, stop=True)
                    ins.then_inc(scores_in_psum, 1)
                if middle(t, 2, TT + 2):
                    pe.wait_ge(o_ready, t - 1)
                    if middle(t, 3, TT + 2) and not (isinstance(t, int) and t < 3):
                        pe.wait_ge(x1_ready, t - 2)
                    for k in range(DK):
                        ins = pe.transpose(bank_o[:, k * P:(k + 1) * P], o_sb[:, parity, k * P:(k + 1) * P], ident[:, :])
                    ins.then_inc(oT_in_psum, 1)
                if middle(t, 0, TT - 1):
                    transpose_xn(t + 1, other)
                if middle(t, 1, TT + 1):
                    pe.wait_ge(probs_ready, t)
                    for g in range(3):
                        if middle(t, 2, TT + 1) or g == 2:
                            pe.wait_ge(probsT_ready, (t - 1) * 3 + g - 1)
                        for c in range(4 * g, min(4 * g + 4, PCH)):
                            ins = pe.transpose(bank_p[(3 * other + g) % 2][:, (c % 4) * P:(c % 4 + 1) * P],
                                               probs[:, other, c * P:(c + 1) * P], ident[:, :])
                        ins.then_inc(probsT_in_psum, 1)
                if middle(t, 2, TT + 2):
                    pe.wait_ge(oT_ready, t - 1)
                    for k in range(DK):
                        ins = pe.matmul(bank_o[:, D:2 * D], oT[:, parity, k, :], wo_sb[:, k, :],
                                        start=k == 0, stop=k == DK - 1)
                    ins.then_inc(attn_in_psum, 1)
                if middle(t, 0, TT - 1):
                    project_q(t + 1, other)
                if middle(t, 1, TT + 1):
                    pe.wait_ge(probsT_ready, t * 3)
                    if middle(t, 2, TT + 1):
                        pe.wait_ge(o_ready, t - 1)
                    for c in range(PCH):
                        ins = pe.matmul(bank_pv[:, head0[c] * VW:(head0[c] + heads_in[c]) * VW], probsT[:, other, c, :],
                                        vblock[:, other, c, 0:heads_in[c], :].rearrange("p s w -> p (s w)"),
                                        start=c == 0, stop=c == PCH - 1, skip_group_check=True)
                    ins.then_inc(pv_in_psum, 1)

            pe.wait_ge(kT_ready, 1)
            pe.wait_ge(v_ready, B)
            transpose_xn(0, 0)
            pe.wait_ge(qo_loaded, 48)
            project_q(0, 0)
            pe.wait_ge(blocks_ready, 3 * B)
            run_steps(pe, attention_step, 2, TT - 2, TT + 2)

            def gate_step(t, parity):
                pe.wait_ge(xg_ready, t + 1)
                if middle(t, 2, TT) and not (isinstance(t, int) and t < 2):
                    pe.wait_ge(xgT_ready, t - 1)
                for k in range(DK):
                    ins = pe.transpose(bank_p[parity][:, k * P:(k + 1) * P], xg[:, parity, k * P:(k + 1) * P], ident[:, :])
                ins.then_inc(xgT_in_psum, 1)
                pe.wait_ge(xgT_ready, t + 1)
                for k in range(DK):
                    ins = pe.matmul(bank[2][:, bass.ds(t * E, E)], xgT[:, parity, k, :], wg_sb[:, k, :],
                                    start=k == 0, stop=k == DK - 1)
                ins.then_inc(logits_in_psum, 1)

            run_steps(pe, gate_step, 2, TT, TT)
            pe.wait_ge(sel_ready, 1)
            sel_flat = sel[:, :, :].rearrange("p t e -> p (t e)")
            pe.matmul(bank[0][:, 0:TT * E], before_b[:, :], sel_flat, start=True, stop=True)
            pe.matmul(bank[1][:, 0:TT * E], ones_b[:, :], sel_flat, start=True, stop=True).then_inc(ranks_in_psum, 1)

            pe.wait_ge(tables_ready, 1)
            pe.wait_ge(experts_loaded, 16 * 3 * E)

            def transpose_x(j, parity):
                pe.wait_ge(tile_loaded[parity], (j // 2) * 16 + 16)
                for k in range(DK):
                    ins = pe.transpose(bank[0][:, k * P:(k + 1) * P], xt[:, parity, k * P:(k + 1) * P], ident[:, :])
                ins.then_inc(xT_in_psum, 1)

            def expert_of(j):
                return pe.value_load(tile_expert_i[0:1, bass.ds(j, 1)], min_val=0, max_val=E - 1)

            def expert_step(j, parity):
                other = 1 - parity
                if middle(j, 0, NT):
                    e = expert_of(j)
                    pe.wait_ge(xT_ready, j + 1)
                    for k in range(DK):
                        if k == 0 and (not isinstance(j, int) or j >= 2):
                            pe.wait_ge(silu_ready, j - 1)
                        ins = pe.matmul(u_bank(parity), xT[:, parity, k, :], w1_sb[:, bass.ds(e, 1), k, :],
                                        start=k == 0, stop=k == DK - 1)
                    ins.then_inc(u_in_psum, 1)
                if middle(j, 1, NT + 1):
                    pe.wait_ge(h_ready, j)
                    if not isinstance(j, int) or j >= 2:
                        pe.wait_ge(hT_ready, j - 1)
                    for k in range(HK):
                        ins = pe.transpose(bank[1][:, k * P:(k + 1) * P], h[:, other, k * P:(k + 1) * P], ident[:, :])
                    ins.then_inc(hT_in_psum, 1)
                if middle(j, 0, NT):
                    for k in range(DK):
                        ins = pe.matmul(v_bank(parity), xT[:, parity, k, :], w2_sb[:, bass.ds(e, 1), k, :],
                                        start=k == 0, stop=k == DK - 1)
                    ins.then_inc(v2_in_psum, 1)
                if middle(j, 0, NT - 1):
                    pe.wait_ge(xT_ready, j + 1)
                    transpose_x(j + 1, other)
                if middle(j, 1, NT + 1):
                    e_before = expert_of(j - 1)
                    pe.wait_ge(hT_ready, j)
                    if not isinstance(j, int) or j >= 3:
                        pe.wait_ge(y_ready, j - 2)
                    for k in range(HK):
                        ins = pe.matmul(y_bank(other), hT[:, other, k, :], w3_sb[:, bass.ds(e_before, 1), k, :],
                                        start=k == 0, stop=k == HK - 1)
                    ins.then_inc(y_in_psum, 1)

            transpose_x(0, 0)
            run_steps(pe, expert_step, 4, NT - 1, NT + 1)

        @block.vector
        def _(dve):
            steps = [0]

            def done(ins):
                steps[0] += 1
                ins.then_inc(dve_step, 1)
                dve.wait_ge(dve_step, steps[0])

            dve.memset(v_sb[:, :, :, HD:VW], 1.0).then_inc(v_ready, 1)
            dve.memset(vflat[:, :, :, :], 0.0).then_inc(vflat_cleared, 1)
            dve.wait_ge(x_loaded, 16 * B)
            for t in range(TT):
                ins = dve.bn_stats(st1[:, t, :], x_sb[:, t, :])
            done(ins)
            for t in range(TT):
                ins = dve.bn_aggr(mv1[:, t, :], st1[:, t, :])
            done(ins)
            dve.tensor_scalar(std1[:, :], mv1[:, :, 1:2].rearrange("p t o -> p (t o)"), EPS, None, ALU.add).then_inc(var1_ready, 1)
            dve.wait_ge(small_loaded, 96)
            dve.wait_ge(kT_in_psum, 1)
            for m in range(DK):
                ins = dve.tensor_scalar(kT[:, m, :], bank[1][:, m * B * KEYS:(m + 1) * B * KEYS], bk_sb[:, m:m + 1],
                                        None, ALU.add)
            ins.then_inc(kT_ready, 1)
            dve.wait_ge(kT_ready, 1)
            dve.wait_ge(v_in_psum, 1)
            for b in range(B):
                dve.tensor_tensor(v_sb[:, b, :, 0:HD], bank[2][0:KEYS, b * D:(b + 1) * D].rearrange("p (h d) -> p h d", h=HEADS),
                                  bv_sb[:, :].rearrange("p (h d) -> p h d", h=HEADS), ALU.add).then_inc(v_ready, 1)
            dve.wait_ge(std1_ready, 1)
            done(dve.reciprocal(rstd1[:, :], std1[:, :]))

            def normalise_x(t, parity):
                dve.tensor_scalar(xn[:, parity:parity + 1, :], x_sb[:, bass.ds(t, 1), :], mv1[:, bass.ds(t, 1), 0:1],
                                  rstd1[:, bass.ds(t, 1)], ALU.subtract, ALU.mult).then_inc(xn_ready, 1)

            def bias_q(t, parity):
                dve.wait_ge(q_in_psum, t + 1)
                dve.tensor_tensor(qT[:, parity, :, :], q_psum, bcast(bq_sb[:, :], 2, P), ALU.add).then_inc(q_ready, 1)

            normalise_x(0, 0)
            normalise_x(1, 1)
            dve.wait_ge(pool_step, N_POOL_SETUP[0])
            for b in range(B):
                for m in range(DK):
                    dve.tensor_tensor(kblock[:, b, m, :, :], bcast(kT[:, m, b * KEYS:(b + 1) * KEYS], 1, HEADS_HALF),
                                      bcast(kmask[:, :], 2, KEYS), ALU.mult).then_inc(blocks_ready, 1)
            bias_q(0, 0)
            dve.wait_ge(vflat_loaded, 32 * B)
            for b in range(B):
                dve.tensor_tensor(vblock[:, b, :, :, :], bcast(vflat[:, b, :, :], 2, SPAN),
                                  bcast(vmask[:, :, :], 3, VW), ALU.mult).then_inc(blocks_ready, 1)
            dve.wait_ge(residual_ready, 2)
            dve.wait_ge(tanh_ready, 1)

            def attention_step(t, parity):
                other = 1 - parity
                if middle(t, 2, TT + 2):
                    dve.wait_ge(pv_in_psum, t - 1)
                    dve.reciprocal(rden[:, parity:parity + 1, :],
                                   pv_psum[:, :, HD:VW].rearrange("p h o -> p o h")).then_inc(rden_ready, 1)
                    dve.wait_ge(rden_ready, t - 1)
                    dve.tensor_tensor(o_sb[:, parity, :].rearrange("p (h d) -> p h d", h=HEADS), pv_psum[:, :, 0:HD],
                                      bcast(rden[:, parity, :], 2, HD), ALU.mult).then_inc(o_ready, 1)
                if middle(t, 0, TT):
                    dve.wait_ge(scores_in_psum, t + 1)
                    s01 = score_banks[:, :, 0:BANK_HEADS * KEYS].rearrange("p b (h k) -> p b h k", k=KEYS)
                    s2 = scores_last[:, 0:(HEADS - 2 * BANK_HEADS) * KEYS].rearrange("p (h k) -> p h k", k=KEYS)
                    nm01 = negmax[:, parity, 0:2 * BANK_HEADS].rearrange("p (b h) -> p b h", b=2)
                    nm2 = negmax[:, parity, 2 * BANK_HEADS:HEADS]
                    dve.tensor_reduce(nm01, s01, AX_X, ALU.max, negate=True)
                    dve.tensor_reduce(nm2, s2, AX_X, ALU.max, negate=True).then_inc(max_ready, 1)
                    dve.wait_ge(max_ready, t + 1)
                    if middle(t, 2, TT) and not (isinstance(t, int) and t < 2):
                        dve.wait_ge(probs_ready, t - 1)
                    cut = 2 * BANK_HEADS * KEYS
                    for b in range(2):
                        dve.tensor_tensor(
                            shifted[:, parity, b * BANK_HEADS * KEYS:(b + 1) * BANK_HEADS * KEYS].rearrange("p (h k) -> p h k", k=KEYS),
                            s01[:, b, :, :], bcast(nm01[:, b, :], 2, KEYS), ALU.add)
                    dve.tensor_tensor(shifted[:, parity, cut:FLAT].rearrange("p (h k) -> p h k", k=KEYS), s2,
                                      bcast(nm2, 2, KEYS), ALU.add).then_inc(shifted_ready, 1)
                if middle(t, 2, TT + 2):
                    dve.wait_ge(attn_in_psum, t - 1)
                    dve.scalar_tensor_tensor(out=x1[:, bass.ds(t - 2, 1), :], in0=bank_o[:, D:2 * D].unsqueeze(1),
                                             scalar=tg[:, 0:1], in1=x1[:, bass.ds(t - 2, 1), :],
                                             op0=ALU.mult, op1=ALU.add).then_inc(x1_ready, 1)
                if middle(t, 0, TT - 1):
                    bias_q(t + 1, other)
                if middle(t, 2, TT + 2):
                    dve.wait_ge(x1_ready, t - 1)
                    dve.bn_stats(st2[:, bass.ds(t - 2, 1), :], x1[:, bass.ds(t - 2, 1), :]).then_inc(stats_ready, 1)
                if middle(t, 0, TT - 2):
                    normalise_x(t + 2, parity)

            run_steps(dve, attention_step, 2, TT - 2, TT + 2)

            dve.wait_ge(stats_ready, TT)
            dve.tensor_tensor(mean2[:, :].unsqueeze(2), st2[:, :, 1:2], st2[:, :, 4:5], ALU.add)
            dve.tensor_tensor(half_diff[:, :].unsqueeze(2), st2[:, :, 1:2], st2[:, :, 4:5], ALU.subtract)
            done(dve.tensor_tensor(var2[:, :].unsqueeze(2), st2[:, :, 2:3], st2[:, :, 5:6], ALU.add))
            dve.tensor_scalar(mean2[:, :], mean2[:, :], 0.5, None, ALU.mult)
            dve.tensor_scalar(half_diff[:, :], half_diff[:, :], 0.5, None, ALU.mult)
            done(dve.tensor_scalar(var2[:, :], var2[:, :], 1.0 / D, EPS, ALU.mult, ALU.add))
            done(dve.tensor_tensor(half_diff[:, :], half_diff[:, :], half_diff[:, :], ALU.mult))
            dve.tensor_tensor(var2[:, :], var2[:, :], half_diff[:, :], ALU.add).then_inc(var2_ready, 1)
            dve.wait_ge(std2_ready, 1)
            done(dve.reciprocal(rstd2[:, :], std2[:, :]))

            def gate_step(t, parity):
                if middle(t, 2, TT) and not (isinstance(t, int) and t < 2):
                    dve.wait_ge(xg_copied, t - 1)
                    dve.wait_ge(xgT_in_psum, t - 1)
                dve.tensor_scalar(xg[:, parity:parity + 1, :], x1[:, bass.ds(t, 1), :], mean2[:, bass.ds(t, 1)],
                                  rstd2[:, bass.ds(t, 1)], ALU.subtract, ALU.mult).then_inc(xg_ready, 1)

            run_steps(dve, gate_step, 2, TT, TT)
            dve.wait_ge(logits_in_psum, TT)
            done(dve.tensor_copy(logits[:, :, :].rearrange("p t e -> p (t e)"), bank[2][:, 0:TT * E]))
            source = logits
            for c in range(TOPK):
                done(dve.tensor_reduce(best[c][:, :], source[:, :, :], AX_X, ALU.max))
                done(dve.tensor_tensor(scratch[:, :, :], source[:, :, :], bcast(best[c][:, :], 2, E), ALU.is_equal))
                done(dve.tensor_tensor(scratch[:, :, :], scratch[:, :, :], bcast(desc[:, :], 1, TT), ALU.mult))
                done(dve.tensor_reduce(key[c][:, :], scratch[:, :, :], AX_X, ALU.max))
                done(dve.tensor_tensor(onehot[c][:, :, :], scratch[:, :, :], bcast(key[c][:, :], 2, E), ALU.is_equal))
                if c == 0:
                    done(dve.scalar_tensor_tensor(out=logits2[:, :, :], in0=onehot[0][:, :, :], scalar=-3.0e38,
                                                  in1=logits[:, :, :], op0=ALU.mult, op1=ALU.add))
                    source = logits2
            dve.tensor_tensor(sel[:, :, :], onehot[0][:, :, :], onehot[1][:, :, :], ALU.add).then_inc(sel_ready, 1)
            dve.tensor_tensor(gap[:, :], best[1][:, :], best[0][:, :], ALU.subtract).then_inc(gap_ready, 1)
            dve.wait_ge(ranks_in_psum, 1)
            done(dve.tensor_copy(totals[:, :, :], bank[1][:, 0:TT * E].rearrange("p (t e) -> p e t", e=E)))
            flat = "p e t -> p (e t)"
            done(dve.tensor_tensor_scan(upto[:, :, :].rearrange(flat), scan_keep[:, :, :].rearrange(flat),
                                        totals[:, :, :].rearrange(flat), 0.0, ALU.mult, ALU.add))
            dve.tensor_copy(counts_i[:, :].unsqueeze(2), upto[:, :, TT - 1:TT]).then_inc(counts_ready, 1)
            done(dve.tensor_tensor(offset[:, :, :], upto[:, :, :], totals[:, :, :], ALU.subtract))
            done(dve.tensor_tensor(offset[:, :, :], offset[:, :, :], bcast(cap_base[:, :], 2, TT), ALU.add))
            done(dve.tensor_tensor(position[:, :, :], bank[0][:, 0:TT * E].rearrange("p (t e) -> p t e", e=E),
                                   offset[:, :, :].rearrange("p e t -> p t e"), ALU.add))
            for c in range(TOPK):
                done(dve.tensor_tensor(scratch[:, :, :], position[:, :, :], onehot[c][:, :, :], ALU.mult))
                done(dve.tensor_reduce(slot_f[c][:, :], scratch[:, :, :], AX_X, ALU.add))
                done(dve.tensor_copy(slot[c][:, :], slot_f[c][:, :]))
            dve.wait_ge(egap_ready, 1)
            done(dve.tensor_scalar(esum[:, :], egap[:, :], 1.0, None, ALU.add))
            done(dve.reciprocal(p1[:, :], esum[:, :]))
            done(dve.tensor_scalar(p1g[:, :], p1[:, :], tg[:, 1:2], None, ALU.mult))
            done(dve.tensor_tensor(rows[:, :, D + 3:D + 4], p1g[:, :].unsqueeze(2), egap[:, :].unsqueeze(2), ALU.mult))
            dve.tensor_tensor(rows[:, :, D + 2:D + 3], p1g[:, :].unsqueeze(2), rows[:, :, D + 3:D + 4], ALU.subtract)
            done(dve.tensor_scalar(rows[:, :, D + 1:D + 2], key[0][:, :].unsqueeze(2), -1.0, float(E), ALU.mult, ALU.add))
            dve.engine_nop().then_inc(slots_ready, 1)
            done(dve.tensor_tensor(tile_cmp[:, :, :], bcast(upto[:, :, TT - 1], 2, TT), bcast(tile_128[:, :], 1, E), ALU.is_gt))
            done(dve.tensor_reduce(ntiles[:, :], tile_cmp[:, :, :], AX_X, ALU.add))
            done(dve.tensor_tensor_scan(tiles_upto[:, :], ones_f[:, 0:E], ntiles[:, :], 0.0, ALU.mult, ALU.add))
            done(dve.tensor_tensor(past[:, :, :], bcast(tile_no[:, :], 2, E), bcast(tiles_upto[:, :], 1, NT), ALU.is_ge))
            done(dve.tensor_tensor(past_n[:, :, :], past[:, :, :], bcast(ntiles[:, :], 1, NT), ALU.mult))
            dve.tensor_reduce(tile_expert[:, :], past[:, :, 0:E - 1], AX_X, ALU.add)
            done(dve.tensor_reduce(tiles_before[:, :], past_n[:, :, 0:E - 1], AX_X, ALU.add))
            dve.tensor_copy(tile_expert_i[:, :], tile_expert[:, :])
            dve.tensor_scalar(tile_used[:, :].unsqueeze(2), past[:, :, E - 1:E], -1.0, 1.0, ALU.mult, ALU.add)
            done(dve.tensor_tensor(tile_row[:, :], tile_no[:, :], tiles_before[:, :], ALU.subtract))
            done(dve.tensor_scalar(tile_row[:, :], tile_row[:, :], float(P), float(-E * CAPACITY), ALU.mult, ALU.add))
            done(dve.scalar_tensor_tensor(out=tile_row[:, :], in0=tile_expert[:, :], scalar=float(CAPACITY),
                                          in1=tile_row[:, :], op0=ALU.mult, op1=ALU.add))
            done(dve.tensor_tensor(tile_row[:, :], tile_row[:, :], tile_used[:, :], ALU.mult))
            done(dve.tensor_scalar(tile_row[:, :], tile_row[:, :], float(E * CAPACITY), None, ALU.add))
            dve.tensor_copy(tile_row_i[:, :], tile_row[:, :]).then_inc(tables_ready, 1)

            def meta(j, parity):
                dve.wait_ge(tile_loaded[parity], (j // 2) * 16 + 16)
                dve.tensor_scalar(weight1[:, parity:parity + 1], xt[:, parity, D + 1:D + 2], tile_expert[:, bass.ds(j, 1)],
                                  xt[:, parity, D + 2:D + 3], ALU.is_equal, ALU.mult).then_inc(weight1_ready, 1)
                dve.wait_ge(weight1_ready, j + 1)
                dve.tensor_tensor(weight[:, bass.ds(j, 1)], weight1[:, parity:parity + 1], xt[:, parity, D + 3:D + 4], ALU.add)
                dve.tensor_copy(ids[:, bass.ds(j, 1)], xt[:, parity, D:D + 1].bitcast(I32)).then_inc(meta_ready, 1)

            def expert_step(j, parity):
                other = 1 - parity
                if middle(j, 0, NT):
                    meta(j, parity)
                    dve.wait_ge(silu_ready, j + 1)
                    dve.wait_ge(v2_in_psum, j + 1)
                    dve.tensor_tensor(h[:, parity, :], silu[:, parity, :], v_bank(parity), ALU.mult).then_inc(h_ready, 1)
                if middle(j, 1, NT + 1):
                    dve.wait_ge(y_in_psum, j)
                    if not isinstance(j, int) or j >= 3:
                        dve.wait_ge(y_added, (j - 2) * 16)
                    dve.tensor_scalar(y_sb[other], y_bank(other), weight[:, bass.ds(j - 1, 1)], None,
                                      ALU.mult).then_inc(y_ready, 1)

            run_steps(dve, expert_step, 4, NT - 1, NT + 1)


_INS = ['x', 'ctx_1024', 'g_xattn', 'g_ffn', 'L0_xattn_Wq', 'L0_xattn_bq', 'L0_xattn_Wk', 'L0_xattn_bk', 'L0_xattn_Wv',
        'L0_xattn_bv', 'L0_xattn_Wo', 'L0_xattn_bo', 'L0_ffn_Wg', 'L0_ffn_W1', 'L0_ffn_W2', 'L0_ffn_W3']
_OUTS = [((2, 1024, 256), 'float32')]


def kernel(**inputs):
    import numpy as _np
    import concourse.bacc as _bacc
    from concourse import mybir as _mybir
    from concourse.bass_utils import run_bass_kernel_spmd as _run

    nc = _bacc.Bacc("TRN2", target_bir_lowering=False, num_devices=1)
    arrays, args = {}, []
    for name in _INS:
        a = _np.ascontiguousarray(inputs[name])
        arrays[f"in_{name}_dram"] = a
        args.append(nc.dram_tensor(f"in_{name}_dram", a.shape, _mybir.dt.from_np(a.dtype), kind="ExternalInput").ap())
    for i, (shape, dtype) in enumerate(_OUTS):
        dt = _mybir.dt.from_np(_np.dtype(dtype))
        args.append(nc.dram_tensor(f"out_{i}_dram", shape, dt, kind="ExternalOutput").ap())
    flamingo_layer(nc, *args)
    r = _run(nc, [arrays], core_ids=[0])
    got = tuple(r.results[0][f"out_{i}_dram"] for i in range(len(_OUTS)))
    return got[0]
```

```python
from contextlib import ExitStack

import concourse.bass as bass
from concourse import mybir

P = 128
ALU = mybir.AluOpType
ACT = mybir.ActivationFunctionType
AX_X = mybir.AxisListType.X
F32 = mybir.dt.float32
BF16 = mybir.dt.bfloat16
I32 = mybir.dt.int32
U32 = mybir.dt.uint32
F32R = mybir.dt.float32r


def middle(t, low, high):
    return low <= t < high if isinstance(t, int) else True


def run_steps(eng, step, first, last):
    with eng.Fori(first // 2, last // 2) as i:
        for parity in range(2):
            step(i * 2 + parity, parity, i)


def flamingo_layer(nc, x, ctx, g_xattn, g_ffn, wq, bq, wk, bk, wv, bv, wo, bo, wg, w1, w2, w3, out):
    B, S, D = x.shape
    KEYS = ctx.shape[1]
    HD = 16
    HEADS = D // HD
    E, _, HID = w1.shape
    DK = D // P
    HK = HID // P
    T = B * S
    TT = T // P
    HEADS_HALF = P // HD
    FLAT = HEADS * KEYS
    PCH = -(-FLAT // P)
    VW = HD + 1
    BANK_HEADS = 6
    TOPK = 2
    SQ = 1.0 / float(HD) ** 0.5
    EPS = 1e-5
    META = 4
    ROW = D + META
    CAPACITY = T + P
    XS_ROWS = E * CAPACITY + P
    NT = T * TOPK // P + E - 1
    GROUPS = ((0, TT // 2), (TT // 2, TT))
    NG = len(GROUPS)
    NGT = max(b - a for a, b in GROUPS)
    READY = [-(-(b * P * TOPK - E * (P - 1)) // P) for _, b in GROUPS[:-1]] + [NT]
    COLS = max(b - a for a, b in zip([0] + READY, READY))
    LOOP_A = (6, 12)
    LOOP_E = ((NT - 1 - (NT - 1 - 16) // 2 * 2, NT - 1),)
    SCHEDULE = ([("A", t) for t in range(LOOP_A[0])] + [("loop A",) + LOOP_A, ("top", 0, 0), ("A", 12),
                 ("top", 0, 1), ("A", 13), ("weights", 0), ("A", 14), ("slots", 0), ("A", 15), ("A", 16), ("tables", 0),
                 ("A", 17), ("E", 0), ("A", 18), ("E", 1), ("A", 19), ("top", 1, 0), ("E", 2), ("top", 1, 1), ("E", 3),
                 ("ranks", 1), ("weights", 1), ("E", 4), ("slots", 1), ("E", 5), ("tables", 1)]
                + [("E", j) for j in range(6, LOOP_E[0][0])] + [("loop E",) + r for r in LOOP_E]
                + [("E", NT - 1), ("E", NT)])
    SPLIT = (2, 2 + 2 * E)
    PIECE = 512
    PIECES = 3 * DK * HID // PIECE
    RANK_STEP = 13
    assert HID == PIECE and PIECES == 6 and HK * D == 2 * PIECE
    assert B == 2 and S % P == 0 and DK == 2 and HEADS == 16 and TT % 2 == 0 and NT % 2 == 1
    head0 = [c * P // KEYS for c in range(PCH)]
    heads_in = [min(c * P + P - 1, FLAT - 1) // KEYS - head0[c] + 1 for c in range(PCH)]
    SPAN = max(heads_in)

    xs = nc.dram_tensor("sorted_rows", (XS_ROWS, ROW), F32).ap()
    acc = nc.dram_tensor("accumulator", (T + P, D), F32).ap()
    vflat_dram = nc.dram_tensor("values_by_head", (B, PCH * P, VW), F32).ap()

    with ExitStack() as stack:
        def sb(name, shape, dt=F32):
            return stack.enter_context(nc.sbuf_tensor(name, shape, dt))

        def sem(name):
            return stack.enter_context(nc.semaphore(name))

        bank = [stack.enter_context(nc.psum_tensor(f"bank{i}", [P, 512], F32)) for i in range(6)]
        score_banks = stack.enter_context(nc.psum_tensor("score_banks", [P, 2, 512], F32))

        ident = sb("ident", [P, P])
        ones_f = sb("ones_f", [P, P])
        before_b = sb("before_b", [P, P], BF16)
        ones_b = sb("ones_b", [P, P], BF16)
        kmask = sb("kmask", [P, HEADS_HALF])
        vmask = sb("vmask", [P, PCH, SPAN])
        expert_step_c = sb("expert_step_c", [P, NG, E])
        desc = sb("desc", [P, E])
        cap_base = sb("cap_base", [P, E])
        tile_no = sb("tile_no", [P, NT])
        tile_128 = sb("tile_128", [P, TT])
        scan_keep = sb("scan_keep", [P, E, NGT])

        wqo_sb = sb("wqo_sb", [P, 2, DK, D])
        wq_sb, wo_sb = wqo_sb[:, 0, :, :], wqo_sb[:, 1, :, :]
        wg_sb = sb("wg_sb", [P, DK, E])
        bq_sb = sb("bq_sb", [P, DK])
        bk_sb = sb("bk_sb", [P, DK])
        bo_sb = sb("bo_sb", [P, D])
        gates = sb("gates", [P, 2])
        tg = sb("tg", [P, 2])
        wh_sb = sb("wh_sb", [P, E, PIECES, PIECE], F32R)
        low_words, kblock_words = PIECES * PIECE // 2, B * DK * HEADS_HALF * KEYS
        low_area = sb("low_area", [P, (E - 1) * low_words + kblock_words])
        wl_sb = low_area[:, 0:E * low_words].bitcast(BF16).rearrange("p (e c n) -> p e c n", e=E, c=PIECES)
        w_piece = sb("w_piece", [P, 3, PIECE])
        pad_rows = w_piece[:, 0, 0:ROW]
        xTh = sb("xTh", [P, DK, P], F32R)
        hTh = sb("hTh", [P, HK, P], F32R)
        setup_at = [(E - 1) * low_words]

        def setup_buffer(words, partitions=P):
            setup_at[0] -= words
            return low_area[0:partitions, setup_at[0]:setup_at[0] + words]

        ctx_sb = setup_buffer(B * D, KEYS).rearrange("p (b d) -> p b d", b=B)
        wk_sb, wv_sb = (setup_buffer(DK * D).rearrange("p (k n) -> p k n", k=DK) for _ in range(2))
        bv_sb = setup_buffer(D, KEYS)
        ctxT = setup_buffer(DK * B * KEYS).rearrange("p (k n) -> p k n", k=DK)
        kT = setup_buffer(DK * B * KEYS).rearrange("p (k n) -> p k n", k=DK)
        v_sb = setup_buffer(B * HEADS * VW, KEYS).rearrange("p (b h w) -> p b h w", b=B, h=HEADS)
        vflat = setup_buffer(B * PCH * VW).rearrange("p (b c w) -> p b c w", b=B, c=PCH)
        assert setup_at[0] >= 0
        kblock = low_area[:, (E - 1) * low_words:].rearrange("p (b m h k) -> p b m h k", b=B, m=DK, h=HEADS_HALF)
        vblock = sb("vblock", [P, B, PCH, SPAN, VW])

        rows = sb("rows", [P, TT, ROW])
        x_sb = x1 = rows[:, :, 0:D]
        mv1 = sb("mv1", [P, TT, 2])
        var1 = sb("var1", [P, TT])
        shift1 = sb("shift1", [P, TT])
        eps = sb("eps", [P, TT])
        minus_half = sb("minus_half", [P, TT])
        rstd1 = sb("rstd1", [P, TT])
        small_area = sb("small_area", [P, 5 * D])
        xn, o_sb = small_area[:, 0:D], small_area[:, D:2 * D]
        xnT, qT, oT = (small_area[:, a * D:(a + 1) * D].rearrange("p (k n) -> p k n", k=DK) for a in range(2, 5))
        negmax = sb("negmax", [P, 2, HEADS])
        probs = sb("probs", [P, PCH * P])
        shifted = probs[:, 0:FLAT]
        before = shifted[:, 0:P]
        st1 = shifted[:, P:P + 6 * TT].rearrange("p (t s) -> p t s", t=TT)
        desc_i, cap_base_i, tile_no_i, tile_128_i = (
            shifted[:, (2 + a) * P:(2 + a) * P + n].bitcast(I32) for a, n in enumerate((E, E, NT, TT)))
        probsT = sb("probsT", [P, PCH + DK, P])
        rden = sb("rden", [P, 2, HEADS])
        st2 = sb("st2", [P, 2, 6])
        mv2 = sb("mv2", [P, 2, 2])
        var2 = sb("var2", [P, 2])
        rstd2 = sb("rstd2", [P, 2])
        shift2 = sb("shift2", [P, 2])
        xg = sb("xg", [P, D])

        logits = sb("logits", [P, TT, E])
        best = [sb(f"best{c}", [P, NGT]) for c in range(TOPK)]
        key = [sb(f"key{c}", [P, NGT]) for c in range(TOPK)]
        onehot = [sb(f"onehot{c}", [P, NGT, E]) for c in range(TOPK)]
        scratch = sb("scratch", [P, NGT, E])
        logits2 = sb("logits2", [P, NGT, E])
        gap = sb("gap", [P, NGT])
        egap = sb("egap", [P, NGT])
        esum = sb("esum", [P, NGT])
        p1 = sb("p1", [P, NGT])
        p1g = sb("p1g", [P, NGT])
        sel = sb("sel", [P, NGT, E], BF16)
        ranks = sb("ranks", [P, 2, NGT, E])
        totals = sb("totals", [P, E, NGT])
        upto = sb("upto", [P, E, NGT])
        position = logits2
        counts = sb("counts", [P, NG, E])
        slot_f = [sb(f"slot_f{c}", [P, NGT]) for c in range(TOPK)]
        slot = [sb(f"slot{c}", [P, TT], I32) for c in range(TOPK)]
        blocks = sb("blocks", [P, NG, E])
        blocks_new = sb("blocks_new", [P, NG, E])
        blocks_upto = sb("blocks_upto", [P, NG, E])
        lead = sb("lead", [P, NG, E])
        lead_step = sb("lead_step", [P, NG, E])
        counts_i = sb("counts_i", [P, E], I32)
        NV = NG * E
        past_area = probsT[:, :, :].rearrange("p c n -> p (c n)")[:, 2 * D:]
        weighted_area = low_area[:, E * low_words:]
        assert max(E * TT, COLS * NV) <= (PCH + DK) * P - 2 * D
        tile_expert = sb("tile_expert", [P, NT])
        tile_expert_i = sb("tile_expert_i", [P, NT], I32)
        tile_used = sb("tile_used", [P, COLS])
        tile_row = sb("tile_row", [P, COLS])
        tile_row_i = sb("tile_row_i", [P, NT], I32)

        xTl = small_area[:, 0:D // 2].bitcast(BF16).rearrange("p (k n) -> p k n", k=DK)
        hTl = small_area[:, D:D + HID // 2].bitcast(BF16).rearrange("p (k n) -> p k n", k=HK)
        silu = wqo_sb[:, 0, :, :].rearrange("p k n -> p (k n)")
        h = probs[:, 2 * ROW:2 * ROW + HID]
        xt = probs[:, 0:2 * ROW].rearrange("p (a f) -> p a f", a=2)
        assert 2 * ROW + HID <= PCH * P
        y_sb = [probsT[:, c * DK:(c + 1) * DK, :].rearrange("p k n -> p (k n)") for c in range(2)]
        weight1 = sb("weight1", [P, 2])
        weight = sb("weight", [P, NT])
        ids = sb("ids", [P, NT], I32)

        ctx_loaded = sem("ctx_loaded")
        kv_weights_loaded = sem("kv_weights_loaded")
        small_loaded = sem("small_loaded")
        x_loaded = sem("x_loaded")
        qo_loaded = sem("qo_loaded")
        pool_step = sem("pool_step")
        tanh_ready = sem("tanh_ready")
        ctxT_in_psum = sem("ctxT_in_psum")
        ctxT_ready = sem("ctxT_ready")
        kT_in_psum = sem("kT_in_psum")
        kT_ready = sem("kT_ready")
        v_in_psum = sem("v_in_psum")
        v_ready = sem("v_ready")
        v_stored = sem("v_stored")
        vflat_cleared = sem("vflat_cleared")
        vflat_loaded = sem("vflat_loaded")
        blocks_ready = sem("blocks_ready")
        dve_step = sem("dve_step")
        residual_ready = sem("residual_ready")
        xn_ready = sem("xn_ready")
        xnT_in_psum = sem("xnT_in_psum")
        xnT_ready = sem("xnT_ready")
        q_in_psum = sem("q_in_psum")
        q_ready = sem("q_ready")
        scores_in_psum = sem("scores_in_psum")
        max_ready = sem("max_ready")
        shifted_ready = sem("shifted_ready")
        probs_ready = sem("probs_ready")
        probsT_in_psum = sem("probsT_in_psum")
        probsT_ready = sem("probsT_ready")
        pv_in_psum = sem("pv_in_psum")
        rden_ready = sem("rden_ready")
        o_ready = sem("o_ready")
        oT_in_psum = sem("oT_in_psum")
        oT_ready = sem("oT_ready")
        attn_in_psum = sem("attn_in_psum")
        x1_ready = sem("x1_ready")
        st2_ready = sem("st2_ready")
        w_high_loaded = sem("w_high_loaded")
        w_piece_loaded = [sem(f"w_piece_loaded{k}") for k in range(3)]
        w_low_ready = sem("w_low_ready")
        pad_ready = sem("pad_ready")
        stats_ready = sem("stats_ready")
        acc_written = sem("acc_written")
        xg_ready = sem("xg_ready")
        logits_in_psum = sem("logits_in_psum")
        rstd2_ready = sem("rstd2_ready")
        rows_kept = sem("rows_kept")
        pv_bank_read = sem("pv_bank_read")
        stats1_ready = sem("stats1_ready")
        xn_scale_ready = sem("xn_scale_ready")
        gap_ready = sem("gap_ready")
        egap_ready = sem("egap_ready")
        sel_ready = sem("sel_ready")
        ranks_in_psum = sem("ranks_in_psum")
        slots_ready = sem("slots_ready")
        counts_ready = sem("counts_ready")
        tables_ready = sem("tables_ready")
        rows_scattered = [sem(f"rows_scattered{g}") for g in range(NG)]
        padding_written = sem("padding_written")
        tile_loaded = [sem(f"tile_loaded{c}") for c in range(2)]
        xT_in_psum = sem("xT_in_psum")
        xTh_ready = sem("xTh_ready")
        xTl_ready = sem("xTl_ready")
        u_in_psum = sem("u_in_psum")
        v2_in_psum = sem("v2_in_psum")
        silu_ready = sem("silu_ready")
        weight1_ready = sem("weight1_ready")
        meta_ready = sem("meta_ready")
        h_ready = sem("h_ready")
        hT_in_psum = sem("hT_in_psum")
        hTh_ready = sem("hTh_ready")
        hTl_ready = sem("hTl_ready")
        y_in_psum = sem("y_in_psum")
        y_ready = sem("y_ready")
        y_added = sem("y_added")
        out_written = sem("out_written")

        bank_x, bank_o, bank_pv = bank[0], bank[1], bank[2]
        bank_p = [bank[3], bank[4]]
        scores_last = bank[5]
        logits_psum = bank_pv[:, HEADS * VW:HEADS * VW + E]
        ranks_psum = bank_pv[:, 512 - 2 * NGT * E:512].rearrange("p (a t e) -> p a t e", a=2, e=E)
        assert HEADS * VW + E <= 512 - 2 * NGT * E
        q_psum = bank_x[:, D:2 * D].rearrange("p (k n) -> p k n", k=DK)
        pv_psum = bank_pv[:, 0:HEADS * VW].rearrange("p (h w) -> p h w", h=HEADS)

        N_POOL_SETUP = [0]

        u_psum, v_psum = score_banks[:, 0, :], score_banks[:, 1, :]
        xT_psum, hT_psum, y_psum = scores_last[:, 0:D], bank_x[:, :], bank_o[:, 0:D]

        def bcast(ap, axis, n):
            shape = list(ap.shape)
            shape.insert(axis, n)
            return ap.unsqueeze(axis).to_broadcast(shape)

        def token_view(dram, b):
            return dram[b * S:(b + 1) * S, :].rearrange("(m p) d -> p m d", p=P)

        def tiles_of(tensor, b):
            return tensor[:, :, :].rearrange("p (m b) d -> p m b d", b=B)[:, :, b, :]

        def upper(ap):
            return ap.bitcast(BF16).rearrange("p (n two) -> p n two", two=2)[:, :, 1]

        def chunk_groups(t, g):
            if isinstance(t, int) and t > TT:
                return 3 * TT + t - TT
            return (t - 1) * 3 + g + 1

        block = stack.enter_context(nc.Block())

        @block.gpsimd
        def _(pool):
            def done(ins):
                N_POOL_SETUP[0] += 1
                ins.then_inc(pool_step, 1)
                pool.wait_ge(pool_step, N_POOL_SETUP[0])

            done(pool.memset(ones_f[:, :], 1.0))
            done(pool.affine_select(out=ident[:, :], in_=ones_f[:, :], compare_op=ALU.is_equal, fill=0.0,
                                    base=0, pattern=[[-1, P]], channel_multiplier=1))
            done(pool.affine_select(out=kmask[:, :], in_=ones_f[:, 0:HEADS_HALF], compare_op=ALU.is_ge, fill=0.0,
                                    base=0, pattern=[[-HD, HEADS_HALF]], channel_multiplier=1))
            done(pool.affine_select(out=kmask[:, :], in_=kmask[:, :], compare_op=ALU.is_ge, fill=0.0,
                                    base=HD - 1, pattern=[[HD, HEADS_HALF]], channel_multiplier=-1))
            for c in range(PCH):
                pool.affine_select(out=vmask[:, c, :], in_=ones_f[:, 0:SPAN], compare_op=ALU.is_ge, fill=0.0,
                                   base=c * P - KEYS * head0[c], pattern=[[-KEYS, SPAN]],
                                   channel_multiplier=1).then_inc(pool_step, 1)
            N_POOL_SETUP[0] += PCH
            pool.wait_ge(pool_step, N_POOL_SETUP[0])
            for c in range(PCH):
                pool.affine_select(out=vmask[:, c, :], in_=vmask[:, c, :], compare_op=ALU.is_ge, fill=0.0,
                                   base=KEYS * head0[c] + KEYS - 1 - c * P, pattern=[[KEYS, SPAN]],
                                   channel_multiplier=-1).then_inc(pool_step, 1)
            N_POOL_SETUP[0] += PCH
            pool.memset(probs[:, FLAT:PCH * P], 0.0).then_inc(pool_step, 1)
            pool.memset(scan_keep[:, :, :], 1.0).then_inc(pool_step, 1)
            pool.memset(expert_step_c[:, :, :], 1.0).then_inc(pool_step, 1)
            pool.memset(eps[:, :], EPS).then_inc(pool_step, 1)
            pool.memset(minus_half[:, :], -0.5).then_inc(pool_step, 1)
            pool.affine_select(out=before, in_=ones_f[:, :], compare_op=ALU.is_gt, fill=0.0,
                               base=0, pattern=[[1, P]], channel_multiplier=-1).then_inc(pool_step, 1)
            pool.iota(desc_i, pattern=[[-1, E]], base=E, channel_multiplier=0).then_inc(pool_step, 1)
            pool.iota(cap_base_i, pattern=[[CAPACITY, E]], base=0, channel_multiplier=0).then_inc(pool_step, 1)
            pool.iota(tile_no_i, pattern=[[1, NT]], base=0, channel_multiplier=0).then_inc(pool_step, 1)
            pool.iota(tile_128_i, pattern=[[P, TT]], base=0, channel_multiplier=0).then_inc(pool_step, 1)
            pool.iota(rows[:, :, D:D + 1].bitcast(I32), pattern=[[P, TT // B], [S, B], [0, 1]], base=0,
                      channel_multiplier=1).then_inc(pool_step, 1)
            N_POOL_SETUP[0] += 11
            pool.wait_ge(pool_step, N_POOL_SETUP[0])
            pool.memset(scan_keep[:, :, 0:1], 0.0).then_inc(pool_step, 1)
            pool.tensor_copy(before_b[:, :], before).then_inc(pool_step, 1)
            pool.tensor_copy(ones_b[:, :], ones_f[:, :]).then_inc(pool_step, 1)
            pool.tensor_copy(desc[:, :], desc_i).then_inc(pool_step, 1)
            pool.tensor_copy(cap_base[:, :], cap_base_i).then_inc(pool_step, 1)
            pool.tensor_copy(tile_no[:, :], tile_no_i).then_inc(pool_step, 1)
            pool.tensor_copy(tile_128[:, :], tile_128_i).then_inc(pool_step, 1)
            pool.memset(expert_step_c[:, :, E - 1:E], -float(E - 1)).then_inc(pool_step, 1)
            N_POOL_SETUP[0] += 8
            pool.wait_ge(tanh_ready, 1)
            pool.wait_ge(x_loaded, 16 * B)
            pool.tensor_scalar(bo_sb[:, :], bo_sb[:, :], tg[:, 0:1], 0.0, ALU.mult, ALU.add).then_inc(residual_ready, 1)

            pool.wait_ge(stats1_ready, 1)
            pool.tensor_tensor(var1[:, :].unsqueeze(2), mv1[:, :, 1:2], eps[:, :].unsqueeze(2), ALU.add).then_inc(xn_scale_ready, 1)
            pool.wait_ge(xn_scale_ready, 1)
            pool.tensor_tensor(rstd1[:, :], var1[:, :], minus_half[:, :], ALU.pow).then_inc(xn_scale_ready, 1)
            pool.wait_ge(xn_scale_ready, 2)
            pool.tensor_tensor(shift1[:, :].unsqueeze(2), mv1[:, :, 0:1], rstd1[:, :].unsqueeze(2), ALU.mult).then_inc(xn_scale_ready, 1)
            pool.wait_ge(xn_scale_ready, 3)
            pool.tensor_scalar(shift1[:, :], shift1[:, :], -1.0, 0.0, ALU.mult, ALU.add).then_inc(xn_scale_ready, 1)
            pool.wait_ge(xn_scale_ready, 4)

            def normalise_x(t):
                if t >= 1:
                    pool.wait_ge(xnT_in_psum, t)
                pool.tensor_scalar(xn, x_sb[:, t, :], rstd1[:, t:t + 1], shift1[:, t:t + 1],
                                   ALU.mult, ALU.add).then_inc(xn_ready, 1)

            def residual(t):
                pool.tensor_tensor(x1[:, t, :], x_sb[:, t, :], bo_sb[:, :], ALU.add).then_inc(residual_ready, 1)

            def normalise_x1(t):
                p = t % 2
                pool.wait_ge(stats_ready, t + 1)
                pool.tensor_tensor(var2[:, p:p + 1], mv2[:, p, 1:2], eps[:, 0:1], ALU.add).then_inc(rstd2_ready, 1)
                pool.wait_ge(rstd2_ready, 3 * t + 1)
                pool.tensor_tensor(rstd2[:, p:p + 1], var2[:, p:p + 1], minus_half[:, 0:1], ALU.pow).then_inc(rstd2_ready, 1)
                pool.wait_ge(rstd2_ready, 3 * t + 2)
                pool.tensor_scalar(shift2[:, p:p + 1], mv2[:, p, 0:1], rstd2[:, p:p + 1], -1.0, ALU.mult, ALU.mult).then_inc(rstd2_ready, 1)
                pool.wait_ge(rstd2_ready, 3 * t + 3)
                if t >= 1:
                    pool.wait_ge(probsT_in_psum, chunk_groups(t + 2, 2))
                pool.tensor_scalar(xg[:, :], x1[:, t, :], rstd2[:, p:p + 1], shift2[:, p:p + 1],
                                   ALU.mult, ALU.add).then_inc(xg_ready, 1)

            def keep_rows(t):
                p = t % 2
                pool.wait_ge(acc_written, 16 * (t + 1))
                pool.tensor_scalar(rows[:, t, 0:D], x1[:, t, :], rstd2[:, p:p + 1], shift2[:, p:p + 1],
                                   ALU.mult, ALU.add).then_inc(rows_kept, 1)

            def scatter(t):
                for c in range(TOPK):
                    pool.indirect_dma_start(
                        out=xs, out_offset=bass.IndirectOffsetOnAxis(ap=slot[c][:, t:t + 1].bitcast(U32), axis=0),
                        in_=rows[:, t, :], in_offset=None).then_inc(rows_scattered[0 if t < GROUPS[0][1] else 1], 16)

            def add_rows(j):
                pool.wait_ge(y_ready, j + 1)
                if j >= 1:
                    pool.wait_ge(y_added, j * 16)
                pool.indirect_dma_start(
                    out=acc, out_offset=bass.IndirectOffsetOnAxis(ap=ids[:, j:j + 1].bitcast(U32), axis=0),
                    in_=y_sb[j % 2], in_offset=None, compute_op=ALU.add).then_inc(y_added, 16)

            def load_high(e):
                if e >= 1:
                    pool.wait_ge(w_high_loaded, 16 * 3 * e)
                for w, at in ((w1[e], 0), (w2[e], 2), (w3[e], 4)):
                    pool.dma_start(wh_sb[:, e, at:at + 2, :].rearrange("p c n -> p (c n)").rearrange(
                        "p (k n) -> p k n", n=w.shape[1]), w.rearrange("(k p) n -> p k n", p=P)).then_inc(w_high_loaded, 16)

            load_high(0)
            normalise_x(0)
            pool.wait_ge(residual_ready, 1)
            residual(0)
            normalise_x(1)
            to_scatter = []
            for what, *at in SCHEDULE:
                if what == "loop A":
                    steps = range(*at)
                elif what in ("A", "E"):
                    steps = at[:1]
                elif what == "loop E":
                    steps = range(*at)
                else:
                    steps = ()
                for t in steps:
                    if what in ("A", "loop A"):
                        if t == SPLIT[1]:
                            pool.wait_ge(w_low_ready, 3 * (SPLIT[1] - SPLIT[0]))
                            pool.memset(pad_rows, 0.0).then_inc(pad_ready, 1)
                            pool.wait_ge(pad_ready, 1)
                            pool.iota(pad_rows[:, D:D + 1].bitcast(I32), pattern=[[0, 1]], base=T,
                                      channel_multiplier=1).then_inc(pad_ready, 1)
                        if t + 1 < TT:
                            residual(t + 1)
                        if 3 <= t < TT + 3:
                            normalise_x1(t - 3)
                        if 4 <= t < TT + 4:
                            keep_rows(t - 4)
                        if t + 2 < TT:
                            normalise_x(t + 2)
                        if t % 2 == 1 and (t + 1) // 2 < E:
                            load_high((t + 1) // 2)
                    elif t >= 1:
                        if t == 1:
                            pool.wait_ge(acc_written, 16 * (TT + 1))
                        add_rows(t - 1)
                    if to_scatter:
                        n = 2 if what == "A" else 3
                        for u in to_scatter[:n]:
                            scatter(u)
                        del to_scatter[:n]
                if what == "slots":
                    g = at[0]
                    pool.wait_ge(slots_ready, 2 * g + 2)
                    pool.wait_ge(rows_kept, GROUPS[g][1])
                    to_scatter += range(*GROUPS[g])
            assert not to_scatter

        @block.sync
        def _(sp):
            sp.dma_start(ctx_sb[:, :, :], ctx.rearrange("b k d -> k b d")).then_inc(ctx_loaded, 16)
            for w, dst in ((wk, wk_sb), (wv, wv_sb)):
                sp.dma_start(dst[:, :, :], w.rearrange("(k p) n -> p k n", p=P)).then_inc(kv_weights_loaded, 16)
            x_rows = x.rearrange("b s d -> (b s) d")
            for b in range(B):
                sp.dma_start(tiles_of(x_sb, b), token_view(x_rows, b)).then_inc(x_loaded, 16)
            for w, dst in ((wq, wq_sb), (wo, wo_sb), (wg, wg_sb)):
                sp.dma_start(dst[:, :, :], w.rearrange("(k p) n -> p k n", p=P)).then_inc(qo_loaded, 16)
            sp.wait_ge(v_ready, B + 1)
            for b in range(B):
                sp.dma_start(vflat_dram[b, 0:FLAT, :].rearrange("(h k) w -> k h w", h=HEADS),
                             v_sb[:, b, :, :]).then_inc(v_stored, 16)
            sp.wait_ge(v_stored, 16 * B)
            sp.wait_ge(vflat_cleared, 1)
            full = FLAT // P
            for b in range(B):
                sp.dma_start(vflat[:, b, 0:full, :],
                             vflat_dram[b, 0:full * P, :].rearrange("(c p) w -> p c w", p=P)).then_inc(vflat_loaded, 16)
                sp.dma_start(vflat[0:FLAT - full * P, b, full, :],
                             vflat_dram[b, full * P:FLAT, :]).then_inc(vflat_loaded, 16)
            for step in range(SPLIT[0], TT + 3):
                t = step - 3
                if t >= 0:
                    sp.wait_ge(x1_ready, t + 1)
                    if t >= 1:
                        sp.wait_ge(acc_written, 16 * t)
                    row = t % B * S + t // B * P
                    sp.dma_start(acc[row:row + P, :], x1[:, t, :]).then_inc(acc_written, 16)
                if step < SPLIT[1]:
                    e, half = (step - SPLIT[0]) // 2, step % 2
                    for k in range(3):
                        n = (step - SPLIT[0]) * 3 + k
                        if n >= 3:
                            sp.wait_ge(w_low_ready, n - 2)
                        w, c = (w1, w2, w3)[(half * 3 + k) // 2], (half * 3 + k) % 2
                        rows_of = DK * P // 2 * (1 if w is not w3 else HK // DK)
                        sp.dma_start(w_piece[:, k, :].rearrange("p (k n) -> p k n", n=w.shape[2]),
                                     w[e, c * rows_of:(c + 1) * rows_of, :].rearrange("(k p) n -> p k n", p=P)
                                     ).then_inc(w_piece_loaded[k], 16)
            sp.wait_ge(pad_ready, 2)
            sp.wait_ge(acc_written, 16 * TT)
            sp.dma_start(acc[T:T + P, :], pad_rows[:, 0:D]).then_inc(acc_written, 16)
            sp.dma_start(xs[E * CAPACITY:XS_ROWS, :], pad_rows).then_inc(padding_written, 16)

            def load(j, parity, pair=None):
                if not isinstance(j, int) or j >= 2:
                    sp.wait_ge(xT_in_psum, j - 1)
                    sp.wait_ge(meta_ready, j - 1)
                row = sp.value_load(tile_row_i[0:1, bass.ds(j, 1)], min_val=0, max_val=XS_ROWS - P)
                sp.dma_start(xt[:, parity, :], xs[bass.ds(row, P), :]).then_inc(tile_loaded[parity], 16)

            sp.wait_ge(tables_ready, 1)
            sp.wait_ge(rows_scattered[0], 16 * TOPK * (GROUPS[0][1] - GROUPS[0][0]))
            sp.wait_ge(probsT_in_psum, 3 * TT)
            for j in range(READY[0]):
                load(j, j % 2)
            sp.wait_ge(tables_ready, 2)
            for e in range(E):
                n = sp.value_load(counts_i[0:1, e:e + 1], min_val=0, max_val=T)
                sp.dma_start(xs[bass.ds(n + e * CAPACITY, P), :], pad_rows).then_inc(padding_written, 16)
            sp.wait_ge(padding_written, 16 * (E + 1))
            sp.wait_ge(rows_scattered[1], 16 * TOPK * (GROUPS[1][1] - GROUPS[1][0]))
            first = READY[0] + READY[0] % 2
            for j in range(READY[0], first):
                load(j, j % 2)
            run_steps(sp, load, first, NT - 1)
            load(NT - 1, (NT - 1) % 2)
            sp.wait_ge(y_added, 16 * NT)
            sp.dma_start(out.rearrange("b s d -> (b s) d"), acc[0:T, :]).then_inc(out_written, 16)
            sp.wait_ge(out_written, 16)

        @block.scalar
        def _(act):
            act.dma_start(gates[:, 0:1], g_xattn.partition_broadcast(P)).then_inc(small_loaded, 16)
            act.dma_start(gates[:, 1:2], g_ffn.partition_broadcast(P)).then_inc(small_loaded, 16)
            act.dma_start(bk_sb[:, :], bk.rearrange("(k p) -> p k", p=P), allow_slow_non_contiguous=True).then_inc(small_loaded, 16)
            act.dma_start(bq_sb[:, :], bq.rearrange("(k p) -> p k", p=P), allow_slow_non_contiguous=True).then_inc(small_loaded, 16)
            act.dma_start(bv_sb[:, :], bv.partition_broadcast(KEYS)).then_inc(small_loaded, 16)
            act.dma_start(bo_sb[:, :], bo.partition_broadcast(P)).then_inc(small_loaded, 16)
            act.wait_ge(small_loaded, 96)
            act.activation(tg[:, :], gates[:, :], ACT.Tanh).then_inc(tanh_ready, 1)
            act.wait_ge(ctxT_in_psum, 1)
            act.copy(ctxT[:, :, :], bank[0][:, 0:DK * B * KEYS].rearrange("p (k n) -> p k n", k=DK)).then_inc(ctxT_ready, 1)

            def evacuate_xnT(t, parity):
                act.wait_ge(xnT_in_psum, t + 1)
                act.copy(xnT.rearrange("p k n -> p (k n)"), bank_x[:, 0:D]).then_inc(xnT_ready, 1)

            def attention_step(t, parity, pair):
                other = 1 - parity
                if middle(t, 2, TT + 2):
                    act.wait_ge(oT_in_psum, t - 1)
                    act.copy(oT.rearrange("p k n -> p (k n)"), bank_o[:, 0:D]).then_inc(oT_ready, 1)
                if middle(t, 0, TT - 1):
                    evacuate_xnT(t + 1, other)
                for g in range(3):
                    of_probs = middle(t, 1, TT + 1)
                    if of_probs or (g == 2 and middle(t, 3, TT + 3)):
                        rows_too = g == 2 and middle(t, 3, TT + 3)
                        c0, c1 = 4 * g if of_probs else PCH, 4 * g + 4 if g < 2 or rows_too else PCH
                        act.wait_ge(probsT_in_psum, chunk_groups(t, g))
                        act.copy(probsT[:, c0:c1, :].rearrange("p k n -> p (k n)"),
                                 bank_p[(3 * other + g) % 2][:, (c0 - 4 * g) * P:(c1 - 4 * g) * P]).then_inc(probsT_ready, 1)
                if middle(t, 0, TT):
                    act.wait_ge(shifted_ready, t + 1)
                    act.activation(shifted, shifted, ACT.Exp, scale=SQ).then_inc(probs_ready, 1)

            evacuate_xnT(0, 0)
            def evacuate_xT(j, parity):
                act.wait_ge(xT_in_psum, j + 1)
                act.copy(xTh.rearrange("p k n -> p (k n)"), xT_psum).then_inc(xTh_ready, 1)

            def expert_step(j, parity, pair):
                other = 1 - parity
                if middle(j, 0, NT):
                    act.wait_ge(u_in_psum, j + 1)
                    if not isinstance(j, int) or j >= 1:
                        act.wait_ge(h_ready, j)
                    act.activation(silu, u_psum, ACT.Silu).then_inc(silu_ready, 1)
                if middle(j, 1, NT + 1):
                    act.wait_ge(hT_in_psum, j)
                    act.copy(hTh.rearrange("p k n -> p (k n)"), hT_psum).then_inc(hTh_ready, 1)
                if middle(j, 0, NT - 1):
                    evacuate_xT(j + 1, other)

            def softmax_exp(g):
                act.wait_ge(gap_ready, g + 1)
                n = GROUPS[g][1] - GROUPS[g][0]
                act.activation(egap[:, 0:n], gap[:, 0:n], ACT.Exp).then_inc(egap_ready, 1)

            for what, *at in SCHEDULE:
                if what == "A":
                    attention_step(at[0], at[0] % 2, at[0] // 2)
                elif what == "loop A":
                    run_steps(act, attention_step, *at)
                elif what == "E":
                    if at[0] == 0:
                        evacuate_xT(0, 0)
                    expert_step(at[0], at[0] % 2, at[0] // 2)
                elif what == "loop E":
                    run_steps(act, expert_step, *at)
                elif what == "top" and at[1] == TOPK - 1:
                    softmax_exp(at[0])

        @block.tensor
        def _(pe):
            pe.wait_ge(pool_step, 2)
            pe.wait_ge(ctx_loaded, 16)
            for b in range(B):
                for k in range(DK):
                    at = (k * B + b) * KEYS
                    ins = pe.transpose(bank[0][:, at:at + KEYS], ctx_sb[:, b, k * P:(k + 1) * P], ident[0:KEYS, 0:KEYS])
            ins.then_inc(ctxT_in_psum, 1)
            pe.wait_ge(ctxT_ready, 1)
            pe.wait_ge(kv_weights_loaded, 32)
            for m in range(DK):
                for k in range(DK):
                    ins = pe.matmul(bank[1][:, m * B * KEYS:(m + 1) * B * KEYS], wk_sb[:, k, m * P:(m + 1) * P],
                                    ctxT[:, k, :], start=k == 0, stop=k == DK - 1)
            ins.then_inc(kT_in_psum, 1)
            for b in range(B):
                for k in range(DK):
                    ins = pe.matmul(bank[2][0:KEYS, b * D:(b + 1) * D], ctxT[:, k, b * KEYS:(b + 1) * KEYS],
                                    wv_sb[:, k, :], start=k == 0, stop=k == DK - 1)
            ins.then_inc(v_in_psum, 1)

            def transpose_xn(t, parity):
                pe.wait_ge(xn_ready, t + 1)
                for k in range(DK):
                    ins = pe.transpose(bank_x[:, k * P:(k + 1) * P], xn[:, k * P:(k + 1) * P], ident[:, :])
                ins.then_inc(xnT_in_psum, 1)

            def project_q(t, parity):
                pe.wait_ge(xnT_ready, t + 1)
                for m in range(DK):
                    for k in range(DK):
                        ins = pe.matmul(q_psum[:, m, :], wq_sb[:, k, m * P:(m + 1) * P], xnT[:, k, :],
                                        start=k == 0, stop=k == DK - 1)
                ins.then_inc(q_in_psum, 1)

            def rank_products(g):
                n = GROUPS[g][1] - GROUPS[g][0]
                pe.wait_ge(sel_ready, g + 1)
                for a, w in ((0, before_b), (1, ones_b)):
                    ins = pe.matmul(ranks_psum[:, a, 0:n, :], w[:, :], sel[:, 0:n, :].rearrange("p t e -> p (t e)"),
                                    start=True, stop=True)
                ins.then_inc(ranks_in_psum, 1)

            def attention_step(t, parity, pair):
                other = 1 - parity
                if middle(t, 0, TT):
                    pe.wait_ge(q_ready, t + 1)
                    if middle(t, 1, TT):
                        pe.wait_ge(shifted_ready, t)
                    for m, h0, h1 in ((0, 0, 6), (0, 6, 8), (1, 8, 12), (1, 12, 16)):
                        target = scores_last if h0 // BANK_HEADS == 2 else score_banks[:, h0 // BANK_HEADS, :]
                        at = h0 % BANK_HEADS * KEYS
                        half0 = m * HEADS_HALF
                        ins = pe.matmul(target[:, at:at + (h1 - h0) * KEYS], qT[:, m, :],
                                        kblock[:, parity, m, h0 - half0:h1 - half0, :].rearrange("p h k -> p (h k)"),
                                        start=True, stop=True)
                    ins.then_inc(scores_in_psum, 1)
                if middle(t, 2, TT + 2):
                    pe.wait_ge(o_ready, t - 1)
                    if middle(t, 3, TT + 2) and not (isinstance(t, int) and t < 3):
                        pe.wait_ge(x1_ready, t - 2)
                    for k in range(DK):
                        ins = pe.transpose(bank_o[:, k * P:(k + 1) * P], o_sb[:, k * P:(k + 1) * P], ident[:, :])
                    ins.then_inc(oT_in_psum, 1)
                if middle(t, 0, TT - 1):
                    transpose_xn(t + 1, other)
                if middle(t, 1, TT + 1):
                    pe.wait_ge(probs_ready, t)
                for g in range(3):
                    of_probs = middle(t, 1, TT + 1)
                    of_rows = g == 2 and middle(t, 3, TT + 3)
                    if of_probs or of_rows:
                        if middle(t, 2, TT + 3) or g == 2:
                            pe.wait_ge(probsT_ready, chunk_groups(t, g) - 2)
                        target = bank_p[(3 * other + g) % 2]
                        for c in range(4 * g, min(4 * g + 4, PCH)):
                            if of_probs:
                                ins = pe.transpose(target[:, (c % 4) * P:(c % 4 + 1) * P],
                                                   probs[:, c * P:(c + 1) * P], ident[:, :])
                        if of_rows:
                            pe.wait_ge(xg_ready, t - 2)
                            for k in range(DK):
                                at = (PCH + k) % 4 * P
                                ins = pe.transpose(target[:, at:at + P], xg[:, k * P:(k + 1) * P], ident[:, :])
                        ins.then_inc(probsT_in_psum, 1)
                if middle(t, 2, TT + 2):
                    pe.wait_ge(oT_ready, t - 1)
                    for k in range(DK):
                        ins = pe.matmul(bank_o[:, D:2 * D], oT[:, k, :], wo_sb[:, k, :],
                                        start=k == 0, stop=k == DK - 1)
                    ins.then_inc(attn_in_psum, 1)
                if middle(t, 0, TT - 1):
                    project_q(t + 1, other)
                if middle(t, 1, TT + 3):
                    if middle(t, 2, TT + 3):
                        pe.wait_ge(pv_bank_read, t - 1)
                    if middle(t, 3, TT + 3):
                        pe.wait_ge(probsT_ready, chunk_groups(t, 2))
                        for k in range(DK):
                            ins = pe.matmul(logits_psum, probsT[:, PCH + k, :], wg_sb[:, k, :],
                                            start=k == 0, stop=k == DK - 1)
                        if isinstance(t, int) and t > TT:
                            ins.then_inc(pv_in_psum, 1)
                    if isinstance(t, int) and t == RANK_STEP:
                        rank_products(0)
                    if middle(t, 1, TT + 1):
                        pe.wait_ge(probsT_ready, t * 3)
                        for c in range(PCH):
                            ins = pe.matmul(bank_pv[:, head0[c] * VW:(head0[c] + heads_in[c]) * VW], probsT[:, c, :],
                                            vblock[:, other, c, 0:heads_in[c], :].rearrange("p s w -> p (s w)"),
                                            start=c == 0, stop=c == PCH - 1, skip_group_check=True)
                        ins.then_inc(pv_in_psum, 1)

            pe.wait_ge(kT_ready, 1)
            pe.wait_ge(v_ready, B)
            transpose_xn(0, 0)
            pe.wait_ge(qo_loaded, 48)
            project_q(0, 0)
            pe.wait_ge(blocks_ready, 3 * B)
            def transpose_x(j, parity):
                pe.wait_ge(tile_loaded[parity], (j // 2) * 16 + 16)
                for k in range(DK):
                    ins = pe.transpose(xT_psum[:, k * P:(k + 1) * P], xt[:, parity, k * P:(k + 1) * P], ident[:, :])
                ins.then_inc(xT_in_psum, 1)

            wh_upper = wh_sb[:, :, :, :].bitcast(BF16).rearrange("p e c (n two) -> p e c n two", two=2)

            def products(psum, high, low, e, piece0, finished, low_ready=None, count=None):
                chunks = high.shape[1]
                width = psum.shape[1]
                at = [(piece0 + k * width // PIECE, k * width % PIECE) for k in range(chunks)]
                for k, (c, n) in enumerate(at):
                    pe.matmul(psum, high[:, k, :], wh_sb[:, bass.ds(e, 1), c, n:n + width], start=k == 0, stop=False)
                for k, (c, n) in enumerate(at):
                    pe.matmul(psum, upper(high[:, k, :]), wl_sb[:, bass.ds(e, 1), c, n:n + width], start=False, stop=False)
                if low_ready is not None:
                    pe.wait_ge(low_ready, count)
                for k, (c, n) in enumerate(at):
                    ins = pe.matmul(psum, low[:, k, :], wh_upper[:, bass.ds(e, 1), c, n:n + width, 1],
                                    start=False, stop=k == chunks - 1)
                ins.then_inc(finished, 1)

            def expert_of(j):
                return pe.value_load(tile_expert_i[0:1, bass.ds(j, 1)], min_val=0, max_val=E - 1)

            def expert_step(j, parity, e, e_before):
                other = 1 - parity
                e_next = None
                if middle(j, 0, NT):
                    pe.wait_ge(xTl_ready, j + 1)
                    products(u_psum, xTh, xTl, e, 0, u_in_psum)
                if middle(j, 1, NT + 1):
                    if isinstance(j, int) and j == NT:
                        pe.wait_ge(h_ready, NT)
                    for k in range(HK):
                        ins = pe.transpose(hT_psum[:, k * P:(k + 1) * P], h[:, k * P:(k + 1) * P], ident[:, :])
                    ins.then_inc(hT_in_psum, 1)
                if middle(j, 0, NT):
                    products(v_psum, xTh, xTl, e, 2, v2_in_psum)
                if middle(j, 0, NT - 1):
                    e_next = expert_of(j + 1)
                    transpose_x(j + 1, other)
                if middle(j, 1, NT + 1):
                    if not isinstance(j, int) or j >= 2:
                        pe.wait_ge(y_ready, j - 1)
                    pe.wait_ge(hTh_ready, j)
                    products(y_psum, hTh, hTl, e_before, 4, y_in_psum, hTl_ready, j)
                return e_next

            e_before = e = None
            for what, *at in SCHEDULE:
                if what == "A":
                    attention_step(at[0], at[0] % 2, at[0] // 2)
                elif what == "loop A":
                    run_steps(pe, attention_step, *at)
                elif what == "E":
                    if at[0] == 0:
                        pe.wait_ge(tables_ready, 1)
                        pe.wait_ge(w_low_ready, 6 * E)
                        pe.wait_ge(shifted_ready, TT)
                        transpose_x(0, 0)
                        e = expert_of(0)
                    if at[0] == 1:
                        pe.wait_ge(x1_ready, TT)
                    if at[0] == READY[0] - 1:
                        pe.wait_ge(tables_ready, 2)
                    e_before, e = e, expert_step(at[0], at[0] % 2, e, e_before)
                elif what == "loop E":
                    kept = [pe.alloc_register(f"expert_kept{i}") for i in range(2)]
                    for reg, value in zip(kept, (e_before, e)):
                        pe.reg_mov(reg, value)

                    def kept_expert(i):
                        return bass.RuntimeValue.of_register_unchecked(kept[i]).with_bounds(min_val=0, max_val=E - 1)

                    with pe.Fori(at[0] // 2, at[1] // 2) as i:
                        e_before, e = kept_expert(0), kept_expert(1)
                        for parity in range(2):
                            e_before, e = e, expert_step(i * 2 + parity, parity, e, e_before)
                        for reg, value in zip(kept, (e_before, e)):
                            pe.reg_mov(reg, value)
                    e_before, e = kept_expert(0), kept_expert(1)
                elif what == "ranks":
                    pe.wait_ge(pv_bank_read, TT + 2)
                    rank_products(at[0])

        @block.vector
        def _(dve):
            steps = [0]

            def done(ins):
                steps[0] += 1
                ins.then_inc(dve_step, 1)
                dve.wait_ge(dve_step, steps[0])

            dve.memset(v_sb[:, :, :, HD:VW], 1.0).then_inc(v_ready, 1)
            dve.memset(vflat[:, :, :, :], 0.0).then_inc(vflat_cleared, 1)
            dve.wait_ge(x_loaded, 16 * B)
            for t in range(TT):
                ins = dve.bn_stats(st1[:, t, :], x_sb[:, t, :])
            done(ins)
            for t in range(TT):
                ins = dve.bn_aggr(mv1[:, t, :], st1[:, t, :])
            ins.then_inc(stats1_ready, 1)
            dve.wait_ge(small_loaded, 96)
            dve.wait_ge(kT_in_psum, 1)
            for m in range(DK):
                ins = dve.tensor_scalar(kT[:, m, :], bank[1][:, m * B * KEYS:(m + 1) * B * KEYS], bk_sb[:, m:m + 1],
                                        None, ALU.add)
            ins.then_inc(kT_ready, 1)
            dve.wait_ge(kT_ready, 1)
            dve.wait_ge(v_in_psum, 1)
            for b in range(B):
                dve.tensor_tensor(v_sb[:, b, :, 0:HD], bank[2][0:KEYS, b * D:(b + 1) * D].rearrange("p (h d) -> p h d", h=HEADS),
                                  bv_sb[:, :].rearrange("p (h d) -> p h d", h=HEADS), ALU.add).then_inc(v_ready, 1)

            def bias_q(t, parity):
                dve.wait_ge(q_in_psum, t + 1)
                dve.tensor_tensor(qT, q_psum, bcast(bq_sb[:, :], 2, P), ALU.add).then_inc(q_ready, 1)

            dve.wait_ge(pool_step, N_POOL_SETUP[0])
            for b in range(B):
                for m in range(DK):
                    dve.tensor_tensor(kblock[:, b, m, :, :], bcast(kT[:, m, b * KEYS:(b + 1) * KEYS], 1, HEADS_HALF),
                                      bcast(kmask[:, :], 2, KEYS), ALU.mult).then_inc(blocks_ready, 1)
            bias_q(0, 0)
            dve.wait_ge(vflat_loaded, 32 * B)
            for b in range(B):
                dve.tensor_tensor(vblock[:, b], bcast(vflat[:, b, :, :], 2, SPAN),
                                  bcast(vmask[:, :, :], 3, VW), ALU.mult).then_inc(blocks_ready, 1)
            dve.wait_ge(tanh_ready, 1)

            def attention_step(t, parity, pair):
                other = 1 - parity
                if middle(t, 3, TT + 3):
                    dve.wait_ge(st2_ready, t - 2)
                if middle(t, 5, TT + 3):
                    dve.wait_ge(rstd2_ready, (t - 4) * 3)
                if middle(t, 2, TT + 2):
                    dve.wait_ge(pv_in_psum, t - 1)
                    dve.reciprocal(rden[:, parity:parity + 1, :],
                                   pv_psum[:, :, HD:VW].rearrange("p h o -> p o h")).then_inc(rden_ready, 1)
                if middle(t, 3, TT + 3):
                    dve.bn_aggr(mv2[:, other, :], st2[:, other, :]).then_inc(stats_ready, 1)
                if middle(t, 2, TT + 2):
                    dve.wait_ge(rden_ready, t - 1)
                    dve.tensor_tensor(o_sb.rearrange("p (h d) -> p h d", h=HEADS), pv_psum[:, :, 0:HD],
                                      bcast(rden[:, parity, :], 2, HD), ALU.mult).then_inc(o_ready, 1)
                if middle(t, 2, TT + 4):
                    if not middle(t, 2, TT + 2):
                        dve.wait_ge(pv_in_psum, t - 1)
                    if isinstance(t, int) and t == RANK_STEP + 1:
                        copy_ranks(0)
                    if middle(t, 4, TT + 4):
                        dve.tensor_copy(logits[:, bass.ds(t - 4, 1), :], logits_psum.unsqueeze(1)).then_inc(pv_bank_read, 1)
                    else:
                        dve.engine_nop().then_inc(pv_bank_read, 1)
                if middle(t, 0, TT):
                    dve.wait_ge(scores_in_psum, t + 1)
                    s01 = score_banks[:, :, 0:BANK_HEADS * KEYS].rearrange("p b (h k) -> p b h k", k=KEYS)
                    s2 = scores_last[:, 0:(HEADS - 2 * BANK_HEADS) * KEYS].rearrange("p (h k) -> p h k", k=KEYS)
                    nm01 = negmax[:, parity, 0:2 * BANK_HEADS].rearrange("p (b h) -> p b h", b=2)
                    nm2 = negmax[:, parity, 2 * BANK_HEADS:HEADS]
                    dve.tensor_reduce(nm01, s01, AX_X, ALU.max, negate=True)
                    dve.tensor_reduce(nm2, s2, AX_X, ALU.max, negate=True).then_inc(max_ready, 1)
                    dve.wait_ge(max_ready, t + 1)
                    if middle(t, 1, TT):
                        dve.wait_ge(probsT_in_psum, t * 3)
                    cut = 2 * BANK_HEADS * KEYS
                    for b in range(2):
                        dve.tensor_tensor(
                            shifted[:, b * BANK_HEADS * KEYS:(b + 1) * BANK_HEADS * KEYS].rearrange("p (h k) -> p h k", k=KEYS),
                            s01[:, b, :, :], bcast(nm01[:, b, :], 2, KEYS), ALU.add)
                    dve.tensor_tensor(shifted[:, cut:FLAT].rearrange("p (h k) -> p h k", k=KEYS), s2,
                                      bcast(nm2, 2, KEYS), ALU.add).then_inc(shifted_ready, 1)
                if middle(t, 2, TT + 2):
                    dve.wait_ge(attn_in_psum, t - 1)
                    dve.wait_ge(residual_ready, t)
                    dve.scalar_tensor_tensor(out=x1[:, bass.ds(t - 2, 1), :], in0=bank_o[:, D:2 * D].unsqueeze(1),
                                             scalar=tg[:, 0:1], in1=x1[:, bass.ds(t - 2, 1), :],
                                             op0=ALU.mult, op1=ALU.add).then_inc(x1_ready, 1)
                if middle(t, 2, TT + 2):
                    dve.wait_ge(x1_ready, t - 1)
                if middle(t, 0, TT - 1):
                    bias_q(t + 1, other)
                if middle(t, 2, TT + 2):
                    dve.bn_stats(st2[:, parity, :], x1[:, bass.ds(t - 2, 1), :]).then_inc(st2_ready, 1)
                if middle(t, *SPLIT):
                    for k in range(3):
                        split_low(t, parity, pair, k)

            def split_low(t, parity, pair, k):
                if k == 0:
                    dve.wait_ge(w_high_loaded, pair * 16 * 3)
                dve.wait_ge(w_piece_loaded[k], (t - SPLIT[0] + 1) * 16)
                at = bass.ds(pair - 1, 1)
                dve.tensor_tensor(wl_sb[:, at, 3 * parity + k, :], w_piece[:, k, :].unsqueeze(1),
                                  wh_sb[:, at, 3 * parity + k, :].bitcast(F32), ALU.subtract).then_inc(w_low_ready, 1)

            def top(g, c):
                t0, t1 = GROUPS[g]
                n = t1 - t0
                source = logits[:, t0:t1, :] if c == 0 else logits2[:, 0:n, :]
                tmp, hot = scratch[:, 0:n, :], onehot[c][:, 0:n, :]
                if c == 0:
                    dve.wait_ge(pv_bank_read, t1 + 2)
                done(dve.tensor_reduce(best[c][:, 0:n], source, AX_X, ALU.max))
                done(dve.tensor_tensor(tmp, source, bcast(best[c][:, 0:n], 2, E), ALU.is_equal))
                done(dve.tensor_tensor(tmp, tmp, bcast(desc[:, :], 1, n), ALU.mult))
                done(dve.tensor_reduce(key[c][:, 0:n], tmp, AX_X, ALU.max))
                done(dve.tensor_tensor(hot, tmp, bcast(key[c][:, 0:n], 2, E), ALU.is_equal))
                if c == 0:
                    done(dve.scalar_tensor_tensor(out=logits2[:, 0:n, :], in0=hot, scalar=-3.0e38, in1=source,
                                                  op0=ALU.mult, op1=ALU.add))
                else:
                    dve.tensor_tensor(sel[:, 0:n, :], onehot[0][:, 0:n, :], hot, ALU.add).then_inc(sel_ready, 1)
                    dve.tensor_tensor(gap[:, 0:n], best[1][:, 0:n], best[0][:, 0:n], ALU.subtract).then_inc(gap_ready, 1)

            def copy_ranks(g):
                n = GROUPS[g][1] - GROUPS[g][0]
                dve.wait_ge(ranks_in_psum, g + 1)
                done(dve.tensor_copy(ranks[:, :, 0:n, :], ranks_psum[:, :, 0:n, :]))

            def slots(g):
                t0, t1 = GROUPS[g]
                n = t1 - t0
                done(dve.tensor_copy(totals[:, :, 0:n], ranks[:, 1, 0:n, :].rearrange("p t e -> p e t")))
                assert n == NGT
                flat = "p e t -> p (e t)"
                done(dve.tensor_tensor_scan(upto[:, :, :].rearrange(flat), scan_keep[:, :, :].rearrange(flat),
                                            totals[:, :, :].rearrange(flat), 0.0, ALU.mult, ALU.add))
                if g == 0:
                    dve.tensor_copy(counts[:, 0, :].unsqueeze(2), upto[:, :, n - 1:n])
                else:
                    dve.tensor_tensor(counts[:, g, :].unsqueeze(2), upto[:, :, n - 1:n], counts[:, g - 1, :].unsqueeze(2), ALU.add)
                done(dve.tensor_tensor(totals[:, :, 0:n], upto[:, :, 0:n], totals[:, :, 0:n], ALU.subtract))
                if g > 0:
                    done(dve.tensor_tensor(totals[:, :, 0:n], totals[:, :, 0:n], bcast(counts[:, g - 1, :], 2, n), ALU.add))
                done(dve.tensor_tensor(totals[:, :, 0:n], totals[:, :, 0:n], bcast(cap_base[:, :], 2, n), ALU.add))
                done(dve.tensor_tensor(position[:, 0:n, :], ranks[:, 0, 0:n, :], totals[:, :, 0:n].rearrange("p e t -> p t e"), ALU.add))
                for c in range(TOPK):
                    done(dve.tensor_tensor(scratch[:, 0:n, :], position[:, 0:n, :], onehot[c][:, 0:n, :], ALU.mult))
                    done(dve.tensor_reduce(slot_f[c][:, 0:n], scratch[:, 0:n, :], AX_X, ALU.add))
                    done(dve.tensor_copy(slot[c][:, t0:t1], slot_f[c][:, 0:n]))
                dve.engine_nop().then_inc(slots_ready, 1)

            def weights(g):
                t0, t1 = GROUPS[g]
                n = t1 - t0
                kept = rows[:, t0:t1, :]
                dve.wait_ge(egap_ready, g + 1)
                done(dve.tensor_scalar(esum[:, 0:n], egap[:, 0:n], 1.0, None, ALU.add))
                done(dve.reciprocal(p1[:, 0:n], esum[:, 0:n]))
                done(dve.tensor_scalar(p1g[:, 0:n], p1[:, 0:n], tg[:, 1:2], None, ALU.mult))
                done(dve.tensor_tensor(kept[:, :, D + 3:D + 4], p1g[:, 0:n].unsqueeze(2), egap[:, 0:n].unsqueeze(2), ALU.mult))
                dve.tensor_tensor(kept[:, :, D + 2:D + 3], p1g[:, 0:n].unsqueeze(2), kept[:, :, D + 3:D + 4], ALU.subtract)
                done(dve.tensor_scalar(kept[:, :, D + 1:D + 2], key[0][:, 0:n].unsqueeze(2), -1.0, float(E), ALU.mult, ALU.add))
                dve.engine_nop().then_inc(slots_ready, 1)

            def tables(g):
                j0, j1 = ([0] + READY)[g], READY[g]
                cols, nv = j1 - j0, (g + 1) * E
                last = g == NG - 1
                if last:
                    marks_area, passed_area, weighted_words = past_area, past_area, weighted_area
                else:
                    marks_area, passed_area = weighted_area, weighted_area[:, E * TT:]
                    weighted_words = passed_area[:, cols * nv:]
                marks = marks_area[:, 0:E * TT].rearrange("p (e t) -> p e t", e=E)
                if last:
                    done(dve.tensor_tensor(marks, bcast(counts[:, g, :], 2, TT), bcast(tile_128[:, :], 1, E), ALU.is_gt))
                else:
                    done(dve.tensor_tensor(marks[:, :, 0:TT - 1], bcast(counts[:, g, :], 2, TT - 1),
                                           bcast(tile_128[:, 1:TT], 1, E), ALU.is_ge))
                done(dve.tensor_reduce(blocks[:, g, :], marks if last else marks[:, :, 0:TT - 1], AX_X, ALU.add))
                if g == 0:
                    done(dve.tensor_copy(blocks_new[:, 0, :], blocks[:, 0, :]))
                else:
                    done(dve.tensor_tensor(blocks_new[:, g, :], blocks[:, g, :], blocks[:, g - 1, :], ALU.subtract))
                flat = "p g e -> p (g e)"
                new, upto_v = blocks_new[:, 0:g + 1, :].rearrange(flat), blocks_upto[:, 0:g + 1, :].rearrange(flat)
                done(dve.tensor_tensor_scan(upto_v, ones_f[:, 0:nv], new, 0.0, ALU.mult, ALU.add))
                done(dve.tensor_tensor(lead[:, g, :], blocks[:, g, :], blocks_upto[:, g, :], ALU.subtract))
                done(dve.scalar_tensor_tensor(out=lead[:, g, :], in0=lead[:, g, :], scalar=float(P), in1=cap_base[:, :],
                                              op0=ALU.mult, op1=ALU.add))
                lead_v, step_v = lead[:, 0:g + 1, :].rearrange(flat), lead_step[:, 0:g + 1, :].rearrange(flat)
                done(dve.tensor_tensor(step_v[:, 0:nv - 1], lead_v[:, 1:nv], lead_v[:, 0:nv - 1], ALU.subtract))
                passed = passed_area[:, 0:cols * nv].rearrange("p (j v) -> p j v", v=nv)
                done(dve.tensor_tensor(passed, bcast(tile_no[:, j0:j1], 2, nv), bcast(upto_v, 1, cols), ALU.is_ge))
                wt = weighted_words[:, 0:cols * (nv - 1)].rearrange("p (j v) -> p j v", v=nv - 1)
                done(dve.tensor_tensor(wt, passed[:, :, 0:nv - 1],
                                       bcast(expert_step_c[:, 0:g + 1, :].rearrange(flat)[:, 0:nv - 1], 1, cols), ALU.mult))
                done(dve.tensor_reduce(tile_expert[:, j0:j1], wt, AX_X, ALU.add))
                dve.tensor_copy(tile_expert_i[:, j0:j1], tile_expert[:, j0:j1])
                done(dve.tensor_tensor(wt, passed[:, :, 0:nv - 1], bcast(step_v[:, 0:nv - 1], 1, cols), ALU.mult))
                row = tile_row[:, 0:cols]
                done(dve.tensor_reduce(row, wt, AX_X, ALU.add))
                done(dve.scalar_tensor_tensor(out=row, in0=tile_no[:, j0:j1], scalar=float(P), in1=row,
                                              op0=ALU.mult, op1=ALU.add))
                if last:
                    used = tile_used[:, 0:cols]
                    done(dve.tensor_scalar(used.unsqueeze(2), passed[:, :, nv - 1:nv], -1.0, 1.0, ALU.mult, ALU.add))
                    done(dve.tensor_scalar(row, row, float(-E * CAPACITY), None, ALU.add))
                    done(dve.tensor_tensor(row, row, used, ALU.mult))
                    done(dve.tensor_scalar(row, row, float(E * CAPACITY), None, ALU.add))
                    dve.tensor_copy(counts_i[:, :], counts[:, g, :])
                dve.tensor_copy(tile_row_i[:, j0:j1], row).then_inc(tables_ready, 1)

            def meta(j, parity):
                dve.wait_ge(tile_loaded[parity], (j // 2) * 16 + 16)
                dve.tensor_scalar(weight1[:, parity:parity + 1], xt[:, parity, D + 1:D + 2], tile_expert[:, bass.ds(j, 1)],
                                  xt[:, parity, D + 2:D + 3], ALU.is_equal, ALU.mult).then_inc(weight1_ready, 1)
                dve.wait_ge(weight1_ready, j + 1)
                dve.tensor_tensor(weight[:, bass.ds(j, 1)], weight1[:, parity:parity + 1], xt[:, parity, D + 3:D + 4], ALU.add)
                dve.tensor_copy(ids[:, bass.ds(j, 1)], xt[:, parity, D:D + 1].bitcast(I32)).then_inc(meta_ready, 1)

            def low_xT(j, parity):
                dve.wait_ge(xTh_ready, j + 1)
                dve.tensor_tensor(xTl.rearrange("p k n -> p (k n)"), xT_psum,
                                  xTh.rearrange("p k n -> p (k n)").bitcast(F32),
                                  ALU.subtract).then_inc(xTl_ready, 1)

            def expert_step(j, parity, pair):
                other = 1 - parity
                if middle(j, 0, NT):
                    if isinstance(j, int) and j == 0:
                        dve.wait_ge(probs_ready, TT)
                    meta(j, parity)
                if middle(j, 1, NT + 1):
                    dve.wait_ge(hTh_ready, j)
                    dve.tensor_tensor(hTl.rearrange("p k n -> p (k n)"), hT_psum,
                                      hTh.rearrange("p k n -> p (k n)").bitcast(F32),
                                      ALU.subtract).then_inc(hTl_ready, 1)
                if middle(j, 0, NT):
                    dve.wait_ge(silu_ready, j + 1)
                    dve.wait_ge(v2_in_psum, j + 1)
                    dve.tensor_tensor(h, silu, v_psum, ALU.mult).then_inc(h_ready, 1)
                if middle(j, 0, NT - 1):
                    low_xT(j + 1, other)
                if middle(j, 1, NT + 1):
                    dve.wait_ge(y_in_psum, j)
                    if not isinstance(j, int) or j >= 3:
                        dve.wait_ge(y_added, (j - 2) * 16)
                    dve.tensor_scalar(y_sb[other], y_psum, weight[:, bass.ds(j - 1, 1)], None,
                                      ALU.mult).then_inc(y_ready, 1)

            for what, *at in SCHEDULE:
                if what == "A":
                    attention_step(at[0], at[0] % 2, at[0] // 2)
                elif what == "loop A":
                    run_steps(dve, attention_step, *at)
                elif what == "E":
                    if at[0] == 0:
                        low_xT(0, 0)
                    expert_step(at[0], at[0] % 2, at[0] // 2)
                elif what == "loop E":
                    run_steps(dve, expert_step, *at)
                elif what == "top":
                    top(*at)
                elif what == "ranks":
                    copy_ranks(at[0])
                else:
                    {"slots": slots, "weights": weights, "tables": tables}[what](at[0])


_INS = ['x', 'ctx_1024', 'g_xattn', 'g_ffn', 'L0_xattn_Wq', 'L0_xattn_bq', 'L0_xattn_Wk', 'L0_xattn_bk', 'L0_xattn_Wv',
        'L0_xattn_bv', 'L0_xattn_Wo', 'L0_xattn_bo', 'L0_ffn_Wg', 'L0_ffn_W1', 'L0_ffn_W2', 'L0_ffn_W3']
_OUTS = [((2, 1024, 256), 'float32')]


def kernel(**inputs):
    import numpy as _np
    import concourse.bacc as _bacc
    from concourse import mybir as _mybir
    from concourse.bass_utils import run_bass_kernel_spmd as _run

    nc = _bacc.Bacc("TRN2", target_bir_lowering=False, num_devices=1)
    arrays, args = {}, []
    for name in _INS:
        a = _np.ascontiguousarray(inputs[name])
        arrays[f"in_{name}_dram"] = a
        args.append(nc.dram_tensor(f"in_{name}_dram", a.shape, _mybir.dt.from_np(a.dtype), kind="ExternalInput").ap())
    for i, (shape, dtype) in enumerate(_OUTS):
        dt = _mybir.dt.from_np(_np.dtype(dtype))
        args.append(nc.dram_tensor(f"out_{i}_dram", shape, dt, kind="ExternalOutput").ap())
    flamingo_layer(nc, *args)
    r = _run(nc, [arrays], core_ids=[0])
    got = tuple(r.results[0][f"out_{i}_dram"] for i in range(len(_OUTS)))
    return got[0]
```

```python
from contextlib import ExitStack

import concourse.bass as bass
from concourse import mybir

P = 128
ALU = mybir.AluOpType
ACT = mybir.ActivationFunctionType
AX_X = mybir.AxisListType.X
F32 = mybir.dt.float32
BF16 = mybir.dt.bfloat16
I32 = mybir.dt.int32
U32 = mybir.dt.uint32
F32R = mybir.dt.float32r


def middle(t, low, high):
    return low <= t < high if isinstance(t, int) else True


def run_steps(eng, step, first, last):
    with eng.Fori(first // 2, last // 2) as i:
        for parity in range(2):
            step(i * 2 + parity, parity, i)


def flamingo_layer(nc, x, ctx, g_xattn, g_ffn, wq, bq, wk, bk, wv, bv, wo, bo, wg, w1, w2, w3, out):
    B, S, D = x.shape
    KEYS = ctx.shape[1]
    HD = 16
    HEADS = D // HD
    E, _, HID = w1.shape
    DK = D // P
    HK = HID // P
    T = B * S
    TT = T // P
    HEADS_HALF = P // HD
    FLAT = HEADS * KEYS
    PCH = -(-FLAT // P)
    VW = HD + 1
    BANK_HEADS = 6
    TOPK = 2
    SQ = 1.0 / float(HD) ** 0.5
    EPS = 1e-5
    META = 4
    ROW = D + META
    CAPACITY = T + P
    XS_ROWS = E * CAPACITY + P
    NT = T * TOPK // P + E - 1
    GROUPS = ((0, TT // 2), (TT // 2, TT))
    NG = len(GROUPS)
    NGT = max(b - a for a, b in GROUPS)
    READY = [-(-(b * P * TOPK - E * (P - 1)) // P) for _, b in GROUPS[:-1]] + [NT]
    COLS = max(b - a for a, b in zip([0] + READY, READY))
    LOOP_A = (6, 12)
    LOOP_E = ((NT - 1 - (NT - 1 - 10) // 2 * 2, NT - 1),)
    SCHEDULE = ([("A", t) for t in range(LOOP_A[0])] + [("loop A",) + LOOP_A] + [("A", t) for t in range(LOOP_A[1], TT + 2)]
                + [("E", 0), ("A", TT + 2), ("A", TT + 3), ("top", 1, 0), ("E", 1), ("top", 1, 1), ("weights", 1), ("E", 2), ("ranks", 1), ("slots", 1, 0), ("slots", 1, 1), ("E", 3),
                 ("E", 4), ("tables", 1, 0), ("E", 5), ("tables", 1, 1), ("E", 6), ("tables", 1, 2)]
                + [("E", j) for j in range(7, LOOP_E[0][0])] + [("loop E",) + r for r in LOOP_E]
                + [("E", NT - 1), ("E", NT)])
    SPLIT = (2, 2 + 2 * E)
    PIECE = 512
    PIECES = 3 * DK * HID // PIECE
    AHEAD = list(SCHEDULE)
    AHEAD.remove(("A", TT + 2))
    AHEAD.insert(AHEAD.index(("A", TT + 1)) + 1, ("A", TT + 2))
    BEHIND_MAX = {12: [("top", 0, 0)], 13: [("slots", 0, 0)], 15: [("tables", 0, 0)]}
    BEHIND_SUB = {12: [("top", 0, 1)], 13: [("slots", 0, 1), ("weights", 0)], 15: [("tables", 0, 1)], 16: [("tables", 0, 2)]}
    SCATTERS = {13: (0, 1), 14: (0, 2), 15: (0, 1), 16: (1, 2), 17: (1, 0)}
    RANK_EXPERT_STEP = 2
    RANK_STEP = 12
    assert HID == PIECE and PIECES == 6 and HK * D == 2 * PIECE
    assert B == 2 and S % P == 0 and DK == 2 and HEADS == 16 and TT % 2 == 0 and NT % 2 == 1
    head0 = [c * P // KEYS for c in range(PCH)]
    heads_in = [min(c * P + P - 1, FLAT - 1) // KEYS - head0[c] + 1 for c in range(PCH)]
    SPAN = max(heads_in)

    xs = nc.dram_tensor("sorted_rows", (XS_ROWS, ROW), F32).ap()
    acc = nc.dram_tensor("accumulator", (T + P, D), F32).ap()
    vflat_dram = nc.dram_tensor("values_by_head", (B, PCH * P, VW), F32).ap()

    with ExitStack() as stack:
        def sb(name, shape, dt=F32):
            return stack.enter_context(nc.sbuf_tensor(name, shape, dt))

        def sem(name):
            return stack.enter_context(nc.semaphore(name))

        bank = [stack.enter_context(nc.psum_tensor(f"bank{i}", [P, 512], F32)) for i in range(6)]
        score_banks = stack.enter_context(nc.psum_tensor("score_banks", [P, 2, 512], F32))

        ident = sb("ident", [P, P])
        ones_f = sb("ones_f", [P, P])
        before_b = sb("before_b", [P, P], BF16)
        ones_b = sb("ones_b", [P, P], BF16)
        kmask = sb("kmask", [P, HEADS_HALF])
        vmask = sb("vmask", [P, PCH, SPAN])
        expert_step_c = sb("expert_step_c", [P, NG, E])
        desc = sb("desc", [P, E])
        cap_base = sb("cap_base", [P, E])
        tile_no = sb("tile_no", [P, NT])
        tile_128 = sb("tile_128", [P, TT])
        scan_keep = sb("scan_keep", [P, E, NGT])

        wqo_sb = sb("wqo_sb", [P, 2, DK, D])
        wq_sb, wo_sb = wqo_sb[:, 0, :, :], wqo_sb[:, 1, :, :]
        wg_sb = sb("wg_sb", [P, DK, E])
        bq_sb = sb("bq_sb", [P, DK])
        bk_sb = sb("bk_sb", [P, DK])
        bo_sb = sb("bo_sb", [P, D])
        gates = sb("gates", [P, 2])
        unused = sb("unused", [P, 1])
        tg = sb("tg", [P, 2])
        wh_sb = sb("wh_sb", [P, E, PIECES, PIECE], F32R)
        low_words, kblock_words = PIECES * PIECE // 2, B * DK * HEADS_HALF * KEYS
        low_area = sb("low_area", [P, (E - 1) * low_words + kblock_words])
        wl_sb = low_area[:, 0:E * low_words].bitcast(BF16).rearrange("p (e c n) -> p e c n", e=E, c=PIECES)
        w_piece = sb("w_piece", [P, 3, PIECE])
        pad_rows = w_piece[:, 0, 0:ROW]
        xTh = sb("xTh", [P, DK, P], F32R)
        hTh = sb("hTh", [P, HK, P], F32R)
        setup_at = [(E - 1) * low_words]

        def setup_buffer(words, partitions=P):
            setup_at[0] -= words
            return low_area[0:partitions, setup_at[0]:setup_at[0] + words]

        ctx_sb = setup_buffer(B * D, KEYS).rearrange("p (b d) -> p b d", b=B)
        wk_sb, wv_sb = (setup_buffer(DK * D).rearrange("p (k n) -> p k n", k=DK) for _ in range(2))
        bv_sb = setup_buffer(D, KEYS)
        ctxT = setup_buffer(DK * B * KEYS).rearrange("p (k n) -> p k n", k=DK)
        kT = setup_buffer(DK * B * KEYS).rearrange("p (k n) -> p k n", k=DK)
        v_sb = setup_buffer(B * HEADS * VW, KEYS).rearrange("p (b h w) -> p b h w", b=B, h=HEADS)
        vflat = setup_buffer(B * PCH * VW).rearrange("p (b c w) -> p b c w", b=B, c=PCH)
        st1 = setup_buffer(6 * TT).rearrange("p (t s) -> p t s", t=TT)
        assert setup_at[0] >= 0
        kblock = low_area[:, (E - 1) * low_words:].rearrange("p (b m h k) -> p b m h k", b=B, m=DK, h=HEADS_HALF)
        vblock = sb("vblock", [P, B, PCH, SPAN, VW])

        rows = sb("rows", [P, TT, ROW])
        x_sb = x1 = rows[:, :, 0:D]
        mv1 = sb("mv1", [P, TT, 2])
        var1 = sb("var1", [P, TT])
        shift1 = sb("shift1", [P, TT])
        eps = sb("eps", [P, TT])
        minus_half = sb("minus_half", [P, TT])
        rstd1 = sb("rstd1", [P, TT])
        small_area = sb("small_area", [P, 5 * D])
        xn, o_sb = small_area[:, 0:D], small_area[:, D:2 * D]
        xnT, qT, oT = (small_area[:, a * D:(a + 1) * D].rearrange("p (k n) -> p k n", k=DK) for a in range(2, 5))
        negmax = sb("negmax", [P, 2, HEADS])
        probs = sb("probs", [P, PCH * P])
        shifted = probs[:, 0:FLAT]
        before = shifted[:, 0:P]
        desc_i, cap_base_i, tile_no_i, tile_128_i = (
            shifted[:, (2 + a) * P:(2 + a) * P + n].bitcast(I32) for a, n in enumerate((E, E, NT, TT)))
        probsT = sb("probsT", [P, PCH + DK, P])
        rden = sb("rden", [P, 2, HEADS])
        st2 = sb("st2", [P, 2, 6])
        mv2 = sb("mv2", [P, 2, 2])
        var2 = sb("var2", [P, 2])
        rstd2 = sb("rstd2", [P, TT])
        shift2 = sb("shift2", [P, TT])
        xg = sb("xg", [P, D])

        logits = sb("logits", [P, TT, E])
        best = [sb(f"best{c}", [P, NGT]) for c in range(TOPK)]
        key = [sb(f"key{c}", [P, NGT]) for c in range(TOPK)]
        onehot = [sb(f"onehot{c}", [P, NGT, E]) for c in range(TOPK)]
        scratch = sb("scratch", [P, NGT, E])
        logits2 = sb("logits2", [P, NGT, E])
        gap = sb("gap", [P, NGT])
        egap = sb("egap", [P, NGT])
        esum = sb("esum", [P, NGT])
        p1 = sb("p1", [P, NGT])
        p1g = sb("p1g", [P, NGT])
        sel = sb("sel", [P, NGT, E], BF16)
        ranks = sb("ranks", [P, 2, NGT, E])
        totals = sb("totals", [P, E, NGT])
        upto = sb("upto", [P, E, NGT])
        position = logits2
        counts = sb("counts", [P, NG, E])
        slot_f = [sb(f"slot_f{c}", [P, NGT]) for c in range(TOPK)]
        slot = [sb(f"slot{c}", [P, TT], I32) for c in range(TOPK)]
        blocks = sb("blocks", [P, NG, E])
        blocks_new = sb("blocks_new", [P, NG, E])
        blocks_upto = sb("blocks_upto", [P, NG, E])
        lead = sb("lead", [P, NG, E])
        lead_step = sb("lead_step", [P, NG, E])
        counts_i = sb("counts_i", [P, E], I32)
        NV = NG * E
        past_area = probsT[:, :, :].rearrange("p c n -> p (c n)")[:, 2 * D:]
        weighted_area = low_area[:, E * low_words:]
        assert max(E * TT, COLS * NV) <= (PCH + DK) * P - 2 * D
        tile_expert = sb("tile_expert", [P, NT])
        tile_expert_i = sb("tile_expert_i", [P, NT], I32)
        tile_used = sb("tile_used", [P, COLS])
        tile_row = sb("tile_row", [P, COLS])
        tile_row_i = sb("tile_row_i", [P, NT], I32)

        xTl = small_area[:, 0:D // 2].bitcast(BF16).rearrange("p (k n) -> p k n", k=DK)
        hTl = small_area[:, D:D + HID // 2].bitcast(BF16).rearrange("p (k n) -> p k n", k=HK)
        silu = wqo_sb[:, 0, :, :].rearrange("p k n -> p (k n)")
        h = probs[:, 2 * ROW:2 * ROW + HID]
        xt = probs[:, 0:2 * ROW].rearrange("p (a f) -> p a f", a=2)
        assert 2 * ROW + HID <= PCH * P
        y_sb = [probsT[:, c * DK:(c + 1) * DK, :].rearrange("p k n -> p (k n)") for c in range(2)]
        weight1 = sb("weight1", [P, 2])
        weight = sb("weight", [P, NT])
        ids = sb("ids", [P, NT], I32)

        ctx_loaded = sem("ctx_loaded")
        kv_weights_loaded = sem("kv_weights_loaded")
        bk_loaded = sem("bk_loaded")
        bv_loaded = sem("bv_loaded")
        bq_loaded = sem("bq_loaded")
        bo_loaded = sem("bo_loaded")
        gates_loaded = sem("gates_loaded")
        x_first_loaded = sem("x_first_loaded")
        x_loaded = [sem(f"x_loaded{b}") for b in range(B)]
        wq_loaded = sem("wq_loaded")
        wo_loaded = sem("wo_loaded")
        pool_step = sem("pool_step")
        tanh_ready = sem("tanh_ready")
        ctxT_in_psum = sem("ctxT_in_psum")
        ctxT_ready = sem("ctxT_ready")
        kT_in_psum = sem("kT_in_psum")
        kT_ready = sem("kT_ready")
        v_in_psum = sem("v_in_psum")
        v_ready = sem("v_ready")
        v_stored = sem("v_stored")
        vflat_cleared = sem("vflat_cleared")
        vflat_loaded = sem("vflat_loaded")
        blocks_ready = sem("blocks_ready")
        dve_step = sem("dve_step")
        residual_ready = sem("residual_ready")
        xn_ready = sem("xn_ready")
        xnT_in_psum = sem("xnT_in_psum")
        xnT_ready = sem("xnT_ready")
        q_in_psum = sem("q_in_psum")
        q_ready = sem("q_ready")
        scores_in_psum = sem("scores_in_psum")
        max_ready = sem("max_ready")
        shifted_ready = sem("shifted_ready")
        probs_ready = sem("probs_ready")
        probsT_in_psum = sem("probsT_in_psum")
        probsT_ready = sem("probsT_ready")
        pv_in_psum = sem("pv_in_psum")
        rden_ready = sem("rden_ready")
        o_ready = sem("o_ready")
        oT_in_psum = sem("oT_in_psum")
        oT_ready = sem("oT_ready")
        attn_in_psum = sem("attn_in_psum")
        x1_ready = sem("x1_ready")
        st2_ready = sem("st2_ready")
        w_high_loaded = sem("w_high_loaded")
        w_piece_loaded = [sem(f"w_piece_loaded{k}") for k in range(3)]
        w_low_ready = [sem(f"w_low_ready{k}") for k in range(3)]
        pad_ready = sem("pad_ready")
        stats_ready = sem("stats_ready")
        acc_written = sem("acc_written")
        xg_ready = sem("xg_ready")
        logits_in_psum = sem("logits_in_psum")
        rstd2_ready = sem("rstd2_ready")
        rows_kept = sem("rows_kept")
        pv_bank_read = sem("pv_bank_read")
        stats1_ready = sem("stats1_ready")
        xn_scale_ready = sem("xn_scale_ready")
        gap_ready = sem("gap_ready")
        egap_ready = sem("egap_ready")
        sel_ready = sem("sel_ready")
        ranks_in_psum = sem("ranks_in_psum")
        slots_ready = sem("slots_ready")
        counts_ready = sem("counts_ready")
        tables_ready = sem("tables_ready")
        rows_scattered = [sem(f"rows_scattered{g}") for g in range(NG)]
        padding_written = sem("padding_written")
        tile_loaded = [sem(f"tile_loaded{c}") for c in range(2)]
        xT_in_psum = sem("xT_in_psum")
        xTh_ready = sem("xTh_ready")
        xTl_ready = sem("xTl_ready")
        u_in_psum = sem("u_in_psum")
        v2_in_psum = sem("v2_in_psum")
        silu_ready = sem("silu_ready")
        weight1_ready = sem("weight1_ready")
        meta_ready = sem("meta_ready")
        h_ready = sem("h_ready")
        hT_in_psum = sem("hT_in_psum")
        hTh_ready = sem("hTh_ready")
        hTl_ready = sem("hTl_ready")
        y_in_psum = sem("y_in_psum")
        y_ready = sem("y_ready")
        y_added = sem("y_added")
        out_written = sem("out_written")

        bank_x, bank_o, bank_pv = bank[0], bank[1], bank[2]
        bank_p = [bank[3], bank[4]]
        scores_last = bank[5]
        logits_psum = bank_pv[:, HEADS * VW:HEADS * VW + E]
        ranks_psum = bank_pv[:, 512 - 2 * NGT * E:512].rearrange("p (a t e) -> p a t e", a=2, e=E)
        assert HEADS * VW + E <= 512 - 2 * NGT * E
        q_psum = bank_x[:, D:2 * D].rearrange("p (k n) -> p k n", k=DK)
        pv_psum = bank_pv[:, 0:HEADS * VW].rearrange("p (h w) -> p h w", h=HEADS)

        N_POOL_SETUP = [0]

        u_psum, v_psum = score_banks[:, 0, :], score_banks[:, 1, :]
        xT_psum, hT_psum, y_psum = scores_last[:, 0:D], bank_x[:, :], bank_o[:, 0:D]

        def bcast(ap, axis, n):
            shape = list(ap.shape)
            shape.insert(axis, n)
            return ap.unsqueeze(axis).to_broadcast(shape)

        def token_view(dram, b):
            return dram[b * S:(b + 1) * S, :].rearrange("(m p) d -> p m d", p=P)

        def tiles_of(tensor, b):
            return tensor[:, :, :].rearrange("p (m b) d -> p m b d", b=B)[:, :, b, :]

        def upper(ap):
            return ap.bitcast(BF16).rearrange("p (n two) -> p n two", two=2)[:, :, 1]

        def chunk_groups(t, g):
            if isinstance(t, int) and t > TT:
                return 3 * TT + t - TT
            return (t - 1) * 3 + g + 1

        block = stack.enter_context(nc.Block())

        @block.gpsimd
        def _(pool):
            def done(ins):
                N_POOL_SETUP[0] += 1
                ins.then_inc(pool_step, 1)
                pool.wait_ge(pool_step, N_POOL_SETUP[0])

            done(pool.memset(ones_f[:, :], 1.0))
            done(pool.affine_select(out=ident[:, :], in_=ones_f[:, :], compare_op=ALU.is_equal, fill=0.0,
                                    base=0, pattern=[[-1, P]], channel_multiplier=1))
            done(pool.affine_select(out=kmask[:, :], in_=ones_f[:, 0:HEADS_HALF], compare_op=ALU.is_ge, fill=0.0,
                                    base=0, pattern=[[-HD, HEADS_HALF]], channel_multiplier=1))
            done(pool.affine_select(out=kmask[:, :], in_=kmask[:, :], compare_op=ALU.is_ge, fill=0.0,
                                    base=HD - 1, pattern=[[HD, HEADS_HALF]], channel_multiplier=-1))
            for c in range(PCH):
                pool.affine_select(out=vmask[:, c, :], in_=ones_f[:, 0:SPAN], compare_op=ALU.is_ge, fill=0.0,
                                   base=c * P - KEYS * head0[c], pattern=[[-KEYS, SPAN]],
                                   channel_multiplier=1).then_inc(pool_step, 1)
            N_POOL_SETUP[0] += PCH
            pool.wait_ge(pool_step, N_POOL_SETUP[0])
            for c in range(PCH):
                pool.affine_select(out=vmask[:, c, :], in_=vmask[:, c, :], compare_op=ALU.is_ge, fill=0.0,
                                   base=KEYS * head0[c] + KEYS - 1 - c * P, pattern=[[KEYS, SPAN]],
                                   channel_multiplier=-1).then_inc(pool_step, 1)
            N_POOL_SETUP[0] += PCH
            pool.memset(probs[:, FLAT:PCH * P], 0.0).then_inc(pool_step, 1)
            pool.memset(scan_keep[:, :, :], 1.0).then_inc(pool_step, 1)
            pool.memset(expert_step_c[:, :, :], 1.0).then_inc(pool_step, 1)
            pool.memset(eps[:, :], EPS).then_inc(pool_step, 1)
            pool.memset(minus_half[:, :], -0.5).then_inc(pool_step, 1)
            pool.affine_select(out=before, in_=ones_f[:, :], compare_op=ALU.is_gt, fill=0.0,
                               base=0, pattern=[[1, P]], channel_multiplier=-1).then_inc(pool_step, 1)
            pool.iota(desc_i, pattern=[[-1, E]], base=E, channel_multiplier=0).then_inc(pool_step, 1)
            pool.iota(cap_base_i, pattern=[[CAPACITY, E]], base=0, channel_multiplier=0).then_inc(pool_step, 1)
            pool.iota(tile_no_i, pattern=[[1, NT]], base=0, channel_multiplier=0).then_inc(pool_step, 1)
            pool.iota(tile_128_i, pattern=[[P, TT]], base=0, channel_multiplier=0).then_inc(pool_step, 1)
            pool.iota(rows[:, :, D:D + 1].bitcast(I32), pattern=[[P, TT // B], [S, B], [0, 1]], base=0,
                      channel_multiplier=1).then_inc(pool_step, 1)
            N_POOL_SETUP[0] += 11
            pool.wait_ge(pool_step, N_POOL_SETUP[0])
            pool.memset(scan_keep[:, :, 0:1], 0.0).then_inc(pool_step, 1)
            pool.tensor_copy(before_b[:, :], before).then_inc(pool_step, 1)
            pool.tensor_copy(ones_b[:, :], ones_f[:, :]).then_inc(pool_step, 1)
            pool.tensor_copy(desc[:, :], desc_i).then_inc(pool_step, 1)
            pool.tensor_copy(cap_base[:, :], cap_base_i).then_inc(pool_step, 1)
            pool.tensor_copy(tile_no[:, :], tile_no_i).then_inc(pool_step, 1)
            pool.tensor_copy(tile_128[:, :], tile_128_i).then_inc(pool_step, 1)
            pool.memset(expert_step_c[:, :, E - 1:E], -float(E - 1)).then_inc(pool_step, 1)
            N_POOL_SETUP[0] += 8
            scale_steps = [0]

            def scale_x(t0, t1, step=1):
                tiles = slice(t0, t1, step)
                var, std, shift = var1[:, tiles], rstd1[:, tiles], shift1[:, tiles]

                def scaled(ins):
                    scale_steps[0] += 1
                    ins.then_inc(xn_scale_ready, 1)
                    pool.wait_ge(xn_scale_ready, scale_steps[0])

                scaled(pool.tensor_tensor(var.unsqueeze(2), mv1[:, tiles, 1:2], eps[:, tiles].unsqueeze(2), ALU.add))
                scaled(pool.tensor_tensor(std, var, minus_half[:, tiles], ALU.pow))
                scaled(pool.tensor_tensor(shift.unsqueeze(2), mv1[:, tiles, 0:1], std.unsqueeze(2), ALU.mult))
                scaled(pool.tensor_scalar(shift, shift, -1.0, 0.0, ALU.mult, ALU.add))

            def normalise_x(t):
                if t >= 1:
                    pool.wait_ge(xnT_in_psum, t)
                pool.tensor_scalar(xn, x_sb[:, t, :], rstd1[:, t:t + 1], shift1[:, t:t + 1],
                                   ALU.mult, ALU.add).then_inc(xn_ready, 1)

            def residual(t):
                pool.tensor_tensor(x1[:, t, :], x_sb[:, t, :], bo_sb[:, :], ALU.add).then_inc(residual_ready, 1)

            def normalise_x1(t):
                p = t % 2
                pool.wait_ge(stats_ready, t + 1)
                pool.tensor_tensor(var2[:, p:p + 1], mv2[:, p, 1:2], eps[:, 0:1], ALU.add).then_inc(rstd2_ready, 1)
                pool.wait_ge(rstd2_ready, 3 * t + 1)
                pool.tensor_tensor(rstd2[:, t:t + 1], var2[:, p:p + 1], minus_half[:, 0:1], ALU.pow).then_inc(rstd2_ready, 1)
                pool.wait_ge(rstd2_ready, 3 * t + 2)
                pool.tensor_scalar(shift2[:, t:t + 1], mv2[:, p, 0:1], rstd2[:, t:t + 1], -1.0, ALU.mult, ALU.mult).then_inc(rstd2_ready, 1)
                pool.wait_ge(rstd2_ready, 3 * t + 3)
                if t >= 1:
                    pool.wait_ge(probsT_in_psum, chunk_groups(t + 2, 2))
                pool.tensor_scalar(xg[:, :], x1[:, t, :], rstd2[:, t:t + 1], shift2[:, t:t + 1],
                                   ALU.mult, ALU.add).then_inc(xg_ready, 1)

            def keep_rows(t):
                pool.wait_ge(acc_written, 16 * (t + 1))
                pool.tensor_scalar(rows[:, t, 0:D], x1[:, t, :], rstd2[:, t:t + 1], shift2[:, t:t + 1],
                                   ALU.mult, ALU.add).then_inc(rows_kept, 1)

            def scatter(t):
                for c in range(TOPK):
                    pool.indirect_dma_start(
                        out=xs, out_offset=bass.IndirectOffsetOnAxis(ap=slot[c][:, t:t + 1].bitcast(U32), axis=0),
                        in_=rows[:, t, :], in_offset=None).then_inc(rows_scattered[0 if t < GROUPS[0][1] else 1], 16)

            def add_rows(j):
                pool.wait_ge(y_ready, j + 1)
                if j >= 1:
                    pool.wait_ge(y_added, j * 16)
                pool.indirect_dma_start(
                    out=acc, out_offset=bass.IndirectOffsetOnAxis(ap=ids[:, j:j + 1].bitcast(U32), axis=0),
                    in_=y_sb[j % 2], in_offset=None, compute_op=ALU.add).then_inc(y_added, 16)

            def load_high(e):
                if e >= 1:
                    pool.wait_ge(w_high_loaded, 16 * 3 * e)
                for w, at in ((w1[e], 0), (w2[e], 2), (w3[e], 4)):
                    pool.dma_start(wh_sb[:, e, at:at + 2, :].rearrange("p c n -> p (c n)").rearrange(
                        "p (k n) -> p k n", n=w.shape[1]), w.rearrange("(k p) n -> p k n", p=P)).then_inc(w_high_loaded, 16)

            def split_low(t):
                e, at = (t - SPLIT[0]) // 2, t % 2 * 3 + 2
                pool.wait_ge(w_high_loaded, 16 * 3 * (e + 1))
                pool.wait_ge(w_piece_loaded[2], (t - SPLIT[0] + 1) * 16)
                pool.tensor_tensor(wl_sb[:, e, at, :], w_piece[:, 2, :], wh_sb[:, e, at, :].bitcast(F32),
                                   ALU.subtract).then_inc(w_low_ready[2], 1)

            pool.wait_ge(stats1_ready, 1)
            scale_x(0, B)
            normalise_x(0)
            load_high(0)
            normalise_x(1)
            pool.wait_ge(stats1_ready, 2)
            scale_x(B, TT, B)
            pool.wait_ge(bo_loaded, 16)
            pool.wait_ge(tanh_ready, 1)
            pool.tensor_scalar(bo_sb[:, :], bo_sb[:, :], tg[:, 0:1], 0.0, ALU.mult, ALU.add).then_inc(residual_ready, 1)
            pool.wait_ge(residual_ready, 1)
            residual(0)
            to_scatter = []

            def route_rows(g):
                pool.wait_ge(slots_ready, 2 * g + 2)
                pool.wait_ge(rows_kept, GROUPS[g][1])
                to_scatter.extend(range(*GROUPS[g]))

            def scatter_some(n):
                for u in to_scatter[:n]:
                    scatter(u)
                del to_scatter[:n]

            for what, *at in AHEAD:
                if what == "loop A":
                    steps = range(*at)
                elif what in ("A", "E"):
                    steps = at[:1]
                elif what == "loop E":
                    steps = range(*at)
                else:
                    steps = ()
                for t in steps:
                    if what in ("A", "loop A"):
                        if t == 1:
                            pool.wait_ge(stats1_ready, 3)
                            scale_x(B + 1, TT, B)
                        scatter_some(SCATTERS.get(t, (0, 0))[0])
                        if t == SPLIT[1]:
                            pool.wait_ge(w_low_ready[0], SPLIT[1] - SPLIT[0])
                            pool.memset(pad_rows, 0.0).then_inc(pad_ready, 1)
                            pool.wait_ge(pad_ready, 1)
                            pool.iota(pad_rows[:, D:D + 1].bitcast(I32), pattern=[[0, 1]], base=T,
                                      channel_multiplier=1).then_inc(pad_ready, 1)
                        if 3 <= t < TT + 3:
                            normalise_x1(t - 3)
                        if t + 1 < TT:
                            residual(t + 1)
                        late = range(15, 18)
                        if 4 <= t < TT + 4 and t not in late:
                            keep_rows(t - 4)
                        if t == TT + 3:
                            for u in late:
                                keep_rows(u - 4)
                        if t + 2 < TT:
                            normalise_x(t + 2)
                        if SPLIT[0] <= t < TT:
                            split_low(t)
                        if t % 2 == 1 and (t + 1) // 2 < E:
                            load_high((t + 1) // 2)
                    if what == "A" and t == min(SCATTERS):
                        route_rows(0)
                    scatter_some(SCATTERS.get(t, (0, 0))[1] if what == "A" else 2)
                    if what in ("E", "loop E") and t >= 1:
                        if t == 1:
                            pool.wait_ge(acc_written, 16 * (TT + 1))
                        add_rows(t - 1)
                if (what, *at) == ("slots", 1, 1):
                    route_rows(1)
            assert not to_scatter

        @block.sync
        def _(sp):
            sp.dma_start(ctx_sb[:, :, :], ctx.rearrange("b k d -> k b d")).then_inc(ctx_loaded, 16)
            for w, dst in ((wk, wk_sb), (wv, wv_sb)):
                sp.dma_start(dst[:, :, :], w.rearrange("(k p) n -> p k n", p=P)).then_inc(kv_weights_loaded, 16)
            x_rows = x.rearrange("b s d -> (b s) d")
            for b in range(B):
                sp.dma_start(tiles_of(x_sb, b)[:, 0:1, :], token_view(x_rows, b)[:, 0:1, :]).then_inc(x_first_loaded, 16)
            sp.dma_start(wq_sb, wq.rearrange("(k p) n -> p k n", p=P)).then_inc(wq_loaded, 16)
            sp.dma_start(bq_sb[:, :], bq.rearrange("(k p) -> p k", p=P), allow_slow_non_contiguous=True).then_inc(bq_loaded, 16)
            sp.dma_start(bo_sb[:, :], bo.partition_broadcast(P)).then_inc(bo_loaded, 16)
            sp.dma_start(gates[:, 0:1], g_xattn.partition_broadcast(P)).then_inc(gates_loaded, 16)
            sp.dma_start(gates[:, 1:2], g_ffn.partition_broadcast(P)).then_inc(gates_loaded, 16)
            for b in range(B):
                sp.dma_start(tiles_of(x_sb, b)[:, 1:, :], token_view(x_rows, b)[:, 1:, :]).then_inc(x_loaded[b], 16)
            for w, dst in ((wo, wo_sb), (wg, wg_sb[:, :, :])):
                sp.dma_start(dst, w.rearrange("(k p) n -> p k n", p=P)).then_inc(wo_loaded, 16)
            sp.wait_ge(v_ready, B + 1)
            for b in range(B):
                sp.dma_start(vflat_dram[b, 0:FLAT, :].rearrange("(h k) w -> k h w", h=HEADS),
                             v_sb[:, b, :, :]).then_inc(v_stored, 16)
            sp.wait_ge(v_stored, 16 * B)
            sp.wait_ge(vflat_cleared, 1)
            full = FLAT // P
            for b in range(B):
                sp.dma_start(vflat[:, b, 0:full, :],
                             vflat_dram[b, 0:full * P, :].rearrange("(c p) w -> p c w", p=P)).then_inc(vflat_loaded, 16)
                sp.dma_start(vflat[0:FLAT - full * P, b, full, :],
                             vflat_dram[b, full * P:FLAT, :]).then_inc(vflat_loaded, 16)
            def store_x1(t):
                sp.wait_ge(x1_ready, t + 1)
                if t >= 1:
                    sp.wait_ge(acc_written, 16 * t)
                row = t % B * S + t // B * P
                sp.dma_start(acc[row:row + P, :], x1[:, t, :]).then_inc(acc_written, 16)

            for step in range(*SPLIT):
                if step >= 3:
                    store_x1(step - 3)
                e, half = (step - SPLIT[0]) // 2, step % 2
                for k in range(3):
                    n = (step - SPLIT[0]) * 3 + k
                    if n >= 3:
                        sp.wait_ge(w_low_ready[k], n // 3)
                    w, c = (w1, w2, w3)[(half * 3 + k) // 2], (half * 3 + k) % 2
                    rows_of = w.shape[1] // 2
                    sp.dma_start(w_piece[:, k, :].rearrange("p (k n) -> p k n", n=w.shape[2]),
                                 w[e, c * rows_of:(c + 1) * rows_of, :].rearrange("(k p) n -> p k n", p=P)
                                 ).then_inc(w_piece_loaded[k], 16)

            def load(j, parity, pair=None):
                if not isinstance(j, int) or j >= 2:
                    sp.wait_ge(xT_in_psum, j - 1)
                    sp.wait_ge(meta_ready, j - 1)
                row = sp.value_load(tile_row_i[0:1, bass.ds(j, 1)], min_val=0, max_val=XS_ROWS - P)
                sp.dma_start(xt[:, parity, :], xs[bass.ds(row, P), :]).then_inc(tile_loaded[parity], 16)

            sp.wait_ge(tables_ready, 1)
            sp.wait_ge(rows_scattered[0], 16 * TOPK * (GROUPS[0][1] - GROUPS[0][0]))
            sp.wait_ge(probsT_in_psum, 3 * TT)
            for j in range(2):
                load(j, j)
            store_x1(TT - 1)
            sp.wait_ge(pad_ready, 2)
            sp.wait_ge(acc_written, 16 * TT)
            sp.dma_start(acc[T:T + P, :], pad_rows[:, 0:D]).then_inc(acc_written, 16)
            sp.dma_start(xs[E * CAPACITY:XS_ROWS, :], pad_rows).then_inc(padding_written, 16)
            for j in range(2, READY[0]):
                load(j, j % 2)
                if j == READY[0] - 3:
                    sp.wait_ge(counts_ready, 1)
                if j >= READY[0] - 3:
                    for e in range((j - READY[0] + 3) * 3, min((j - READY[0] + 4) * 3, E)):
                        n = sp.value_load(counts_i[0:1, e:e + 1], min_val=0, max_val=T)
                        sp.dma_start(xs[bass.ds(n + e * CAPACITY, P), :], pad_rows).then_inc(padding_written, 16)
            sp.wait_ge(tables_ready, 2)
            sp.wait_ge(padding_written, 16 * (E + 1))
            sp.wait_ge(rows_scattered[1], 16 * TOPK * (GROUPS[1][1] - GROUPS[1][0]))
            first = READY[0] + READY[0] % 2
            for j in range(READY[0], first):
                load(j, j % 2)
            run_steps(sp, load, first, NT - 1)
            load(NT - 1, (NT - 1) % 2)
            sp.wait_ge(y_added, 16 * NT)
            sp.dma_start(out.rearrange("b s d -> (b s) d"), acc[0:T, :]).then_inc(out_written, 16)
            sp.wait_ge(out_written, 16)

        @block.scalar
        def _(act):
            act.dma_start(bk_sb[:, :], bk.rearrange("(k p) -> p k", p=P), allow_slow_non_contiguous=True).then_inc(bk_loaded, 16)
            act.dma_start(bv_sb, bv.partition_broadcast(KEYS)).then_inc(bv_loaded, 16)
            act.wait_ge(pool_step, 1)
            act.activation(unused[:, :], ones_f[:, 0:1], ACT.Exp)
            act.wait_ge(ctxT_in_psum, 1)
            act.copy(ctxT[:, :, :], bank[0][:, 0:DK * B * KEYS].rearrange("p (k n) -> p k n", k=DK)).then_inc(ctxT_ready, 1)

            def evacuate_xnT(t, parity):
                act.wait_ge(xnT_in_psum, t + 1)
                act.copy(xnT.rearrange("p k n -> p (k n)"), bank_x[:, 0:D]).then_inc(xnT_ready, 1)

            def bias_q(t):
                act.wait_ge(q_in_psum, t + 1)
                for k in range(DK):
                    ins = act.activation(qT[:, k, :], q_psum[:, k, :], ACT.Identity, bias=bq_sb[:, k:k + 1])
                ins.then_inc(q_ready, 1)

            def attention_step(t, parity, pair):
                other = 1 - parity
                for g in range(3):
                    if g == 1 and middle(t, 2, TT + 2):
                        act.wait_ge(oT_in_psum, t - 1)
                        act.copy(oT.rearrange("p k n -> p (k n)"), bank_o[:, 0:D]).then_inc(oT_ready, 1)
                    if g == 1 and middle(t, 0, TT - 1):
                        evacuate_xnT(t + 1, other)
                    of_probs = middle(t, 1, TT + 1)
                    if of_probs or (g == 2 and middle(t, 3, TT + 3)):
                        rows_too = g == 2 and middle(t, 3, TT + 3)
                        c0, c1 = 4 * g if of_probs else PCH, 4 * g + 4 if g < 2 or rows_too else PCH
                        act.wait_ge(probsT_in_psum, chunk_groups(t, g))
                        act.copy(probsT[:, c0:c1, :].rearrange("p k n -> p (k n)"),
                                 bank_p[(3 * other + g) % 2][:, (c0 - 4 * g) * P:(c1 - 4 * g) * P]).then_inc(probsT_ready, 1)
                if middle(t, 0, TT - 1):
                    bias_q(t + 1)
                if middle(t, 0, TT):
                    act.wait_ge(shifted_ready, t + 1)
                    act.activation(shifted, shifted, ACT.Exp, scale=SQ).then_inc(probs_ready, 1)

            evacuate_xnT(0, 0)
            act.wait_ge(bq_loaded, 16)
            bias_q(0)
            act.wait_ge(gates_loaded, 32)
            act.activation(tg[:, :], gates[:, :], ACT.Tanh).then_inc(tanh_ready, 1)
            def evacuate_xT(j, parity):
                act.wait_ge(xT_in_psum, j + 1)
                act.copy(xTh.rearrange("p k n -> p (k n)"), xT_psum).then_inc(xTh_ready, 1)

            def expert_step(j, parity, pair):
                other = 1 - parity
                if middle(j, 0, NT):
                    act.wait_ge(u_in_psum, j + 1)
                    if not isinstance(j, int) or j >= 1:
                        act.wait_ge(h_ready, j)
                    act.activation(silu, u_psum, ACT.Silu).then_inc(silu_ready, 1)
                if middle(j, 1, NT + 1):
                    act.wait_ge(hT_in_psum, j)
                    act.copy(hTh.rearrange("p k n -> p (k n)"), hT_psum).then_inc(hTh_ready, 1)
                if middle(j, 0, NT - 1):
                    evacuate_xT(j + 1, other)
                if middle(j, 1, NT + 1):
                    act.wait_ge(meta_ready, j)
                    act.wait_ge(y_in_psum, j)
                    if not isinstance(j, int) or j >= 3:
                        act.wait_ge(y_added, (j - 2) * 16)
                    act.activation(y_sb[other], y_psum, ACT.Copy, scale=weight[:, bass.ds(j - 1, 1)]).then_inc(y_ready, 1)

            def softmax_exp(g):
                act.wait_ge(gap_ready, g + 1)
                n = GROUPS[g][1] - GROUPS[g][0]
                act.activation(egap[:, 0:n], gap[:, 0:n], ACT.Exp).then_inc(egap_ready, 1)

            for what, *at in SCHEDULE:
                if what == "A":
                    attention_step(at[0], at[0] % 2, at[0] // 2)
                    if ("top", 0, TOPK - 1) in BEHIND_SUB.get(at[0], []):
                        softmax_exp(0)
                elif what == "loop A":
                    run_steps(act, attention_step, *at)
                elif what == "E":
                    if at[0] == 0:
                        act.activation(unused[:, :], ones_f[:, 0:1], ACT.Silu)
                        evacuate_xT(0, 0)
                    expert_step(at[0], at[0] % 2, at[0] // 2)
                elif what == "loop E":
                    run_steps(act, expert_step, *at)
                elif what == "top" and at[1] == TOPK - 1:
                    softmax_exp(at[0])

        @block.tensor
        def _(pe):
            pe.wait_ge(pool_step, 2)
            pe.wait_ge(ctx_loaded, 16)
            for b in range(B):
                for k in range(DK):
                    at = (k * B + b) * KEYS
                    ins = pe.transpose(bank[0][:, at:at + KEYS], ctx_sb[:, b, k * P:(k + 1) * P], ident[0:KEYS, 0:KEYS])
            ins.then_inc(ctxT_in_psum, 1)
            pe.wait_ge(ctxT_ready, 1)
            pe.wait_ge(kv_weights_loaded, 32)
            for m in range(DK):
                for k in range(DK):
                    ins = pe.matmul(bank[1][:, m * B * KEYS:(m + 1) * B * KEYS], wk_sb[:, k, m * P:(m + 1) * P],
                                    ctxT[:, k, :], start=k == 0, stop=k == DK - 1)
            ins.then_inc(kT_in_psum, 1)
            for b in range(B):
                for k in range(DK):
                    ins = pe.matmul(bank[2][0:KEYS, b * D:(b + 1) * D], ctxT[:, k, b * KEYS:(b + 1) * KEYS],
                                    wv_sb[:, k, :], start=k == 0, stop=k == DK - 1)
            ins.then_inc(v_in_psum, 1)

            def transpose_xn(t, parity):
                pe.wait_ge(xn_ready, t + 1)
                for k in range(DK):
                    ins = pe.transpose(bank_x[:, k * P:(k + 1) * P], xn[:, k * P:(k + 1) * P], ident[:, :])
                ins.then_inc(xnT_in_psum, 1)

            def project_q(t, parity):
                pe.wait_ge(xnT_ready, t + 1)
                for m in range(DK):
                    for k in range(DK):
                        ins = pe.matmul(q_psum[:, m, :], wq_sb[:, k, m * P:(m + 1) * P], xnT[:, k, :],
                                        start=k == 0, stop=k == DK - 1)
                ins.then_inc(q_in_psum, 1)

            def rank_products(g):
                n = GROUPS[g][1] - GROUPS[g][0]
                pe.wait_ge(sel_ready, g + 1)
                for a, w in ((0, before_b), (1, ones_b)):
                    ins = pe.matmul(ranks_psum[:, a, 0:n, :], w[:, :], sel[:, 0:n, :].rearrange("p t e -> p (t e)"),
                                    start=True, stop=True)
                ins.then_inc(ranks_in_psum, 1)

            def attention_step(t, parity, pair):
                other = 1 - parity
                if middle(t, 0, TT):
                    pe.wait_ge(q_ready, t + 1)
                    if middle(t, 1, TT):
                        pe.wait_ge(shifted_ready, t)
                    for m, h0, h1 in ((0, 0, 6), (0, 6, 8), (1, 8, 12), (1, 12, 16)):
                        target = scores_last if h0 // BANK_HEADS == 2 else score_banks[:, h0 // BANK_HEADS, :]
                        at = h0 % BANK_HEADS * KEYS
                        half0 = m * HEADS_HALF
                        ins = pe.matmul(target[:, at:at + (h1 - h0) * KEYS], qT[:, m, :],
                                        kblock[:, parity, m, h0 - half0:h1 - half0, :].rearrange("p h k -> p (h k)"),
                                        start=True, stop=True)
                    ins.then_inc(scores_in_psum, 1)
                transpose_group(t, other, 0)
                if middle(t, 2, TT + 2):
                    pe.wait_ge(o_ready, t - 1)
                    if middle(t, 3, TT + 2) and not (isinstance(t, int) and t < 3):
                        pe.wait_ge(x1_ready, t - 2)
                    for k in range(DK):
                        ins = pe.transpose(bank_o[:, k * P:(k + 1) * P], o_sb[:, k * P:(k + 1) * P], ident[:, :])
                    ins.then_inc(oT_in_psum, 1)
                if middle(t, 0, TT - 1):
                    transpose_xn(t + 1, other)
                transpose_group(t, other, 1)
                values(t, other, 0, 4)
                if isinstance(t, int) and t == TT + 1:
                    project_out(t)
                transpose_group(t, other, 2)
                if middle(t, 0, TT - 1):
                    project_q(t + 1, other)
                values(t, other, 4, 8)
                if middle(t, 2, TT + 1):
                    project_out(t)
                values(t, other, 8, PCH)
                if isinstance(t, int) and t == RANK_STEP:
                    rank_products(0)
                if middle(t, 3, TT + 3):
                    pe.wait_ge(probsT_ready, chunk_groups(t, 2))
                    if not middle(t, 1, TT + 1):
                        pe.wait_ge(pv_bank_read, t - 1)
                    for k in range(DK):
                        ins = pe.matmul(logits_psum, probsT[:, PCH + k, :], wg_sb[:, k, :],
                                        start=k == 0, stop=k == DK - 1)
                    ins.then_inc(pv_in_psum, 1)

            def project_out(t):
                pe.wait_ge(oT_ready, t - 1)
                for k in range(DK):
                    ins = pe.matmul(bank_o[:, D:2 * D], oT[:, k, :], wo_sb[:, k, :], start=k == 0, stop=k == DK - 1)
                ins.then_inc(attn_in_psum, 1)

            def transpose_group(t, other, g):
                of_probs = middle(t, 1, TT + 1)
                of_rows = g == 2 and middle(t, 3, TT + 3)
                if not (of_probs or of_rows):
                    return
                if of_probs and g == 0:
                    pe.wait_ge(probs_ready, t)
                if middle(t, 2, TT + 3) or g == 2:
                    pe.wait_ge(probsT_ready, chunk_groups(t, g) - 2)
                target = bank_p[(3 * other + g) % 2]
                for c in range(4 * g, min(4 * g + 4, PCH)):
                    if of_probs:
                        ins = pe.transpose(target[:, (c % 4) * P:(c % 4 + 1) * P],
                                           probs[:, c * P:(c + 1) * P], ident[:, :])
                if of_rows:
                    pe.wait_ge(xg_ready, t - 2)
                    for k in range(DK):
                        at = (PCH + k) % 4 * P
                        ins = pe.transpose(target[:, at:at + P], xg[:, k * P:(k + 1) * P], ident[:, :])
                ins.then_inc(probsT_in_psum, 1)

            def values(t, other, c0, c1):
                if not middle(t, 1, TT + 1):
                    return
                if isinstance(t, int) and (t, c0) == (1, 0):
                    pe.wait_ge(blocks_ready, 3 * B)
                if c0 == 0 and middle(t, 2, TT + 1):
                    pe.wait_ge(pv_bank_read, t - 1)
                pe.wait_ge(probsT_ready, chunk_groups(t, (c1 - 1) // 4))
                for c in range(c0, c1):
                    ins = pe.matmul(bank_pv[:, head0[c] * VW:(head0[c] + heads_in[c]) * VW], probsT[:, c, :],
                                    vblock[:, other, c, 0:heads_in[c], :].rearrange("p s w -> p (s w)"),
                                    start=c == 0, stop=c == PCH - 1, skip_group_check=True)
                if c1 == PCH and not middle(t, 3, TT + 3):
                    ins.then_inc(pv_in_psum, 1)

            transpose_xn(0, 0)
            pe.wait_ge(wq_loaded, 16)
            project_q(0, 0)
            pe.wait_ge(wo_loaded, 32)
            pe.wait_ge(blocks_ready, 2 * B)
            def transpose_x(j, parity):
                pe.wait_ge(tile_loaded[parity], (j // 2) * 16 + 16)
                for k in range(DK):
                    ins = pe.transpose(xT_psum[:, k * P:(k + 1) * P], xt[:, parity, k * P:(k + 1) * P], ident[:, :])
                ins.then_inc(xT_in_psum, 1)

            wh_upper = wh_sb[:, :, :, :].bitcast(BF16).rearrange("p e c (n two) -> p e c n two", two=2)

            def products(psum, high, low, e, piece0, finished, low_ready=None, count=None):
                chunks = high.shape[1]
                width = psum.shape[1]
                at = [(piece0 + k * width // PIECE, k * width % PIECE) for k in range(chunks)]
                for k, (c, n) in enumerate(at):
                    pe.matmul(psum, high[:, k, :], wh_sb[:, bass.ds(e, 1), c, n:n + width], start=k == 0, stop=False)
                for k, (c, n) in enumerate(at):
                    pe.matmul(psum, upper(high[:, k, :]), wl_sb[:, bass.ds(e, 1), c, n:n + width], start=False, stop=False)
                if low_ready is not None:
                    pe.wait_ge(low_ready, count)
                for k, (c, n) in enumerate(at):
                    ins = pe.matmul(psum, low[:, k, :], wh_upper[:, bass.ds(e, 1), c, n:n + width, 1],
                                    start=False, stop=k == chunks - 1)
                ins.then_inc(finished, 1)

            def expert_of(j):
                return pe.value_load(tile_expert_i[0:1, bass.ds(j, 1)], min_val=0, max_val=E - 1)

            def expert_step(j, parity, e, e_before):
                other = 1 - parity
                e_next = None
                if middle(j, 0, NT):
                    pe.wait_ge(xTl_ready, j + 1)
                    products(u_psum, xTh, xTl, e, 0, u_in_psum)
                if middle(j, 1, NT + 1):
                    if isinstance(j, int) and j == NT:
                        pe.wait_ge(h_ready, NT)
                    for k in range(HK):
                        ins = pe.transpose(hT_psum[:, k * P:(k + 1) * P], h[:, k * P:(k + 1) * P], ident[:, :])
                    ins.then_inc(hT_in_psum, 1)
                if middle(j, 0, NT):
                    products(v_psum, xTh, xTl, e, 2, v2_in_psum)
                if isinstance(j, int) and j == RANK_EXPERT_STEP:
                    pe.wait_ge(pv_bank_read, TT + 2)
                    rank_products(1)
                if middle(j, 0, NT - 1):
                    e_next = expert_of(j + 1)
                    transpose_x(j + 1, other)
                if middle(j, 1, NT + 1):
                    if not isinstance(j, int) or j >= 2:
                        pe.wait_ge(y_ready, j - 1)
                    pe.wait_ge(hTh_ready, j)
                    products(y_psum, hTh, hTl, e_before, 4, y_in_psum, hTl_ready, j)
                return e_next

            e_before = e = None
            for what, *at in SCHEDULE:
                if what == "A":
                    attention_step(at[0], at[0] % 2, at[0] // 2)
                elif what == "loop A":
                    run_steps(pe, attention_step, *at)
                elif what == "E":
                    if at[0] == 0:
                        pe.wait_ge(tables_ready, 1)
                        for k in range(3):
                            pe.wait_ge(w_low_ready[k], 2 * E)
                        pe.wait_ge(shifted_ready, TT)
                        transpose_x(0, 0)
                        e = expert_of(0)
                    if at[0] == 1:
                        pe.wait_ge(x1_ready, TT)
                    if at[0] == READY[0] - 1:
                        pe.wait_ge(tables_ready, 2)
                    e_before, e = e, expert_step(at[0], at[0] % 2, e, e_before)
                elif what == "loop E":
                    kept = [pe.alloc_register(f"expert_kept{i}") for i in range(2)]
                    for reg, value in zip(kept, (e_before, e)):
                        pe.reg_mov(reg, value)

                    def kept_expert(i):
                        return bass.RuntimeValue.of_register_unchecked(kept[i]).with_bounds(min_val=0, max_val=E - 1)

                    turn = 4
                    assert (at[1] - at[0]) % turn == 0
                    with pe.Fori(0, (at[1] - at[0]) // turn) as i:
                        e_before, e = kept_expert(0), kept_expert(1)
                        for k in range(at[0], at[0] + turn):
                            e_before, e = e, expert_step(i * turn + k, k % 2, e, e_before)
                        for reg, value in zip(kept, (e_before, e)):
                            pe.reg_mov(reg, value)
                    e_before, e = kept_expert(0), kept_expert(1)

        @block.vector
        def _(dve):
            steps = [0]

            def done(ins):
                steps[0] += 1
                ins.then_inc(dve_step, 1)
                dve.wait_ge(dve_step, steps[0])

            dve.memset(v_sb[:, :, :, HD:VW], 1.0).then_inc(v_ready, 1)
            dve.memset(vflat[:, :, :, :], 0.0).then_inc(vflat_cleared, 1)

            def stats_x(tiles):
                for t in tiles:
                    ins = dve.bn_stats(st1[:, t, :], x_sb[:, t, :])
                return ins

            def mean_variance(tiles):
                for t in tiles:
                    ins = dve.bn_aggr(mv1[:, t, :], st1[:, t, :])
                ins.then_inc(stats1_ready, 1)

            dve.wait_ge(x_first_loaded, 16 * B)
            done(stats_x(range(B)))
            mean_variance(range(B))
            dve.wait_ge(bk_loaded, 16)
            dve.wait_ge(kT_in_psum, 1)
            for m in range(DK):
                ins = dve.tensor_scalar(kT[:, m, :], bank[1][:, m * B * KEYS:(m + 1) * B * KEYS], bk_sb[:, m:m + 1],
                                        None, ALU.add)
            ins.then_inc(kT_ready, 1)
            dve.wait_ge(kT_ready, 1)
            dve.wait_ge(pool_step, N_POOL_SETUP[0])
            for b in range(B):
                for m in range(DK):
                    dve.tensor_tensor(kblock[:, b, m, :, :], bcast(kT[:, m, b * KEYS:(b + 1) * KEYS], 1, HEADS_HALF),
                                      bcast(kmask[:, :], 2, KEYS), ALU.mult).then_inc(blocks_ready, 1)
            dve.wait_ge(v_in_psum, 1)
            dve.wait_ge(bv_loaded, 16)
            for b in range(B):
                dve.tensor_tensor(v_sb[:, b, :, 0:HD], bank[2][0:KEYS, b * D:(b + 1) * D].rearrange("p (h d) -> p h d", h=HEADS),
                                  bv_sb[:, :].rearrange("p (h d) -> p h d", h=HEADS), ALU.add).then_inc(v_ready, 1)

            def statistics(b):
                dve.wait_ge(x_loaded[b], 16)
                done(stats_x(range(B + b, TT, B)))
                mean_variance(range(B + b, TT, B))

            statistics(0)

            def value_blocks():
                dve.wait_ge(vflat_loaded, 32 * B)
                for b in range(B):
                    dve.tensor_tensor(vblock[:, b], bcast(vflat[:, b, :, :], 2, SPAN),
                                      bcast(vmask[:, :, :], 3, VW), ALU.mult).then_inc(blocks_ready, 1)

            dve.wait_ge(tanh_ready, 1)

            def attention_step(t, parity, pair):
                other = 1 - parity
                if middle(t, 3, TT + 3):
                    dve.wait_ge(st2_ready, t - 2)
                if middle(t, 5, TT + 3):
                    dve.wait_ge(rstd2_ready, (t - 4) * 3)
                if middle(t, 2, TT + 2):
                    dve.wait_ge(pv_in_psum, t - 1)
                    dve.reciprocal(rden[:, parity:parity + 1, :],
                                   pv_psum[:, :, HD:VW].rearrange("p h o -> p o h")).then_inc(rden_ready, 1)
                if middle(t, 3, TT + 3):
                    dve.bn_aggr(mv2[:, other, :], st2[:, other, :]).then_inc(stats_ready, 1)
                if middle(t, 2, TT + 2):
                    dve.wait_ge(rden_ready, t - 1)
                    dve.tensor_tensor(o_sb.rearrange("p (h d) -> p h d", h=HEADS), pv_psum[:, :, 0:HD],
                                      bcast(rden[:, parity, :], 2, HD), ALU.mult).then_inc(o_ready, 1)
                if middle(t, 2, TT + 4):
                    if not middle(t, 2, TT + 2):
                        dve.wait_ge(pv_in_psum, t - 1)
                    if isinstance(t, int) and t == RANK_STEP + 1:
                        copy_ranks(0)
                    if middle(t, 4, TT + 4):
                        dve.tensor_copy(logits[:, bass.ds(t - 4, 1), :], logits_psum.unsqueeze(1)).then_inc(pv_bank_read, 1)
                    else:
                        dve.engine_nop().then_inc(pv_bank_read, 1)
                if middle(t, 0, TT):
                    dve.wait_ge(scores_in_psum, t + 1)
                    s01 = score_banks[:, :, 0:BANK_HEADS * KEYS].rearrange("p b (h k) -> p b h k", k=KEYS)
                    s2 = scores_last[:, 0:(HEADS - 2 * BANK_HEADS) * KEYS].rearrange("p (h k) -> p h k", k=KEYS)
                    nm01 = negmax[:, parity, 0:2 * BANK_HEADS].rearrange("p (b h) -> p b h", b=2)
                    nm2 = negmax[:, parity, 2 * BANK_HEADS:HEADS]
                    dve.tensor_reduce(nm01, s01, AX_X, ALU.max, negate=True)
                    dve.tensor_reduce(nm2, s2, AX_X, ALU.max, negate=True).then_inc(max_ready, 1)
                    dve.wait_ge(max_ready, t + 1)
                    for item in BEHIND_MAX.get(t, []) if isinstance(t, int) else []:
                        route(*item)
                    if middle(t, 1, TT):
                        dve.wait_ge(probsT_in_psum, t * 3)
                    cut = 2 * BANK_HEADS * KEYS
                    for b in range(2):
                        dve.tensor_tensor(
                            shifted[:, b * BANK_HEADS * KEYS:(b + 1) * BANK_HEADS * KEYS].rearrange("p (h k) -> p h k", k=KEYS),
                            s01[:, b, :, :], bcast(nm01[:, b, :], 2, KEYS), ALU.add)
                    dve.tensor_tensor(shifted[:, cut:FLAT].rearrange("p (h k) -> p h k", k=KEYS), s2,
                                      bcast(nm2, 2, KEYS), ALU.add).then_inc(shifted_ready, 1)
                for item in BEHIND_SUB.get(t, []) if isinstance(t, int) else []:
                    route(*item)
                split_first = isinstance(t, int) and t >= TT
                if middle(t, *SPLIT) and split_first:
                    for k in range(3):
                        split_low(t, parity, pair, k)
                if middle(t, 2, TT + 2):
                    dve.wait_ge(attn_in_psum, t - 1)
                    dve.wait_ge(residual_ready, t)
                    dve.scalar_tensor_tensor(out=x1[:, bass.ds(t - 2, 1), :], in0=bank_o[:, D:2 * D].unsqueeze(1),
                                             scalar=tg[:, 0:1], in1=x1[:, bass.ds(t - 2, 1), :],
                                             op0=ALU.mult, op1=ALU.add).then_inc(x1_ready, 1)
                if middle(t, 2, TT + 2):
                    dve.wait_ge(x1_ready, t - 1)
                if middle(t, *SPLIT) and not split_first:
                    split_low(t, parity, pair, 0)
                if middle(t, 2, TT + 2):
                    dve.bn_stats(st2[:, parity, :], x1[:, bass.ds(t - 2, 1), :]).then_inc(st2_ready, 1)
                if middle(t, *SPLIT) and not split_first:
                    split_low(t, parity, pair, 1)

            def split_low(t, parity, pair, k):
                if k == 0:
                    dve.wait_ge(w_high_loaded, pair * 16 * 3)
                dve.wait_ge(w_piece_loaded[k], (t - SPLIT[0] + 1) * 16)
                at = bass.ds(pair - 1, 1)
                dve.tensor_tensor(wl_sb[:, at, 3 * parity + k, :], w_piece[:, k, :].unsqueeze(1),
                                  wh_sb[:, at, 3 * parity + k, :].bitcast(F32), ALU.subtract).then_inc(w_low_ready[k], 1)

            def top(g, c):
                t0, t1 = GROUPS[g]
                n = t1 - t0
                source = logits[:, t0:t1, :] if c == 0 else logits2[:, 0:n, :]
                tmp, hot = scratch[:, 0:n, :], onehot[c][:, 0:n, :]
                if c == 0:
                    dve.wait_ge(pv_bank_read, t1 + 2)
                done(dve.tensor_reduce(best[c][:, 0:n], source, AX_X, ALU.max))
                done(dve.tensor_tensor(tmp, source, bcast(best[c][:, 0:n], 2, E), ALU.is_equal))
                done(dve.tensor_tensor(tmp, tmp, bcast(desc[:, :], 1, n), ALU.mult))
                done(dve.tensor_reduce(key[c][:, 0:n], tmp, AX_X, ALU.max))
                done(dve.tensor_tensor(hot, tmp, bcast(key[c][:, 0:n], 2, E), ALU.is_equal))
                if c == 0:
                    done(dve.scalar_tensor_tensor(out=logits2[:, 0:n, :], in0=hot, scalar=-3.0e38, in1=source,
                                                  op0=ALU.mult, op1=ALU.add))
                else:
                    dve.tensor_tensor(sel[:, 0:n, :], onehot[0][:, 0:n, :], hot, ALU.add).then_inc(sel_ready, 1)
                    dve.tensor_tensor(gap[:, 0:n], best[1][:, 0:n], best[0][:, 0:n], ALU.subtract).then_inc(gap_ready, 1)

            def copy_ranks(g):
                n = GROUPS[g][1] - GROUPS[g][0]
                dve.wait_ge(ranks_in_psum, g + 1)
                done(dve.tensor_copy(ranks[:, :, 0:n, :], ranks_psum[:, :, 0:n, :]))

            def slots(g, part):
                t0, t1 = GROUPS[g]
                n = t1 - t0
                assert n == NGT
                flat = "p e t -> p (e t)"
                if part == 0:
                    done(dve.tensor_copy(totals[:, :, 0:n], ranks[:, 1, 0:n, :].rearrange("p t e -> p e t")))
                    done(dve.tensor_tensor_scan(upto[:, :, :].rearrange(flat), scan_keep[:, :, :].rearrange(flat),
                                                totals[:, :, :].rearrange(flat), 0.0, ALU.mult, ALU.add))
                    if g == 0:
                        dve.tensor_copy(counts[:, 0, :].unsqueeze(2), upto[:, :, n - 1:n])
                    else:
                        dve.tensor_tensor(counts[:, g, :].unsqueeze(2), upto[:, :, n - 1:n], counts[:, g - 1, :].unsqueeze(2), ALU.add)
                    done(dve.tensor_tensor(totals[:, :, 0:n], upto[:, :, 0:n], totals[:, :, 0:n], ALU.subtract))
                    if g == NG - 1:
                        dve.tensor_copy(counts_i[:, :], counts[:, g, :]).then_inc(counts_ready, 1)
                    if g > 0:
                        done(dve.tensor_tensor(totals[:, :, 0:n], totals[:, :, 0:n], bcast(counts[:, g - 1, :], 2, n), ALU.add))
                    done(dve.tensor_tensor(totals[:, :, 0:n], totals[:, :, 0:n], bcast(cap_base[:, :], 2, n), ALU.add))
                    done(dve.tensor_tensor(position[:, 0:n, :], ranks[:, 0, 0:n, :], totals[:, :, 0:n].rearrange("p e t -> p t e"), ALU.add))
                else:
                    for c in range(TOPK):
                        done(dve.tensor_tensor(scratch[:, 0:n, :], position[:, 0:n, :], onehot[c][:, 0:n, :], ALU.mult))
                        done(dve.tensor_reduce(slot_f[c][:, 0:n], scratch[:, 0:n, :], AX_X, ALU.add))
                        done(dve.tensor_copy(slot[c][:, t0:t1], slot_f[c][:, 0:n]))
                    dve.engine_nop().then_inc(slots_ready, 1)

            def weights(g):
                t0, t1 = GROUPS[g]
                n = t1 - t0
                kept = rows[:, t0:t1, :]
                dve.wait_ge(egap_ready, g + 1)
                done(dve.tensor_scalar(esum[:, 0:n], egap[:, 0:n], 1.0, None, ALU.add))
                done(dve.reciprocal(p1[:, 0:n], esum[:, 0:n]))
                done(dve.tensor_scalar(p1g[:, 0:n], p1[:, 0:n], tg[:, 1:2], None, ALU.mult))
                done(dve.tensor_tensor(kept[:, :, D + 3:D + 4], p1g[:, 0:n].unsqueeze(2), egap[:, 0:n].unsqueeze(2), ALU.mult))
                dve.tensor_tensor(kept[:, :, D + 2:D + 3], p1g[:, 0:n].unsqueeze(2), kept[:, :, D + 3:D + 4], ALU.subtract)
                done(dve.tensor_scalar(kept[:, :, D + 1:D + 2], key[0][:, 0:n].unsqueeze(2), -1.0, float(E), ALU.mult, ALU.add))
                dve.engine_nop().then_inc(slots_ready, 1)

            def tables(g, part):
                j0, j1 = ([0] + READY)[g], READY[g]
                cols, nv = j1 - j0, (g + 1) * E
                last = g == NG - 1
                if last:
                    marks_area, passed_area, weighted_words = past_area, past_area, weighted_area
                else:
                    marks_area, passed_area = weighted_area, weighted_area[:, E * TT:]
                    weighted_words = passed_area[:, cols * nv:]
                flat = "p g e -> p (g e)"
                new, upto_v = blocks_new[:, 0:g + 1, :].rearrange(flat), blocks_upto[:, 0:g + 1, :].rearrange(flat)
                lead_v, step_v = lead[:, 0:g + 1, :].rearrange(flat), lead_step[:, 0:g + 1, :].rearrange(flat)
                passed = passed_area[:, 0:cols * nv].rearrange("p (j v) -> p j v", v=nv)
                wt = weighted_words[:, 0:cols * (nv - 1)].rearrange("p (j v) -> p j v", v=nv - 1)
                if part == 0:
                    marks = marks_area[:, 0:E * TT].rearrange("p (e t) -> p e t", e=E)
                    if last:
                        done(dve.tensor_tensor(marks, bcast(counts[:, g, :], 2, TT), bcast(tile_128[:, :], 1, E), ALU.is_gt))
                    else:
                        marks = marks[:, :, 0:TT - 1]
                        done(dve.tensor_tensor(marks, bcast(counts[:, g, :], 2, TT - 1),
                                               bcast(tile_128[:, 1:TT], 1, E), ALU.is_ge))
                    done(dve.tensor_reduce(blocks[:, g, :], marks, AX_X, ALU.add))
                    if g == 0:
                        done(dve.tensor_copy(blocks_new[:, 0, :], blocks[:, 0, :]))
                    else:
                        done(dve.tensor_tensor(blocks_new[:, g, :], blocks[:, g, :], blocks[:, g - 1, :], ALU.subtract))
                    done(dve.tensor_tensor_scan(upto_v, ones_f[:, 0:nv], new, 0.0, ALU.mult, ALU.add))
                    done(dve.tensor_tensor(lead[:, g, :], blocks[:, g, :], blocks_upto[:, g, :], ALU.subtract))
                    done(dve.scalar_tensor_tensor(out=lead[:, g, :], in0=lead[:, g, :], scalar=float(P), in1=cap_base[:, :],
                                                  op0=ALU.mult, op1=ALU.add))
                    done(dve.tensor_tensor(step_v[:, 0:nv - 1], lead_v[:, 1:nv], lead_v[:, 0:nv - 1], ALU.subtract))
                elif part == 1:
                    done(dve.tensor_tensor(passed, bcast(tile_no[:, j0:j1], 2, nv), bcast(upto_v, 1, cols), ALU.is_ge))
                    done(dve.tensor_tensor(wt, passed[:, :, 0:nv - 1],
                                           bcast(expert_step_c[:, 0:g + 1, :].rearrange(flat)[:, 0:nv - 1], 1, cols), ALU.mult))
                    done(dve.tensor_reduce(tile_expert[:, j0:j1], wt, AX_X, ALU.add))
                    dve.tensor_copy(tile_expert_i[:, j0:j1], tile_expert[:, j0:j1])
                else:
                    done(dve.tensor_tensor(wt, passed[:, :, 0:nv - 1], bcast(step_v[:, 0:nv - 1], 1, cols), ALU.mult))
                    row = tile_row[:, 0:cols]
                    done(dve.tensor_reduce(row, wt, AX_X, ALU.add))
                    done(dve.scalar_tensor_tensor(out=row, in0=tile_no[:, j0:j1], scalar=float(P), in1=row,
                                                  op0=ALU.mult, op1=ALU.add))
                    if last:
                        used = tile_used[:, 0:cols]
                        done(dve.tensor_scalar(used.unsqueeze(2), passed[:, :, nv - 1:nv], -1.0, 1.0, ALU.mult, ALU.add))
                        done(dve.tensor_scalar(row, row, float(-E * CAPACITY), None, ALU.add))
                        done(dve.tensor_tensor(row, row, used, ALU.mult))
                        done(dve.tensor_scalar(row, row, float(E * CAPACITY), None, ALU.add))
                    dve.tensor_copy(tile_row_i[:, j0:j1], row).then_inc(tables_ready, 1)

            def meta(j, parity):
                dve.wait_ge(tile_loaded[parity], (j // 2) * 16 + 16)
                dve.tensor_scalar(weight1[:, parity:parity + 1], xt[:, parity, D + 1:D + 2], tile_expert[:, bass.ds(j, 1)],
                                  xt[:, parity, D + 2:D + 3], ALU.is_equal, ALU.mult).then_inc(weight1_ready, 1)
                dve.wait_ge(weight1_ready, j + 1)
                dve.tensor_tensor(weight[:, bass.ds(j, 1)], weight1[:, parity:parity + 1], xt[:, parity, D + 3:D + 4], ALU.add)
                dve.tensor_copy(ids[:, bass.ds(j, 1)], xt[:, parity, D:D + 1].bitcast(I32)).then_inc(meta_ready, 1)

            def low_xT(j, parity):
                dve.wait_ge(xTh_ready, j + 1)
                dve.tensor_tensor(xTl.rearrange("p k n -> p (k n)"), xT_psum,
                                  xTh.rearrange("p k n -> p (k n)").bitcast(F32),
                                  ALU.subtract).then_inc(xTl_ready, 1)

            def expert_step(j, parity, pair):
                other = 1 - parity
                if middle(j, 0, NT):
                    if isinstance(j, int) and j == 0:
                        dve.wait_ge(probs_ready, TT)
                    meta(j, parity)
                if middle(j, 1, NT + 1):
                    dve.wait_ge(hTh_ready, j)
                    dve.tensor_tensor(hTl.rearrange("p k n -> p (k n)"), hT_psum,
                                      hTh.rearrange("p k n -> p (k n)").bitcast(F32),
                                      ALU.subtract).then_inc(hTl_ready, 1)
                if middle(j, 0, NT):
                    dve.wait_ge(silu_ready, j + 1)
                    dve.wait_ge(v2_in_psum, j + 1)
                    dve.tensor_tensor(h, silu, v_psum, ALU.mult).then_inc(h_ready, 1)
                if middle(j, 0, NT - 1):
                    low_xT(j + 1, other)

            def route(what, *at):
                {"top": top, "slots": slots, "weights": weights, "tables": tables}[what](*at)

            for what, *at in AHEAD:
                if what == "A":
                    attention_step(at[0], at[0] % 2, at[0] // 2)
                    if at[0] == 0:
                        value_blocks()
                        statistics(1)
                elif what == "loop A":
                    run_steps(dve, attention_step, *at)
                elif what == "E":
                    if at[0] == 0:
                        low_xT(0, 0)
                    expert_step(at[0], at[0] % 2, at[0] // 2)
                elif what == "loop E":
                    run_steps(dve, expert_step, *at)
                elif what == "ranks":
                    copy_ranks(at[0])
                else:
                    route(what, *at)


_INS = ['x', 'ctx_1024', 'g_xattn', 'g_ffn', 'L0_xattn_Wq', 'L0_xattn_bq', 'L0_xattn_Wk', 'L0_xattn_bk', 'L0_xattn_Wv',
        'L0_xattn_bv', 'L0_xattn_Wo', 'L0_xattn_bo', 'L0_ffn_Wg', 'L0_ffn_W1', 'L0_ffn_W2', 'L0_ffn_W3']
_OUTS = [((2, 1024, 256), 'float32')]


def kernel(**inputs):
    import numpy as _np
    import concourse.bacc as _bacc
    from concourse import mybir as _mybir
    from concourse.bass_utils import run_bass_kernel_spmd as _run

    nc = _bacc.Bacc("TRN2", target_bir_lowering=False, num_devices=1)
    arrays, args = {}, []
    for name in _INS:
        a = _np.ascontiguousarray(inputs[name])
        arrays[f"in_{name}_dram"] = a
        args.append(nc.dram_tensor(f"in_{name}_dram", a.shape, _mybir.dt.from_np(a.dtype), kind="ExternalInput").ap())
    for i, (shape, dtype) in enumerate(_OUTS):
        dt = _mybir.dt.from_np(_np.dtype(dtype))
        args.append(nc.dram_tensor(f"out_{i}_dram", shape, dt, kind="ExternalOutput").ap())
    flamingo_layer(nc, *args)
    r = _run(nc, [arrays], core_ids=[0])
    got = tuple(r.results[0][f"out_{i}_dram"] for i in range(len(_OUTS)))
    return got[0]
```
